# Optimizing a Trainium2 kernel written in Bass

```python
import numpy as np
import jax
import jax.numpy as jnp

def _softmax(x, axis=-1):
    return jax.nn.softmax(x, axis=axis)

def _gelu(x):
    return jax.nn.gelu(x, approximate=True)

def _silu(x):
    return jax.nn.silu(x)

def _sigmoid(x):
    return jax.nn.sigmoid(x)

def _layernorm(x, axis=-1, eps=1e-05):
    m = jnp.mean(x, axis=axis, keepdims=True)
    v = jnp.var(x, axis=axis, keepdims=True)
    return (x - m) / jnp.sqrt(v + eps)

def _scatter_add(tgt, idx, src, axis=0):
    return tgt.at[idx].add(src)

def _segment_sum(src, seg, n):
    return jax.ops.segment_sum(src, seg, n)
kernel_name = 'mk_flamingo_gated_d4_seqx_r8_56d2e7'

def setup_inputs(seed: int=0):
    np.random.seed(seed)
    _w = jnp.asarray

    def _rec_inputs():
        import jax
        import jax.numpy as jnp
        _rk = jax.random.key(seed)
        x = -0.0002928 + 1 * jax.random.normal(jax.random.fold_in(_rk, 1), (32, 64, 512), jnp.float32)
        _lenS = 64 - jax.random.randint(jax.random.fold_in(_rk, 7), (32,), 0, max(1, 64 // 4) + 1, jnp.int32)
        _lenS2 = 64 - jax.random.randint(jax.random.fold_in(_rk, 8), (32,), 0, max(1, 64 // 4) + 1, jnp.int32)
        _ctx_4096P = jax.random.normal(jax.random.fold_in(_rk, 11), (32, 16, 512), jnp.float32)
        _ctx_4096c = jax.random.dirichlet(jax.random.fold_in(_rk, 511), 0.3 * jnp.ones((16,), jnp.float32), (32, 64))
        _ctx_4096t = jnp.einsum('bsk,bkd->bsd', _ctx_4096c, _ctx_4096P)
        _ctx_4096t = _ctx_4096t * jax.lax.rsqrt(jnp.mean(jnp.square(_ctx_4096t)) + 1e-12) * 0.953939
        ctx_4096 = -2.8382e-05 + 0.999851 * (_ctx_4096t + 0.3 * jax.random.normal(jax.random.fold_in(_rk, 611), (32, 64, 512), jnp.float32))
        _validS = jnp.arange(64)[None, :] < _lenS[:, None]
        _validS2 = jnp.arange(64)[None, :] < _lenS2[:, None]
        _causal = jnp.tril(jnp.ones((64, 64), dtype=bool))
        mask_1x1xSxS2_ff0 = jnp.where(jnp.ones((1, 1, 64, 64), dtype=bool), 0.0, -1000000000.0).astype(jnp.float32)
        _g = jax.random.normal(jax.random.fold_in(_rk, 9001), (2, 4), jnp.float32)
        _g = jnp.sign(_g) * jnp.maximum(jnp.abs(_g), 1.0) + (_g == 0) * 1.0
        g_xattn = _g[0]
        g_ffn = _g[1]
        return (x, ctx_4096, mask_1x1xSxS2_ff0, g_xattn, g_ffn)
    x, ctx_4096, mask_1x1xSxS2_ff0, g_xattn, g_ffn = _rec_inputs()

    def _L0_xattn_setup():
        import jax, jax.numpy as jnp
        import numpy as np
        B, Q, K, D = (1, 128, 6404, 512)
        H, KVH, HD = (32, 8, 128)
        GROUPS = H // KVH
        EPS = 1e-05

        def _rmsnorm(x, w):
            xf = x.astype(jnp.float32)
            var = jnp.mean(xf * xf, axis=-1, keepdims=True)
            return (xf * jax.lax.rsqrt(var + EPS)).astype(x.dtype) * w
        key = jax.random.key(seed)
        ks = jax.random.split(key, 8)
        s = 0.02
        return {'hidden_states': jax.random.normal(ks[0], (B, Q, D), jnp.float32), 'cross_attention_states': jax.random.normal(ks[1], (B, K, D), jnp.float32), 'attention_mask': jnp.zeros((B, 1, Q, K), jnp.float32), 'Wq': jax.random.normal(ks[2], (H * HD, D), jnp.float32) * s, 'Wk': jax.random.normal(ks[3], (KVH * HD, D), jnp.float32) * s, 'Wv': jax.random.normal(ks[4], (KVH * HD, D), jnp.float32) * s, 'Wo': jax.random.normal(ks[5], (D, H * HD), jnp.float32) * s, 'q_norm_w': jnp.ones((HD,), jnp.float32), 'k_norm_w': jnp.ones((HD,), jnp.float32)}
    _L0_xattn_all = _L0_xattn_setup()
    _L0_xattn_in = {k: v for k, v in _L0_xattn_all.items() if k in ('Wq', 'Wk', 'Wv', 'Wo', 'q_norm_w', 'k_norm_w')}
    del _L0_xattn_all

    def _L0_ffn_setup():
        import jax, jax.numpy as jnp
        import numpy as np
        LORA_SCALE = 16.0 / jnp.sqrt(16.0)
        TOP_K = 2
        key = jax.random.key(seed)
        k1, k2, k3, k4 = jax.random.split(key, 4)
        B_, S, D, O, E, R = (4, 256, 512, 512, 4, 16)
        x = jax.random.normal(k1, (B_, S, D), dtype=jnp.float32)
        router_w = jax.random.normal(k2, (E, D), dtype=jnp.float32) * 0.02
        A = jax.random.normal(k3, (E, R, D), dtype=jnp.float32) * 0.02
        B = jax.random.normal(k4, (O,), dtype=jnp.float32)
        B = jax.random.normal(k4, (E, O, R), dtype=jnp.float32) * 0.02
        return {'x': x, 'router_w': router_w, 'A': A, 'B': B}
    _L0_ffn_all = _L0_ffn_setup()
    _L0_ffn_in = {k: v for k, v in _L0_ffn_all.items() if k in ('router_w', 'A', 'B')}
    del _L0_ffn_all

    def _L1_xattn_setup():
        import jax, jax.numpy as jnp
        import numpy as np
        TEXT_DIM = 512
        FEATURE_DIM = 512

        def _xavier_uniform(key, shape):
            fan_in, fan_out = (shape[1], shape[0])
            limit = float(np.sqrt(6.0 / (fan_in + fan_out)))
            return jax.random.uniform(key, shape, jnp.float32, -limit, limit)
        key = jax.random.key(seed)
        k1, k2, k3, k4 = jax.random.split(key, 4)
        text = jax.random.normal(k1, (8, 256, TEXT_DIM), jnp.float32)
        features = jax.random.normal(k2, (8, 72, FEATURE_DIM), jnp.float32)
        Wq = _xavier_uniform(k3, (FEATURE_DIM, TEXT_DIM))
        bq = jnp.zeros((FEATURE_DIM,), jnp.float32)
        Wk = _xavier_uniform(k4, (FEATURE_DIM, FEATURE_DIM))
        bk = jnp.zeros((FEATURE_DIM,), jnp.float32)
        return {'text': text, 'features': features, 'Wq': Wq, 'bq': bq, 'Wk': Wk, 'bk': bk}
    _L1_xattn_all = _L1_xattn_setup()
    _L1_xattn_in = {k: v for k, v in _L1_xattn_all.items() if k in ('Wq', 'bq', 'Wk', 'bk')}
    del _L1_xattn_all

    def _L1_ffn_setup():
        import jax, jax.numpy as jnp
        import numpy as np
        SCALE = 16.0 / 8.0
        key = jax.random.key(seed)
        ks = jax.random.split(key, 6)
        B, S, IN, OUT, E, R = (4, 256, 512, 512, 4, 8)
        x = jax.random.normal(ks[0], (B, S, IN), dtype=jnp.float32)
        W = jax.random.normal(ks[1], (OUT, IN), dtype=jnp.float32) * 0.02
        b = jax.random.normal(ks[2], (OUT,), dtype=jnp.float32) * 0.02
        A = jax.random.normal(ks[3], (E, R, IN), dtype=jnp.float32) * 0.02
        Bm = jax.random.normal(ks[4], (E, OUT, R), dtype=jnp.float32) * 0.02
        Wr = jax.random.normal(ks[5], (E, IN), dtype=jnp.float32) * 0.02
        return {'x': x, 'W': W, 'b': b, 'A': A, 'Bm': Bm, 'Wr': Wr}
    _L1_ffn_all = _L1_ffn_setup()
    _L1_ffn_in = {k: v for k, v in _L1_ffn_all.items() if k in ('W', 'b', 'A', 'Bm', 'Wr')}
    del _L1_ffn_all

    def _L2_xattn_setup():
        import jax, jax.numpy as jnp
        import numpy as np
        EMBED = 512
        NUM_Q = 32
        NUM_KV = 8
        GROUPS = NUM_Q // NUM_KV
        HEAD_DIM = EMBED // NUM_Q
        KV_DIM = HEAD_DIM * NUM_KV
        key = jax.random.key(seed)
        ks = jax.random.split(key, 12)
        B, S = (2, 256)
        s = 0.02
        return {'query': jax.random.normal(ks[0], (B, S, EMBED), jnp.float32), 'key': jax.random.normal(ks[1], (B, S, EMBED), jnp.float32), 'value': jax.random.normal(ks[2], (B, S, EMBED), jnp.float32), 'Wq': jax.random.normal(ks[3], (EMBED, EMBED), jnp.float32) * s, 'bq': jnp.zeros((EMBED,), jnp.float32), 'Wk': jax.random.normal(ks[4], (EMBED, KV_DIM), jnp.float32) * s, 'bk': jnp.zeros((KV_DIM,), jnp.float32), 'Wv': jax.random.normal(ks[5], (EMBED, KV_DIM), jnp.float32) * s, 'bv': jnp.zeros((KV_DIM,), jnp.float32), 'Wo': jax.random.normal(ks[6], (EMBED, EMBED), jnp.float32) * s, 'bo': jnp.zeros((EMBED,), jnp.float32)}
    _L2_xattn_all = _L2_xattn_setup()
    _L2_xattn_in = {k: v for k, v in _L2_xattn_all.items() if k in ('Wq', 'bq', 'Wk', 'bk', 'Wv', 'bv', 'Wo', 'bo')}
    del _L2_xattn_all

    def _L2_ffn_setup():
        import jax, jax.numpy as jnp
        import numpy as np
        EPS = 1e-05
        QMAX = 127.0

        def _fake_quant_lastdim(x):
            s = jnp.max(jnp.abs(x), axis=-1, keepdims=True) / QMAX
            s = jnp.maximum(s, 1e-08)
            q = jnp.clip(jnp.round(x / s), -QMAX, QMAX) * s
            return q

        def _dyn_quant_linear(x, w, b):
            xq = _fake_quant_lastdim(x)
            wq = _fake_quant_lastdim(w)
            return jnp.einsum('bti,oi->bto', xq, wq) + b

        def _layernorm(x, gamma, beta):
            mu = jnp.mean(x, axis=-1, keepdims=True)
            var = jnp.mean(jnp.square(x - mu), axis=-1, keepdims=True)
            return (x - mu) * jax.lax.rsqrt(var + EPS) * gamma + beta
        key = jax.random.key(seed)
        k1, k2, k3, k4, k5 = jax.random.split(key, 5)
        B, T, INTER, LLM = (8, 32, 512, 512)
        return {'vit_embeds': jax.random.normal(k1, (B, T, INTER), jnp.float32), 'gamma': jnp.ones((INTER,), jnp.float32), 'beta': jnp.zeros((INTER,), jnp.float32), 'w1': jax.random.normal(k2, (LLM, INTER), jnp.float32) * 0.02, 'b1': jax.random.normal(k3, (LLM,), jnp.float32) * 0.02, 'w3': jax.random.normal(k4, (LLM, LLM), jnp.float32) * 0.02, 'b3': jax.random.normal(k5, (LLM,), jnp.float32) * 0.02}
    _L2_ffn_all = _L2_ffn_setup()
    _L2_ffn_in = {k: v for k, v in _L2_ffn_all.items() if k in ('gamma', 'beta', 'w1', 'b1', 'w3', 'b3')}
    del _L2_ffn_all

    def _L3_xattn_setup():
        import jax, jax.numpy as jnp
        import numpy as np
        DIM = 64
        HEADS = 8
        DIM_HEAD = 64
        HIDDEN = HEADS * DIM_HEAD
        SCALE = DIM_HEAD ** (-0.5)
        key = jax.random.key(seed)
        ks = jax.random.split(key, 9)
        b, n = (8, 512)
        std = 1.0 / np.sqrt(DIM)
        return {'q': jax.random.normal(ks[0], (b, DIM, n), jnp.float32), 'k': jax.random.normal(ks[1], (b, DIM, n), jnp.float32), 'v': jax.random.normal(ks[2], (b, DIM, n), jnp.float32), 'Wq': jax.random.normal(ks[3], (HIDDEN, DIM), jnp.float32) * std, 'Wk': jax.random.normal(ks[4], (HIDDEN, DIM), jnp.float32) * std, 'Wv': jax.random.normal(ks[5], (HIDDEN, DIM), jnp.float32) * std, 'Wo': jax.random.normal(ks[6], (DIM, HIDDEN), jnp.float32) * (1.0 / np.sqrt(HIDDEN)), 'bo': jax.random.normal(ks[7], (DIM,), jnp.float32) * 0.01, 'g': jnp.ones((1, DIM, 1), jnp.float32)}
    _L3_xattn_all = _L3_xattn_setup()
    _L3_xattn_in = {k: v for k, v in _L3_xattn_all.items() if k in ('Wq', 'Wk', 'Wv', 'Wo', 'bo', 'g')}
    del _L3_xattn_all

    def _L3_ffn_setup():
        import jax, jax.numpy as jnp
        import numpy as np
        GROUP_SIZE = 128

        def dequantize(imatrix, scales, zeros, group_size, out_dtype):
            rs = jnp.repeat(scales, group_size, axis=0)
            rz = jnp.repeat(zeros, group_size, axis=0)
            return ((imatrix.astype(rs.dtype) - rz.astype(rs.dtype)) * rs).astype(out_dtype)
        key = jax.random.key(seed)
        ks = jax.random.split(key, 10)
        H, I, G = (512, 1792, GROUP_SIZE)
        B, S = (4, 256)
        x = jax.random.normal(ks[0], (B, S, H), dtype=jnp.float32)
        gate_w = jax.random.randint(ks[1], (H, I), 0, 16, dtype=jnp.int32)
        gate_z = jax.random.randint(ks[2], (H // G, I), 0, 16, dtype=jnp.int32)
        gate_s = jax.random.uniform(ks[3], (H // G, I), dtype=jnp.float32) * 0.01
        up_w = jax.random.randint(ks[4], (H, I), 0, 16, dtype=jnp.int32)
        up_z = jax.random.randint(ks[5], (H // G, I), 0, 16, dtype=jnp.int32)
        up_s = jax.random.uniform(ks[6], (H // G, I), dtype=jnp.float32) * 0.01
        down_w = jax.random.randint(ks[7], (I, H), 0, 16, dtype=jnp.int32)
        down_z = jax.random.randint(ks[8], (I // G, H), 0, 16, dtype=jnp.int32)
        down_s = jax.random.uniform(ks[9], (I // G, H), dtype=jnp.float32) * 0.01
        return {'x': x, 'gate_w': gate_w, 'gate_z': gate_z, 'gate_s': gate_s, 'up_w': up_w, 'up_z': up_z, 'up_s': up_s, 'down_w': down_w, 'down_z': down_z, 'down_s': down_s}
    _L3_ffn_all = _L3_ffn_setup()
    _L3_ffn_in = {k: v for k, v in _L3_ffn_all.items() if k in ('gate_w', 'gate_z', 'gate_s', 'up_w', 'up_z', 'up_s', 'down_w', 'down_z', 'down_s')}
    del _L3_ffn_all
    return {'x': x, 'ctx_4096': ctx_4096, 'mask_1x1xSxS2_ff0': mask_1x1xSxS2_ff0, 'g_xattn': g_xattn, 'g_ffn': g_ffn, 'L0_xattn_Wq': _L0_xattn_in['Wq'], 'L0_xattn_Wk': _L0_xattn_in['Wk'], 'L0_xattn_Wv': _L0_xattn_in['Wv'], 'L0_xattn_Wo': _L0_xattn_in['Wo'], 'L0_xattn_q_norm_w': _L0_xattn_in['q_norm_w'], 'L0_xattn_k_norm_w': _L0_xattn_in['k_norm_w'], 'L0_ffn_router_w': _L0_ffn_in['router_w'], 'L0_ffn_A': _L0_ffn_in['A'], 'L0_ffn_B': _L0_ffn_in['B'], 'L1_xattn_Wq': _L1_xattn_in['Wq'], 'L1_xattn_bq': _L1_xattn_in['bq'], 'L1_xattn_Wk': _L1_xattn_in['Wk'], 'L1_xattn_bk': _L1_xattn_in['bk'], 'L1_ffn_W': _L1_ffn_in['W'], 'L1_ffn_b': _L1_ffn_in['b'], 'L1_ffn_A': _L1_ffn_in['A'], 'L1_ffn_Bm': _L1_ffn_in['Bm'], 'L1_ffn_Wr': _L1_ffn_in['Wr'], 'L2_xattn_Wq': _L2_xattn_in['Wq'], 'L2_xattn_bq': _L2_xattn_in['bq'], 'L2_xattn_Wk': _L2_xattn_in['Wk'], 'L2_xattn_bk': _L2_xattn_in['bk'], 'L2_xattn_Wv': _L2_xattn_in['Wv'], 'L2_xattn_bv': _L2_xattn_in['bv'], 'L2_xattn_Wo': _L2_xattn_in['Wo'], 'L2_xattn_bo': _L2_xattn_in['bo'], 'L2_ffn_gamma': _L2_ffn_in['gamma'], 'L2_ffn_beta': _L2_ffn_in['beta'], 'L2_ffn_w1': _L2_ffn_in['w1'], 'L2_ffn_b1': _L2_ffn_in['b1'], 'L2_ffn_w3': _L2_ffn_in['w3'], 'L2_ffn_b3': _L2_ffn_in['b3'], 'L3_xattn_Wq': _L3_xattn_in['Wq'], 'L3_xattn_Wk': _L3_xattn_in['Wk'], 'L3_xattn_Wv': _L3_xattn_in['Wv'], 'L3_xattn_Wo': _L3_xattn_in['Wo'], 'L3_xattn_bo': _L3_xattn_in['bo'], 'L3_xattn_g': _L3_xattn_in['g'], 'L3_ffn_gate_w': _L3_ffn_in['gate_w'], 'L3_ffn_gate_z': _L3_ffn_in['gate_z'], 'L3_ffn_gate_s': _L3_ffn_in['gate_s'], 'L3_ffn_up_w': _L3_ffn_in['up_w'], 'L3_ffn_up_z': _L3_ffn_in['up_z'], 'L3_ffn_up_s': _L3_ffn_in['up_s'], 'L3_ffn_down_w': _L3_ffn_in['down_w'], 'L3_ffn_down_z': _L3_ffn_in['down_z'], 'L3_ffn_down_s': _L3_ffn_in['down_s']}

def reference(x, ctx_4096, mask_1x1xSxS2_ff0, g_xattn, g_ffn, L0_xattn_Wq, L0_xattn_Wk, L0_xattn_Wv, L0_xattn_Wo, L0_xattn_q_norm_w, L0_xattn_k_norm_w, L0_ffn_router_w, L0_ffn_A, L0_ffn_B, L1_xattn_Wq, L1_xattn_bq, L1_xattn_Wk, L1_xattn_bk, L1_ffn_W, L1_ffn_b, L1_ffn_A, L1_ffn_Bm, L1_ffn_Wr, L2_xattn_Wq, L2_xattn_bq, L2_xattn_Wk, L2_xattn_bk, L2_xattn_Wv, L2_xattn_bv, L2_xattn_Wo, L2_xattn_bo, L2_ffn_gamma, L2_ffn_beta, L2_ffn_w1, L2_ffn_b1, L2_ffn_w3, L2_ffn_b3, L3_xattn_Wq, L3_xattn_Wk, L3_xattn_Wv, L3_xattn_Wo, L3_xattn_bo, L3_xattn_g, L3_ffn_gate_w, L3_ffn_gate_z, L3_ffn_gate_s, L3_ffn_up_w, L3_ffn_up_z, L3_ffn_up_s, L3_ffn_down_w, L3_ffn_down_z, L3_ffn_down_s):
    import jax
    import jax.numpy as jnp

    def _L0_xattn_ref(hidden_states, cross_attention_states, attention_mask, Wq, Wk, Wv, Wo, q_norm_w, k_norm_w):
        import jax, jax.numpy as jnp
        import numpy as np
        B, Q, K, D = (1, 128, 6404, 512)
        H, KVH, HD = (32, 8, 128)
        GROUPS = H // KVH
        EPS = 1e-05

        def _rmsnorm(x, w):
            xf = x.astype(jnp.float32)
            var = jnp.mean(xf * xf, axis=-1, keepdims=True)
            return (xf * jax.lax.rsqrt(var + EPS)).astype(x.dtype) * w
        bsz, q_len, _ = hidden_states.shape
        kv_len = cross_attention_states.shape[1]
        q = (hidden_states @ Wq.T).reshape(bsz, q_len, H, HD).transpose(0, 2, 1, 3)
        k = (cross_attention_states @ Wk.T).reshape(bsz, kv_len, KVH, HD).transpose(0, 2, 1, 3)
        v = (cross_attention_states @ Wv.T).reshape(bsz, kv_len, KVH, HD).transpose(0, 2, 1, 3)
        q = _rmsnorm(q, q_norm_w)
        k = jnp.repeat(k, GROUPS, axis=1)
        v = jnp.repeat(v, GROUPS, axis=1)
        k = _rmsnorm(k, k_norm_w)
        scale = 1.0 / np.sqrt(HD)
        scores = jnp.einsum('bhqd,bhkd->bhqk', q, k) * scale
        scores = scores + attention_mask[:, :, :, :kv_len]
        probs = jax.nn.softmax(scores.astype(jnp.float32), axis=-1).astype(q.dtype)
        out = jnp.einsum('bhqk,bhkd->bhqd', probs, v)
        out = out.transpose(0, 2, 1, 3).reshape(bsz, q_len, H * HD)
        return out @ Wo.T

    def _L0_ffn_ref(x, router_w, A, B):
        import jax, jax.numpy as jnp
        import numpy as np
        LORA_SCALE = 16.0 / jnp.sqrt(16.0)
        TOP_K = 2
        D = x.shape[-1]
        flat = x.reshape(-1, D)
        logits = flat @ router_w.T
        topk_vals, topk_idx = jax.lax.top_k(logits, TOP_K)
        sparse = jnp.full_like(logits, -jnp.inf)
        rows = jnp.arange(logits.shape[0])[:, None]
        sparse = sparse.at[rows, topk_idx].set(topk_vals)
        gates = jax.nn.softmax(sparse, axis=-1)
        mid = jnp.einsum('tf,erf->ter', flat, A)
        all_deltas = jnp.einsum('ter,eor->teo', mid, B) * LORA_SCALE
        delta = jnp.einsum('te,teo->to', gates, all_deltas)
        return delta.reshape(*x.shape[:-1], -1)

    def _L1_xattn_ref(text, features, Wq, bq, Wk, bk):
        import jax, jax.numpy as jnp
        import numpy as np
        TEXT_DIM = 512
        FEATURE_DIM = 512

        def _xavier_uniform(key, shape):
            fan_in, fan_out = (shape[1], shape[0])
            limit = float(np.sqrt(6.0 / (fan_in + fan_out)))
            return jax.random.uniform(key, shape, jnp.float32, -limit, limit)
        Q = jnp.einsum('btx,dx->btd', text, Wq) + bq
        K = jnp.einsum('bpx,dx->bpd', features, Wk) + bk
        scale = 1.0 / jnp.sqrt(jnp.asarray(K.shape[-1], K.dtype))
        scores = jnp.einsum('btd,bpd->btp', Q, K) * scale
        attn = jax.nn.softmax(scores, axis=-1)
        attended = jnp.einsum('btp,bpd->btd', attn, features)
        return attended

    def _L1_ffn_ref(x, W, b, A, Bm, Wr):
        import jax, jax.numpy as jnp
        import numpy as np
        SCALE = 16.0 / 8.0
        base_out = jnp.einsum('bsi,oi->bso', x, W) + b
        gates = jax.nn.softmax(jnp.einsum('bsi,ei->bse', x, Wr), axis=-1)
        proj_r = jnp.einsum('bsi,eri->bser', x, A)
        lora_out = jnp.einsum('bser,eor->bseo', proj_r, Bm)
        lora_mix = jnp.einsum('bse,bseo->bso', gates * SCALE, lora_out)
        return base_out + lora_mix

    def _L2_xattn_ref(query, key, value, Wq, bq, Wk, bk, Wv, bv, Wo, bo):
        import jax, jax.numpy as jnp
        import numpy as np
        EMBED = 512
        NUM_Q = 32
        NUM_KV = 8
        GROUPS = NUM_Q // NUM_KV
        HEAD_DIM = EMBED // NUM_Q
        KV_DIM = HEAD_DIM * NUM_KV
        B, S, _ = query.shape
        Q = query @ Wq + bq
        K = key @ Wk + bk
        V = value @ Wv + bv
        Q = Q.reshape(B, S, NUM_KV, GROUPS, HEAD_DIM).transpose(0, 2, 3, 1, 4)
        K = K.reshape(B, S, NUM_KV, HEAD_DIM).transpose(0, 2, 1, 3)
        V = V.reshape(B, S, NUM_KV, HEAD_DIM).transpose(0, 2, 1, 3)
        scale = 1.0 / jnp.sqrt(jnp.asarray(HEAD_DIM, query.dtype))
        scores = jnp.einsum('bhgqd,bhkd->bhgqk', Q, K) * scale
        w = jax.nn.softmax(scores, axis=-1)
        y = jnp.einsum('bhgqk,bhkd->bhgqd', w, V)
        y = y.transpose(0, 3, 1, 2, 4).reshape(B, S, EMBED)
        return y @ Wo + bo

    def _L2_ffn_ref(vit_embeds, gamma, beta, w1, b1, w3, b3):
        import jax, jax.numpy as jnp
        import numpy as np
        EPS = 1e-05
        QMAX = 127.0

        def _fake_quant_lastdim(x):
            s = jnp.max(jnp.abs(x), axis=-1, keepdims=True) / QMAX
            s = jnp.maximum(s, 1e-08)
            q = jnp.clip(jnp.round(x / s), -QMAX, QMAX) * s
            return q

        def _dyn_quant_linear(x, w, b):
            xq = _fake_quant_lastdim(x)
            wq = _fake_quant_lastdim(w)
            return jnp.einsum('bti,oi->bto', xq, wq) + b

        def _layernorm(x, gamma, beta):
            mu = jnp.mean(x, axis=-1, keepdims=True)
            var = jnp.mean(jnp.square(x - mu), axis=-1, keepdims=True)
            return (x - mu) * jax.lax.rsqrt(var + EPS) * gamma + beta
        h = _layernorm(vit_embeds, gamma, beta)
        h = _dyn_quant_linear(h, w1, b1)
        h = jax.nn.gelu(h, approximate=False)
        h = _dyn_quant_linear(h, w3, b3)
        return h

    def _L3_xattn_ref(q, k, v, Wq, Wk, Wv, Wo, bo, g):
        import jax, jax.numpy as jnp
        import numpy as np
        DIM = 64
        HEADS = 8
        DIM_HEAD = 64
        HIDDEN = HEADS * DIM_HEAD
        SCALE = DIM_HEAD ** (-0.5)
        b = q.shape[0]
        qh = jnp.einsum('bcn,oc->bon', q, Wq).reshape(b, HEADS, DIM_HEAD, -1)
        kh = jnp.einsum('bcn,oc->bon', k, Wk).reshape(b, HEADS, DIM_HEAD, -1)
        vh = jnp.einsum('bcn,oc->bon', v, Wv).reshape(b, HEADS, DIM_HEAD, -1)
        qh = jax.nn.softmax(qh, axis=-2) * SCALE
        kh = jax.nn.softmax(kh, axis=-1)
        context = jnp.einsum('bhdn,bhen->bhde', kh, vh)
        out = jnp.einsum('bhde,bhdn->bhen', context, qh)
        out = out.reshape(b, HIDDEN, -1)
        out = jnp.einsum('bcn,oc->bon', out, Wo) + bo[None, :, None]
        norm = jnp.maximum(jnp.sqrt(jnp.sum(out * out, axis=1, keepdims=True)), 1e-12)
        return out / norm * g * np.sqrt(DIM)

    def _L3_ffn_ref(x, gate_w, gate_z, gate_s, up_w, up_z, up_s, down_w, down_z, down_s):
        import jax, jax.numpy as jnp
        import numpy as np
        GROUP_SIZE = 128

        def dequantize(imatrix, scales, zeros, group_size, out_dtype):
            rs = jnp.repeat(scales, group_size, axis=0)
            rz = jnp.repeat(zeros, group_size, axis=0)
            return ((imatrix.astype(rs.dtype) - rz.astype(rs.dtype)) * rs).astype(out_dtype)
        dt = x.dtype
        gate_proj = dequantize(gate_w, gate_s, gate_z, GROUP_SIZE, dt)
        up_proj = dequantize(up_w, up_s, up_z, GROUP_SIZE, dt)
        down_proj = dequantize(down_w, down_s, down_z, GROUP_SIZE, dt)
        gate = jax.nn.silu(jnp.dot(x, gate_proj))
        up = jnp.dot(x, up_proj)
        return jnp.dot(gate * up, down_proj)
    x = x + jnp.tanh(g_xattn[0]) * _L0_xattn_ref(_layernorm(x, axis=-1), ctx_4096, mask_1x1xSxS2_ff0, L0_xattn_Wq, L0_xattn_Wk, L0_xattn_Wv, L0_xattn_Wo, L0_xattn_q_norm_w, L0_xattn_k_norm_w)
    x = x + jnp.tanh(g_ffn[0]) * _L0_ffn_ref(_layernorm(x, axis=-1), L0_ffn_router_w, L0_ffn_A, L0_ffn_B)
    x = x + jnp.tanh(g_xattn[1]) * _L1_xattn_ref(_layernorm(x, axis=-1), ctx_4096, L1_xattn_Wq, L1_xattn_bq, L1_xattn_Wk, L1_xattn_bk)
    x = x + jnp.tanh(g_ffn[1]) * _L1_ffn_ref(_layernorm(x, axis=-1), L1_ffn_W, L1_ffn_b, L1_ffn_A, L1_ffn_Bm, L1_ffn_Wr)
    x = x + jnp.tanh(g_xattn[2]) * _L2_xattn_ref(_layernorm(x, axis=-1), ctx_4096, ctx_4096, L2_xattn_Wq, L2_xattn_bq, L2_xattn_Wk, L2_xattn_bk, L2_xattn_Wv, L2_xattn_bv, L2_xattn_Wo, L2_xattn_bo)
    x = x + jnp.tanh(g_ffn[2]) * _L2_ffn_ref(_layernorm(x, axis=-1), L2_ffn_gamma, L2_ffn_beta, L2_ffn_w1, L2_ffn_b1, L2_ffn_w3, L2_ffn_b3)
    x = x + jnp.tanh(g_xattn[3]) * _L3_xattn_ref(_layernorm(x, axis=-1), ctx_4096, ctx_4096, L3_xattn_Wq, L3_xattn_Wk, L3_xattn_Wv, L3_xattn_Wo, L3_xattn_bo, L3_xattn_g)
    x = x + jnp.tanh(g_ffn[3]) * _L3_ffn_ref(_layernorm(x, axis=-1), L3_ffn_gate_w, L3_ffn_gate_z, L3_ffn_gate_s, L3_ffn_up_w, L3_ffn_up_z, L3_ffn_up_s, L3_ffn_down_w, L3_ffn_down_z, L3_ffn_down_s)
    return x

_drawn_inputs = setup_inputs


def setup_inputs(seed=0):
    import zlib

    import numpy as np

    out = dict(_drawn_inputs(seed))
    spreads = {'L0_xattn_q_norm_w': (1.0, 0.6),
     'L0_xattn_k_norm_w': (1.0, 0.6),
     'L1_xattn_bq': (0.0, 0.421),
     'L1_xattn_bk': (0.0, 2.0),
     'L2_xattn_bq': (0.0, 0.8),
     'L2_xattn_bk': (0.0, 2.0),
     'L2_xattn_bv': (0.0, 0.28),
     'L2_xattn_bo': (0.0, 0.1),
     'L2_ffn_gamma': (1.0, 0.6),
     'L2_ffn_beta': (0.0, 0.8),
     'L3_xattn_g': (1.0, 0.2)}
    factors = {'g_ffn': 22.504,
     'L1_ffn_b': 3.907,
     'L1_ffn_A': 2.852,
     'L1_ffn_Bm': 2.857,
     'L1_ffn_Wr': 7.664,
     'L2_xattn_Wq': 8.0,
     'L2_xattn_Wk': 8.0,
     'L2_ffn_b1': 8.0,
     'L2_ffn_b3': 5.079}
    for name, (base, spread) in spreads.items():
        noise = np.random.default_rng([zlib.crc32(name.encode()), seed]).standard_normal(out[name].shape)
        drawn = base * np.exp(spread * noise) if base else spread * noise
        out[name] = jnp.asarray(drawn.astype(out[name].dtype))
    for name, factor in factors.items():
        out[name] = (out[name] * factor).astype(out[name].dtype)
    return out
```

```python
import numpy as np

import concourse.bass as bass
from concourse import mybir
from contextlib import ExitStack

F32 = mybir.dt.float32
BF16 = mybir.dt.bfloat16
I32 = mybir.dt.int32
ALU = mybir.AluOpType
ACT = mybir.ActivationFunctionType
AX = mybir.AxisListType

P = 128
B, S, D = 32, 64, 512
T = B * S
NT = T // P
KC = D // P
ST = 4
NS = NT // ST
W = ST * P
EPS = 1e-5
PASSES = ((0, 0), (0, 1), (1, 0))


class Env:
    pass


def semaphores(nc, ctx, prefix):
    taken = []

    def sem(name):
        taken.append(nc.alloc_semaphore(name=f"{prefix}{name}"))
        return taken[-1]

    def give_back():
        nc.clear_and_free_semaphores(taken)
        nc.all_engine_barrier()

    ctx.callback(give_back)
    return sem


def layer_norm_phase(nc, env, name, mode):
    plain, split = mode == "plain", mode == "split"
    with ExitStack() as ctx:
        sem = semaphores(nc, ctx, f"{name}_")
        sb = lambda n, shape, dt: ctx.enter_context(nc.sbuf_tensor(f"{name}_{n}", shape, dt))
        stats = sb("stats", [P, NT, 6], F32)
        mv = sb("mv", [P, NT, 2], F32)
        var_eps = sb("var_eps", [P, NT], F32)
        rstd = sb("rstd", [P, NT], F32)
        minus_half = sb("minus_half", [P, NT], F32)
        tiles = sb("tiles", [P, ST, D], F32)
        turned = [ctx.enter_context(nc.psum_tensor(f"{name}_turned{b}", [P, KC, P], F32)) for b in range(ST)]
        const_set, stats_done, mv_done, var_ready, rstd_ready = map(sem, ("const", "stats", "mv", "var", "rstd"))
        tile_ready, turned_ready, high_done, low_done = map(sem, ("tile", "turned", "high", "low"))
        block = ctx.enter_context(nc.Block())

        @block.gpsimd
        def _(pool):
            nc.gpsimd.memset(minus_half[:], -0.5).then_inc(const_set, 1)
            pool.wait_ge(const_set, 1)
            pool.wait_ge(var_ready, 1)
            nc.gpsimd.tensor_tensor(rstd[:], var_eps[:], minus_half[:], ALU.pow).then_inc(rstd_ready, 1)

        def low_part(dve, t):
            dve.wait_ge(high_done, t + 1)
            cols = slice(t * P, (t + 1) * P)
            nc.vector.tensor_tensor(env.xtl[:, :, cols], turned[t % ST][:], env.xth[:, :, cols],
                                    ALU.subtract).then_inc(low_done, 1)

        @block.vector
        def _(dve):
            for t in range(NT):
                nc.vector.bn_stats(stats[:, t, :], env.x[:, t, :]).then_inc(stats_done, 1)
            for t in range(NT):
                dve.wait_ge(stats_done, t + 1)
                nc.vector.bn_aggr(mv[:, t, :], stats[:, t, :]).then_inc(mv_done, 1)
            dve.wait_ge(mv_done, NT)
            nc.vector.tensor_scalar(var_eps[:], mv[:, :, 1], EPS, None, ALU.add).then_inc(var_ready, 1)
            dve.wait_ge(rstd_ready, 1)
            for t in range(NT):
                if plain:
                    out = env.xn[:, t, :]
                else:
                    out = tiles[:, t % ST, :]
                    if t >= ST:
                        dve.wait_ge(turned_ready, t - ST + 1)
                nc.vector.tensor_scalar(out, env.x[:, t, :], mv[:, t, 0:1], rstd[:, t:t + 1],
                                        ALU.subtract, ALU.mult).then_inc(tile_ready, 1)
                if split and t >= 1:
                    low_part(dve, t - 1)
            if split:
                low_part(dve, NT - 1)

        if not plain:
            evacuated = low_done if split else high_done

            @block.tensor
            def _(pe):
                for t in range(NT):
                    pe.wait_ge(tile_ready, t + 1)
                    if t >= ST:
                        pe.wait_ge(evacuated, t - ST + 1)
                    for c in range(KC):
                        last = nc.tensor.transpose(turned[t % ST][:, c, :], tiles[:, t % ST, c * P:(c + 1) * P],
                                                   env.ident[:])
                    last.then_inc(turned_ready, 1)

            @block.scalar
            def _(act):
                for t in range(NT):
                    act.wait_ge(turned_ready, t + 1)
                    out = (env.xth if split else env.xt32)[:, :, t * P:(t + 1) * P]
                    nc.scalar.activation(out, turned[t % ST][:], ACT.Copy).then_inc(high_done, 1)


def load_phase(nc, env, d):
    with ExitStack() as ctx:
        sem = semaphores(nc, ctx, "load_")
        ctx_f = ctx.enter_context(nc.sbuf_tensor("ctx_f", [P, KC, T], F32))
        gates = ctx.enter_context(nc.sbuf_tensor("gates", [P, 8], F32))
        x_in, ctx_in, gates_in, zeroed, made, high_done, low_done, tanh_done = map(
            sem, ("x_in", "ctx_in", "gates_in", "zeroed", "made", "high", "low", "tanh"))
        block = ctx.enter_context(nc.Block())

        @block.sync
        def _(sp):
            sp.dma_start(env.x[:], d["x"].rearrange("(t p) d -> p t d", p=P)).then_inc(x_in, 16)
            sp.dma_start(gates[:], d["gates"]).then_inc(gates_in, 16)
            for c in range(KC):
                sp.dma_start(ctx_f[:, c, :], d["ctxT"][c * P:(c + 1) * P, :]).then_inc(ctx_in, 16)
            sp.wait_ge(x_in, 16)

        @block.gpsimd
        def _(pool):
            nc.gpsimd.memset(env.ident[:], 0.0).then_inc(zeroed, 1)
            nc.gpsimd.memset(env.ones[:], 1.0).then_inc(made, 1)
            pool.wait_ge(zeroed, 1)
            nc.gpsimd.affine_select(out=env.ident[:], in_=env.ident[:], compare_op=ALU.not_equal, fill=1.0, base=0,
                                    pattern=[[-1, P]], channel_multiplier=1).then_inc(made, 1)

        @block.scalar
        def _(act):
            act.wait_ge(gates_in, 16)
            nc.scalar.activation(env.tg[:], gates[:], ACT.Tanh).then_inc(tanh_done, 1)
            for c in range(KC):
                act.wait_ge(ctx_in, 16 * KC)
                nc.scalar.activation(env.cth[:, c, :], ctx_f[:, c, :], ACT.Copy).then_inc(high_done, 1)

        @block.vector
        def _(dve):
            for c in range(KC):
                dve.wait_ge(high_done, c + 1)
                nc.vector.tensor_tensor(env.ctl[:, c, :], ctx_f[:, c, :], env.cth[:, c, :],
                                        ALU.subtract).then_inc(low_done, 1)



G0, H0, HD0 = 8, 4, 128
QCOLS, KVCOLS = H0 * HD0, 2 * HD0
WQ0, WKV0, WO0 = 0, KC * QCOLS, KC * (QCOLS + KVCOLS)
WALL0 = WO0 + H0 * D
CHUNK0 = 512


def attention0_phase(nc, env, d):
    per = 2 * NS
    with ExitStack() as ctx:
        sem = semaphores(nc, ctx, "a0_")
        sb = lambda n, shape, dt: ctx.enter_context(nc.sbuf_tensor(f"a0_{n}", shape, dt))
        ps = lambda n, shape: ctx.enter_context(nc.psum_tensor(f"a0_{n}", shape, F32))
        w_f = sb("w_f", [P, WALL0], F32)
        w_split = [[sb(f"w{g}{part}", [P, WALL0], BF16) for part in range(2)] for g in range(2)]
        mask = sb("mask", [P, S], F32)
        qkw_in = sb("qkw_in", [P, 2], F32)
        qkw = sb("qkw", [P, 1], F32)
        minus_half = sb("minus_half", [P, 16], F32)
        k_f = sb("k_f", [P, ST, HD0], F32)
        k_sq = sb("k_sq", [P, ST, HD0], F32)
        k_ss = sb("k_ss", [P, ST], F32)
        k_se = sb("k_se", [P, ST], F32)
        k_r = sb("k_r", [P, ST], F32)
        k_n = sb("k_n", [P, ST, HD0], F32)
        v = [sb(f"v{part}", [P, 2, ST, HD0], BF16) for part in range(2)]
        kt = [sb(f"kt{part}", [P, W], BF16) for part in range(2)]
        q = [sb(f"q{part}", [P, 2 * ST, H0, S], BF16) for part in range(2)]
        q_sq = sb("q_sq", [P, 2 * ST, H0, S], F32)
        q_se = sb("q_se", [P, 16], F32)
        q_r = sb("q_r", [P, 16], F32)
        sc = sb("sc", [P, 16, S], F32)
        mx = sb("mx", [P, 16], F32)
        den = sb("den", [P, 16], F32)
        rden = sb("rden", [P, 16], F32)
        pt = [sb(f"pt{part}", [P, ST, 2, P], BF16) for part in range(2)]
        ot = [sb(f"ot{part}", [P, H0, W], BF16) for part in range(2)]
        ring = [ps(f"ring{b}", [P, 512]) for b in range(2)]
        scores = ps("scores", [P, 16, S])
        heads = [ps(f"heads{b}", [P, 2, H0, S]) for b in range(2)]
        q_ss = ps("q_ss", [P, 512])
        k_turned = ps("k_turned", [P, 512])

        const_in, const_set, w_in, w_high, w_ready = map(sem, ("const_in", "const_set", "w_in", "w_high", "w_ready"))
        qkw_ready = sem("qkw_ready")
        full, free, act_out = map(sem, ("ring_full", "ring_free", "act_out"))
        ssk_ready, sek_ready, rk_ready, kn_ready = map(sem, ("ssk", "sek", "rk", "kn"))
        kt_full, kt_high, kt_ready = map(sem, ("kt_full", "kt_high", "kt_ready"))
        ssq_ready, seq_ready, rq_ready = map(sem, ("ssq", "seq", "rq"))
        scores_ready, chain, shifted, exp_done, rden_ready, probs_ready = map(
            sem, ("scores", "chain", "shifted", "exp", "rden", "probs"))
        pt_full, pt_high, pt_ready = map(sem, ("pt_full", "pt_high", "pt_ready"))
        heads_full, ot_high, ot_ready = map(sem, ("heads_full", "ot_high", "ot_ready"))
        RING = 10
        KV, QI, OI = 0, 2, 6
        PASSES0 = G0 // 2
        first_high, first_ready = map(sem, ("first_high", "first_ready"))

        block = ctx.enter_context(nc.Block())

        def item(n, k, which):
            m = n * per + k
            if which < OI:
                return which if isinstance(m, int) and m == 0 else m * RING - 4 + which
            last = isinstance(m, int) and m == PASSES0 * per - 1
            return m * RING + (0 if last else 6) + which

        def run(eng, body):
            with eng.Fori(0, PASSES0 - 1) as n:
                for k in range(per):
                    body(n, k, True)
            for k in range(per):
                body(PASSES0 - 1, k, k < per - 1)

        def head_out(part, tp, par):
            return ot[part][:].rearrange("p h (t r q) -> p t r h q", t=ST, r=2)[:, 2 * tp:2 * tp + 2, par, :, :]

        def bank(k, which):
            return ring[which % 2]

        @block.sync
        def _(sp):
            sp.dma_start(mask[0:S, :], d["mask"]).then_inc(const_in, 16)
            sp.dma_start(mask[S:P, :], d["mask"]).then_inc(const_in, 16)
            sp.dma_start(qkw_in[:], d["qk_norm_w"]).then_inc(const_in, 16)
            sp.dma_start(w_f[:], d["w0"][0]).then_inc(w_in, 16)
            sp.wait_ge(first_ready, 10)
            sp.dma_start(w_f[:], d["w0"][1]).then_inc(w_in, 16)
            with sp.Fori(2, G0) as g:
                sp.wait_ge(w_ready, g - 1)
                sp.dma_start(w_f[:], d["w0"][bass.ds(g, 1)].rearrange("a p n -> (a p) n")).then_inc(w_in, 16)
            sp.wait_ge(w_in, 16 * G0)

        @block.gpsimd
        def _(pool):
            nc.gpsimd.memset(minus_half[:], -0.5).then_inc(const_set, 1)
            pool.wait_ge(const_set, 1)

            def split_weights(g, par, chunks):
                for c in chunks:
                    cols = slice(c * CHUNK0, (c + 1) * CHUNK0)
                    nc.gpsimd.tensor_copy(w_split[par][0][:, cols], w_f[:, cols]).then_inc(w_high, 1)
                    pool.wait_ge(w_high, (g - 1) * 10 + c + 1)
                    last = nc.gpsimd.tensor_tensor(w_split[par][1][:, cols], w_f[:, cols],
                                                   w_split[par][0][:, cols], ALU.subtract)
                    if c == 9:
                        last.then_inc(w_ready, 1)

            def normalize(n):
                pool.wait_ge(rden_ready, n + 1)
                nc.gpsimd.tensor_tensor(sc[:], sc[:], rden[:].unsqueeze(2).broadcast_to([P, 16, S]), ALU.mult)\
                    .then_inc(probs_ready, 1)

            def key_factor(m):
                pool.wait_ge(sek_ready, m + 1)
                nc.gpsimd.tensor_tensor(k_r[:], k_se[:], minus_half[:, 0:ST], ALU.pow).then_inc(rk_ready, 1)

            def query_factor(m):
                pool.wait_ge(seq_ready, m + 1)
                nc.gpsimd.tensor_tensor(q_r[:], q_se[:], minus_half[:], ALU.pow).then_inc(rq_ready, 1)

            def body(n, k, front):
                m = n * per + k
                if front:
                    key_factor(m + 1)
                g = 2 * n + k // NS + 1
                more = not (isinstance(g, int) and g == G0)
                if k % NS == 0 and more:
                    pool.wait_ge(w_in, 16 * (g + 1))
                    pool.wait_ge(full, (m - 1) * RING + 6 + OI + 4)
                normalize(m)
                if k % NS < NS - 1 and more:
                    split_weights(g, (k // NS + 1) % 2, (range(0, 4), range(4, 7), range(7, 10))[k % NS])
                if front:
                    query_factor(m + 1)

            key_factor(0)
            query_factor(0)
            run(pool, body)

        @block.tensor
        def _(pe):
            def parts(g, k):
                return w_split[(k // NS) % 2]

            def project_kv(n, k):
                wg = parts(n, k)
                first = isinstance(n, int) and n == k == 0
                if first:
                    pe.wait_ge(first_ready, 10)
                elif k % NS == 0:
                    pe.wait_ge(w_ready, 2 * n + k // NS)
                for h in range(2):
                    out = bank(k, KV + h)
                    it = item(n, k, KV + h)
                    if not first:
                        pe.wait_ge(free, it - 1)
                    for j in range(2):
                        t = (k % NS) * ST + 2 * h + j
                        for c in range(KC):
                            for i, (a, b) in enumerate(PASSES):
                                last = nc.tensor.matmul(
                                    out[:, j * KVCOLS:(j + 1) * KVCOLS], env.ct[a][:, c, t * P:(t + 1) * P],
                                    wg[b][:, WKV0 + c * KVCOLS:WKV0 + (c + 1) * KVCOLS],
                                    start=(c == 0 and i == 0), stop=(c == KC - 1 and i == 2))
                    last.then_inc(full, 1)

            def project_q(n, k, which):
                wg = parts(n, k)
                for h in which:
                    out = bank(k, QI + h)
                    pe.wait_ge(free, item(n, k, QI + h) - 1)
                    for c in range(KC):
                        cols = WQ0 + c * QCOLS + h * HD0
                        for i, (a, b) in enumerate(PASSES):
                            last = nc.tensor.matmul(
                                out[:], wg[a][:, cols:cols + HD0], env.xt[b][:, c, (k % NS) * W:(k % NS + 1) * W],
                                start=(c == 0 and i == 0), stop=(c == KC - 1 and i == 2))
                    last.then_inc(full, 1)

            def turn_k(n, k):
                pe.wait_ge(kn_ready, n * per + k + 1)
                for t in range(ST):
                    last = nc.tensor.transpose(k_turned[:, t * P:(t + 1) * P], k_n[:, t, :], env.ident[:])
                last.then_inc(kt_full, 1)

            def q_squares(n, k):
                pe.wait_ge(act_out, (n * per + k + 1) * 6)
                for t in range(ST):
                    for pair in range(2):
                        for par in range(2):
                            at = 4 * t + 2 * pair + par
                            rows = q_sq[:, 2 * t + par, 2 * pair:2 * pair + 2, :]
                            last = nc.tensor.matmul(q_ss[:, at:at + 1], rows, env.ones[:, 0:1], start=True, stop=True)
                last.then_inc(ssq_ready, 1)

            def score(n, k):
                pe.wait_ge(kt_ready, n * per + k + 1)
                pe.wait_ge(free, item(n, k, QI + 3) + 1)
                for t in range(ST):
                    for pair in range(2):
                        for par in range(2):
                            at = 4 * t + 2 * pair + par
                            cols = slice(t * P + par * S, t * P + (par + 1) * S)
                            for i, (a, b) in enumerate(PASSES):
                                last = nc.tensor.matmul(scores[:, at, :], q[a][:, 2 * t + par, 2 * pair:2 * pair + 2, :],
                                                        kt[b][:, cols], start=(i == 0), stop=(i == 2))
                last.then_inc(scores_ready, 1)

            def turn_probs(n, k):
                pe.wait_ge(probs_ready, n * per + k + 1)
                turned = scores[:].rearrange("p (t u) s -> p t (u s)", t=8)
                source = sc[:].rearrange("p (t u) s -> p t (u s)", t=8)
                for at in range(8):
                    last = nc.tensor.transpose(turned[:, at, :], source[:, at, :], env.ident[:])
                    if at % 4 == 3:
                        last.then_inc(pt_full, 1)

            def mix_values(n, k, tp):
                pe.wait_ge(pt_ready, 2 * (n * per + k) + tp + 1)
                if tp == 1:
                    pe.wait_ge(ot_ready, 4 * (n * per + k) + 2)
                for par in range(2):
                    rows = slice(par * S, (par + 1) * S)
                    for j in range(2):
                        t = 2 * tp + j
                        for i, (a, b) in enumerate(PASSES):
                            last = nc.tensor.matmul(
                                heads[par][:, j, :, :], v[a][rows, k % 2, t, :], pt[b][rows, t, :, :],
                                start=(i == 0), stop=(i == 2))
                    last.then_inc(heads_full, 1)

            def project_out(n, k):
                wg = parts(n, k)
                for t in range(ST):
                    if t % 2 == 0:
                        pe.wait_ge(ot_ready, 4 * (n * per + k) + 2 * (t // 2) + 2)
                    out = bank(k, OI + t)
                    pe.wait_ge(free, item(n, k, OI + t) - 1)
                    for h in range(H0):
                        for i, (a, b) in enumerate(PASSES):
                            last = nc.tensor.matmul(
                                out[:], ot[a][:, h, t * P:(t + 1) * P], wg[b][:, WO0 + h * D:WO0 + (h + 1) * D],
                                start=(h == 0 and i == 0), stop=(h == H0 - 1 and i == 2))
                    last.then_inc(full, 1)

            def body(n, k, front):
                ahead = (n, k + 1) if k < per - 1 else (n + 1, 0)
                score(n, k)
                if front:
                    project_kv(*ahead)
                    project_q(*ahead, range(0, 2))
                turn_probs(n, k)
                if front:
                    project_q(*ahead, range(2, 3))
                mix_values(n, k, 0)
                if front:
                    project_q(*ahead, range(3, 4))
                mix_values(n, k, 1)
                if front:
                    turn_k(*ahead)
                    q_squares(*ahead)
                project_out(n, k)

            project_kv(0, 0)
            project_q(0, 0, range(H0))
            turn_k(0, 0)
            q_squares(0, 0)
            run(pe, body)

        @block.scalar
        def _(act):
            def kv_out(n, k, h):
                act.wait_ge(full, item(n, k, KV + h) + 1)
                src = bank(k, KV + h)[:].rearrange("p (j c) -> p j c", j=2)
                nc.scalar.activation(k_f[:, 2 * h:2 * h + 2, :], src[:, :, 0:HD0], ACT.Copy)
                for j in range(2):
                    last = nc.scalar.activation(k_sq[:, 2 * h + j, :], src[:, j, 0:HD0], ACT.Square,
                                                accum_out=k_ss[:, 2 * h + j:2 * h + j + 1])
                last.then_inc(ssk_ready, 1)
                nc.scalar.activation(v[0][:, k % 2, 2 * h:2 * h + 2, :], src[:, :, HD0:KVCOLS], ACT.Copy)\
                    .then_inc(act_out, 1)

            def q_out(n, k, h):
                act.wait_ge(full, item(n, k, QI + h) + 1)
                src = bank(k, QI + h)[:].rearrange("p (b s) -> p b s", s=S)
                nc.scalar.activation(q_sq[:, :, h, :], src, ACT.Square)
                nc.scalar.activation(q[0][:, :, h, :], src, ACT.Copy).then_inc(act_out, 1)

            def exponent(n, k):
                act.wait_ge(shifted, n * per + k + 1)
                nc.scalar.activation(sc[:], sc[:], ACT.Exp).then_inc(exp_done, 1)

            def probs_out(n, k):
                for h in range(2):
                    act.wait_ge(pt_full, 2 * (n * per + k) + h + 1)
                    nc.scalar.activation(pt[0][:, 2 * h:2 * h + 2, :, :].rearrange("p t u s -> p (t u s)"),
                                         scores[:, 8 * h:8 * h + 8, :].rearrange("p a s -> p (a s)"), ACT.Copy)\
                        .then_inc(pt_high, 1)

            def heads_out(n, k, tp):
                for par in range(2):
                    act.wait_ge(heads_full, 4 * (n * per + k) + 2 * tp + par + 1)
                    nc.scalar.activation(head_out(0, tp, par), heads[par][:], ACT.Copy).then_inc(ot_high, 1)

            def keys_out(n, k):
                act.wait_ge(kt_full, n * per + k + 1)
                nc.scalar.activation(kt[0][:], k_turned[:], ACT.Copy, scale=qkw[:, 0:1]).then_inc(kt_high, 1)

            def body(n, k, front):
                ahead = (n, k + 1) if k < per - 1 else (n + 1, 0)
                if front:
                    for h in range(2):
                        kv_out(*ahead, h)
                exponent(n, k)
                if front:
                    for h in range(2):
                        q_out(*ahead, h)
                probs_out(n, k)
                if front:
                    q_out(*ahead, 2)
                heads_out(n, k, 0)
                if front:
                    q_out(*ahead, 3)
                heads_out(n, k, 1)
                if front:
                    keys_out(*ahead)

            act.wait_ge(w_in, 16)
            for c in range(10):
                cols = slice(c * CHUNK0, (c + 1) * CHUNK0)
                nc.scalar.activation(w_split[0][0][:, cols], w_f[:, cols], ACT.Copy).then_inc(first_high, 1)
            act.wait_ge(qkw_ready, 1)
            for h in range(2):
                kv_out(0, 0, h)
            for h in range(H0):
                q_out(0, 0, h)
            keys_out(0, 0)
            run(act, body)

        @block.vector
        def _(dve):
            dve.wait_ge(const_in, 48)
            nc.vector.tensor_scalar(qkw[:], qkw_in[:, 0:1], qkw_in[:, 1:2], float(np.sqrt(HD0)),
                                    ALU.mult, ALU.mult).then_inc(qkw_ready, 1)
            wide = lambda a: a[:].unsqueeze(2).broadcast_to([P, 16, S])
            LINKS = 4

            def softmax_front(n, k):
                at = (n * per + k) * LINKS
                dve.wait_ge(rq_ready, n * per + k + 1)
                dve.wait_ge(scores_ready, n * per + k + 1)
                nc.vector.tensor_tensor(sc[:], scores[:], wide(q_r), ALU.mult).then_inc(chain, 1)
                dve.wait_ge(chain, at + 1)
                nc.vector.tensor_tensor(sc[:], sc[:], mask[:].unsqueeze(1).broadcast_to([P, 16, S]), ALU.add)\
                    .then_inc(chain, 1)
                dve.wait_ge(chain, at + 2)
                nc.vector.tensor_reduce(mx[:], sc[:], AX.X, ALU.max).then_inc(chain, 1)
                dve.wait_ge(chain, at + 3)
                nc.vector.tensor_tensor(sc[:], sc[:], wide(mx), ALU.subtract).then_inc(shifted, 1)

            def softmax_sum(n, k):
                at = (n * per + k) * LINKS
                dve.wait_ge(exp_done, n * per + k + 1)
                nc.vector.tensor_reduce(den[:], sc[:], AX.X, ALU.add).then_inc(chain, 1)
                dve.wait_ge(chain, at + 4)
                nc.vector.reciprocal(rden[:], den[:]).then_inc(rden_ready, 1)

            def kv_low(n, k, h):
                dve.wait_ge(act_out, 6 * (n * per + k) + h + 1)
                src = bank(k, KV + h)[:].rearrange("p (j c) -> p j c", j=2)
                tiles = slice(2 * h, 2 * h + 2)
                nc.vector.tensor_tensor(v[1][:, k % 2, tiles, :], src[:, :, HD0:KVCOLS], v[0][:, k % 2, tiles, :],
                                        ALU.subtract).then_inc(free, 1)

            def q_low(n, k, h):
                dve.wait_ge(act_out, 6 * (n * per + k) + 2 + h + 1)
                nc.vector.tensor_tensor(q[1][:, :, h, :], bank(k, QI + h)[:].rearrange("p (b s) -> p b s", s=S),
                                        q[0][:, :, h, :], ALU.subtract)\
                    .then_inc(free, 1)

            def probs_low(n, k):
                for h in range(2):
                    dve.wait_ge(pt_high, 2 * (n * per + k) + h + 1)
                    flat = [pt[part][:, 2 * h:2 * h + 2, :, :].rearrange("p t u s -> p (t u s)") for part in range(2)]
                    nc.vector.tensor_tensor(flat[1], scores[:, 8 * h:8 * h + 8, :].rearrange("p a s -> p (a s)"),
                                            flat[0], ALU.subtract).then_inc(pt_ready, 1)

            def heads_low(n, k, tp):
                for par in range(2):
                    dve.wait_ge(ot_high, 4 * (n * per + k) + 2 * tp + par + 1)
                    nc.vector.tensor_tensor(head_out(1, tp, par), heads[par][:], head_out(0, tp, par),
                                            ALU.subtract).then_inc(ot_ready, 1)

            def keys_squared(n, k):
                dve.wait_ge(ssk_ready, 2 * (n * per + k) + 2)
                nc.vector.tensor_scalar(k_se[:], k_ss[:], HD0 * EPS, None, ALU.add).then_inc(sek_ready, 1)

            def keys_scaled(n, k):
                dve.wait_ge(rk_ready, n * per + k + 1)
                for t in range(ST):
                    last = nc.vector.tensor_scalar(k_n[:, t, :], k_f[:, t, :], k_r[:, t:t + 1], None, ALU.mult)
                last.then_inc(kn_ready, 1)

            def norms_out(n, k):
                dve.wait_ge(kt_high, n * per + k + 1)
                nc.vector.scalar_tensor_tensor(kt[1][:], k_turned[:], qkw[:, 0:1], kt[0][:],
                                               ALU.mult, ALU.subtract).then_inc(kt_ready, 1)
                dve.wait_ge(ssq_ready, n * per + k + 1)
                nc.vector.tensor_scalar(q_se[:], q_ss[:, 0:16], HD0 * EPS, None, ALU.add).then_inc(seq_ready, 1)

            def add_out(n, k):
                for t in range(ST):
                    dve.wait_ge(full, item(n, k, OI + t) + 1)
                    tile = env.x[:, (k % NS) * ST + t, :]
                    nc.vector.scalar_tensor_tensor(tile, bank(k, OI + t)[:], env.tg[:, 0:1], tile,
                                                   ALU.mult, ALU.add).then_inc(free, 1)

            def body(n, k, front):
                ahead = (n, k + 1) if k < per - 1 else (n + 1, 0)
                softmax_front(n, k)
                if front:
                    for h in range(2):
                        kv_low(*ahead, h)
                    keys_squared(*ahead)
                softmax_sum(n, k)
                if front:
                    keys_scaled(*ahead)
                    for h in range(2):
                        q_low(*ahead, h)
                probs_low(n, k)
                if front:
                    q_low(*ahead, 2)
                heads_low(n, k, 0)
                if front:
                    q_low(*ahead, 3)
                heads_low(n, k, 1)
                if front:
                    norms_out(*ahead)
                add_out(n, k)

            for c in range(10):
                cols = slice(c * CHUNK0, (c + 1) * CHUNK0)
                dve.wait_ge(first_high, c + 1)
                nc.vector.tensor_tensor(w_split[0][1][:, cols], w_f[:, cols], w_split[0][0][:, cols], ALU.subtract)\
                    .then_inc(first_ready, 1)
            for h in range(2):
                kv_low(0, 0, h)
            keys_squared(0, 0)
            keys_scaled(0, 0)
            for h in range(H0):
                q_low(0, 0, h)
            norms_out(0, 0)
            run(dve, body)



class StepNorm:

    def __init__(self, nc, env, ctx, name, mode):
        sem = semaphores(nc, ctx, f"{name}_norm_")
        sb = lambda n, shape, dt: ctx.enter_context(nc.sbuf_tensor(f"{name}_norm_{n}", shape, dt))
        self.nc, self.env, self.mode = nc, env, mode
        self.stats = sb("stats", [P, ST, 6], F32)
        self.mv = sb("mv", [P, ST, 2], F32)
        self.var_eps = sb("var_eps", [P, ST], F32)
        self.rstd = sb("rstd", [P, ST], F32)
        self.pace = sb("pace", [P, 1], F32)
        self.minus_half = sb("minus_half", [P, ST], F32)
        copies = 2 if mode == "plain" else 1
        self.tiles = sb("tiles", [P, copies, ST, D], F32)
        if mode == "f32":
            self.xt32 = sb("xt", [P, 2, KC, W], F32)
        if mode == "split":
            self.xt = [sb(f"xt{part}", [P, 2, KC, W], BF16) for part in range(2)]
        if mode != "plain":
            self.turned = [ctx.enter_context(nc.psum_tensor(f"{name}_norm_turned{b}", [P, KC, P], F32))
                           for b in range(2)]
        self.const_set, self.stats_done, self.mv_done, self.var_ready, self.rstd_ready = map(
            sem, ("const", "stats", "mv", "var", "rstd"))
        self.tile_ready, self.turned_ready, self.high_done, self.low_done = map(
            sem, ("tile", "turned", "high", "low"))
        self.evacuated = self.low_done if mode == "split" else self.high_done

    def pool_start(self, pool):
        self.nc.gpsimd.memset(self.minus_half[:], -0.5).then_inc(self.const_set, 1)
        pool.wait_ge(self.const_set, 1)

    def pool(self, pool, n):
        pool.wait_ge(self.var_ready, n + 1)
        self.nc.gpsimd.tensor_tensor(self.rstd[:], self.var_eps[:], self.minus_half[:], ALU.pow)\
            .then_inc(self.rstd_ready, 1)

    def dve(self, dve, n, par, tile):
        nc = self.nc
        for t in range(ST):
            last = nc.vector.bn_stats(self.stats[:, t, :], self.env.x[:, tile + t, :])
        last.then_inc(self.stats_done, 1)
        dve.wait_ge(self.stats_done, n + 1)
        nc.vector.memset(self.pace[:], 0.0)
        for t in range(ST):
            last = nc.vector.bn_aggr(self.mv[:, t, :], self.stats[:, t, :])
        last.then_inc(self.mv_done, 1)
        dve.wait_ge(self.mv_done, n + 1)
        nc.vector.tensor_scalar(self.var_eps[:], self.mv[:, :, 1], EPS, None, ALU.add).then_inc(self.var_ready, 1)
        if self.mode != "plain":
            dve.wait_ge(self.turned_ready, ST * n)
        dve.wait_ge(self.rstd_ready, n + 1)
        for t in range(ST):
            nc.vector.tensor_scalar(self.tiles[:, par if self.mode == "plain" else 0, t, :],
                                    self.env.x[:, tile + t, :], self.mv[:, t, 0:1], self.rstd[:, t:t + 1],
                                    ALU.subtract, ALU.mult).then_inc(self.tile_ready, 1)

    def dve_low(self, dve, n, par):
        for t in range(ST):
            dve.wait_ge(self.high_done, ST * n + t + 1)
            cols = slice(t * P, (t + 1) * P)
            self.nc.vector.tensor_tensor(self.xt[1][:, par, :, cols], self.turned[t % 2][:],
                                         self.xt[0][:, par, :, cols], ALU.subtract).then_inc(self.low_done, 1)

    def pe(self, pe, n, t0=0, t1=ST):
        for t in range(t0, t1):
            pe.wait_ge(self.tile_ready, ST * n + t + 1)
            pe.wait_ge(self.evacuated, ST * n + t - 1 if t >= 1 else ST * n)
            for c in range(KC):
                last = self.nc.tensor.transpose(self.turned[t % 2][:, c, :], self.tiles[:, 0, t, c * P:(c + 1) * P],
                                                self.env.ident[:])
            last.then_inc(self.turned_ready, 1)

    def act(self, act, n, par):
        for t in range(ST):
            act.wait_ge(self.turned_ready, ST * n + t + 1)
            out = (self.xt[0] if self.mode == "split" else self.xt32)[:, par, :, t * P:(t + 1) * P]
            self.nc.scalar.activation(out, self.turned[t % 2][:], ACT.Copy).then_inc(self.high_done, 1)


def first_tile(j, k, ahead):
    if not ahead:
        return j * (2 * ST) + k * ST
    return j * (2 * ST) + ST if k == 0 else j * (-2 * ST) + 2 * ST



E_ = 4


def experts_phase(nc, env, d, name, rank, top2, lora_scale, gate):
    R = E_ * rank
    RB = R if top2 else R + 1
    with ExitStack() as ctx:
        sem = semaphores(nc, ctx, f"{name}_")
        sb = lambda n, shape, dt=F32: ctx.enter_context(nc.sbuf_tensor(f"{name}_{n}", shape, dt))
        ps = lambda n, shape: ctx.enter_context(nc.psum_tensor(f"{name}_{n}", shape, F32))
        norm = StepNorm(nc, env, ctx, name, "f32")
        down = sb("down", [P, KC, R + E_])
        up = sb("up", [RB, D])
        dense = None if top2 else sb("dense", [P, KC, D])
        earlier = sb("earlier", [P, E_, E_])
        lg = sb("lg", [P, ST, E_])
        greater = sb("greater", [P, ST, E_, E_])
        equal = sb("equal", [P, ST, E_, E_])
        rank_of = sb("rank", [P, ST, E_])
        keep = sb("keep", [P, ST, E_])
        mx = sb("mx", [P, ST])
        den = sb("den", [P, ST])
        rden = sb("rden", [P, ST])
        ex = sb("ex", [P, ST, E_])
        gates = sb("gates", [P, ST, E_])
        mid = sb("mid", [P, ST, P])
        mid_t = sb("mid_t", [RB, W])
        a_ps = ps("a", [P, ST, P])
        m_ps = ps("m", [P, W])
        out_ps = [ps(f"out{b}", [P, D]) for b in range(2)]
        w_in, const_set, a_full, link, shifted, ex_done, mid_ready, m_full, mid_t_ready, out_full, out_free = map(
            sem, ("w_in", "const", "a_full", "link", "shifted", "ex", "mid", "m_full", "mid_t", "out_full",
                  "out_free"))
        rden_done = sem("rden_done")
        LINKS = 9 if top2 else 3
        block = ctx.enter_context(nc.Block())

        @block.sync
        def _(sp):
            sp.dma_start(down[:], d[f"{name}_down"]).then_inc(w_in, 16)
            sp.dma_start(up[:], d[f"{name}_up"]).then_inc(w_in, 16)
            if not top2:
                sp.dma_start(dense[:], d[f"{name}_dense"]).then_inc(w_in, 16)
            sp.wait_ge(w_in, 32 if top2 else 48)

        @block.gpsimd
        def _(pool):
            norm.pool_start(pool)
            nc.gpsimd.memset(mid[:, :, RB:P], 0.0).then_inc(const_set, 1)
            if top2:
                for e in range(E_):
                    nc.gpsimd.memset(earlier[:, e, 0:e] if e else earlier[:, 0, 0:1], 1.0 if e else 0.0)\
                        .then_inc(const_set, 1)
                    if e:
                        nc.gpsimd.memset(earlier[:, e, e:E_], 0.0).then_inc(const_set, 1)
                nc.gpsimd.memset(earlier[:, 0, 1:E_], 0.0).then_inc(const_set, 1)
            else:
                nc.gpsimd.memset(mid[:, :, R:RB], 1.0).then_inc(const_set, 1)
            norm.pool(pool, 0)
            with pool.Fori(0, NS // 2) as j:
                for k in range(2):
                    norm.pool(pool, 2 * j + k + 1)

        @block.tensor
        def _(pe):
            def rest(n, par):
                pe.wait_ge(mid_ready, n + 1)
                for t in range(ST):
                    last = nc.tensor.transpose(m_ps[:, t * P:(t + 1) * P], mid[:, t, :], env.ident[:])
                last.then_inc(m_full, 1)
                for t in range(ST):
                    pe.wait_ge(out_free, ST * n + t - 1 if t else ST * n)
                    if not top2:
                        for c in range(KC):
                            nc.tensor.matmul(out_ps[t % 2][:], norm.xt32[:, par, c, t * P:(t + 1) * P],
                                             dense[:, c, :], start=(c == 0), stop=False)
                    if t == 0:
                        pe.wait_ge(mid_t_ready, n + 1)
                    nc.tensor.matmul(out_ps[t % 2][:], mid_t[:, t * P:(t + 1) * P], up[:],
                                     start=top2, stop=True).then_inc(out_full, 1)

            norm.pe(pe, 0)
            pe.wait_ge(w_in, 32 if top2 else 48)
            with pe.Fori(0, NS // 2) as j:
                for k in range(2):
                    n = 2 * j + k
                    pe.wait_ge(norm.high_done, ST * n + ST)
                    for t in range(ST):
                        for c in range(KC):
                            last = nc.tensor.matmul(a_ps[:, t, 0:R + E_], norm.xt32[:, k, c, t * P:(t + 1) * P],
                                                    down[:, c, :], start=(c == 0), stop=(c == KC - 1))
                    last.then_inc(a_full, 1)
                    norm.pe(pe, n + 1)
                    rest(n, k)

        @block.scalar
        def _(act):
            norm.act(act, 0, 0)
            with act.Fori(0, NS // 2) as j:
                for k in range(2):
                    n = 2 * j + k
                    act.wait_ge(shifted, n + 1)
                    nc.scalar.activation(ex[:], ex[:], ACT.Exp).then_inc(ex_done, 1)
                    norm.act(act, n + 1, 1 - k)
                    act.wait_ge(m_full, n + 1)
                    nc.scalar.activation(mid_t[:], m_ps[0:RB, :], ACT.Copy).then_inc(mid_t_ready, 1)

        @block.vector
        def _(dve):
            dve.wait_ge(const_set, 9 if top2 else 2)
            wide = lambda a: a.unsqueeze(2).broadcast_to([P, ST, E_])
            norm.dve(dve, 0, 0, 0)
            with dve.Fori(0, NS // 2) as j:
                for k in range(2):
                    n = 2 * j + k
                    at = n * LINKS
                    step = 0
                    dve.wait_ge(a_full, n + 1)
                    nc.vector.tensor_copy(lg[:], a_ps[:, :, R:R + E_]).then_inc(link, 1)
                    dve.wait_ge(link, at + 1)
                    nc.vector.tensor_reduce(mx[:], lg[:], AX.X, ALU.max).then_inc(link, 1)
                    dve.wait_ge(link, at + 2)
                    nc.vector.tensor_tensor(ex[:], lg[:], wide(mx[:]), ALU.subtract).then_inc(shifted, 1)
                    if top2:
                        mine = lg[:].unsqueeze(3).broadcast_to([P, ST, E_, E_])
                        other = lg[:].unsqueeze(2).broadcast_to([P, ST, E_, E_])
                        nc.vector.tensor_tensor(greater[:], other, mine, ALU.is_gt).then_inc(link, 1)
                        nc.vector.tensor_tensor(equal[:], other, mine, ALU.is_equal).then_inc(link, 1)
                        dve.wait_ge(link, at + 4)
                        nc.vector.tensor_tensor(equal[:], equal[:], earlier[:].unsqueeze(1).broadcast_to(
                            [P, ST, E_, E_]), ALU.mult).then_inc(link, 1)
                        dve.wait_ge(link, at + 5)
                        nc.vector.tensor_tensor(greater[:], greater[:], equal[:], ALU.add).then_inc(link, 1)
                        dve.wait_ge(link, at + 6)
                        nc.vector.tensor_reduce(rank_of[:], greater[:], AX.X, ALU.add).then_inc(link, 1)
                        dve.wait_ge(link, at + 7)
                        dve.wait_ge(ex_done, n + 1)
                        nc.vector.scalar_tensor_tensor(ex[:], rank_of[:], 1.5, ex[:], ALU.is_lt, ALU.mult)\
                            .then_inc(link, 1)
                        dve.wait_ge(link, at + 8)
                    dve.wait_ge(ex_done, n + 1)
                    nc.vector.tensor_reduce(den[:], ex[:], AX.X, ALU.add).then_inc(link, 1)
                    dve.wait_ge(link, at + LINKS)
                    nc.vector.reciprocal(rden[:], den[:]).then_inc(rden_done, 1)
                    dve.wait_ge(rden_done, 2 * n + 1)
                    nc.vector.scalar_tensor_tensor(gates[:], ex[:], lora_scale, wide(rden[:]), ALU.mult, ALU.mult)\
                        .then_inc(rden_done, 1)
                    dve.wait_ge(rden_done, 2 * n + 2)
                    nc.vector.tensor_tensor(
                        mid[:, :, 0:R].rearrange("p t (e r) -> p t e r", e=E_),
                        a_ps[:, :, 0:R].rearrange("p t (e r) -> p t e r", e=E_),
                        gates[:].unsqueeze(3).broadcast_to([P, ST, E_, rank]), ALU.mult).then_inc(mid_ready, 1)
                    norm.dve(dve, n + 1, 1 - k, first_tile(j, k, True))
                    for t in range(ST):
                        dve.wait_ge(out_full, ST * n + t + 1)
                        tile = env.x[:, first_tile(j, k, False) + t, :]
                        nc.vector.scalar_tensor_tensor(tile, out_ps[t % 2][:], env.tg[:, gate:gate + 1], tile,
                                                       ALU.mult, ALU.add).then_inc(out_free, 1)



def attention1_phase(nc, env, d):
    scale = float(D) ** -0.5
    with ExitStack() as ctx:
        sem = semaphores(nc, ctx, "a1_")
        sb = lambda n, shape, dt=F32: ctx.enter_context(nc.sbuf_tensor(f"a1_{n}", shape, dt))
        ps = lambda n, shape: ctx.enter_context(nc.psum_tensor(f"a1_{n}", shape, F32))
        norm = StepNorm(nc, env, ctx, "a1", "split")
        w_f = sb("w_f", [P, 2, KC, D])
        w = [sb(f"w{part}", [P, 2, KC, D], BF16) for part in range(2)]
        bias = sb("bias", [P, 2, KC])
        c_rows = sb("c_rows", [P, 2, ST, D])
        qk = [sb(f"qk{part}", [P, 2, KC, W], BF16) for part in range(2)]
        sc = sb("sc", [P, ST, S])
        mx = sb("mx", [P, ST])
        den = sb("den", [P, ST])
        rden = sb("rden", [P, ST])
        probs = sb("probs", [P, ST, P])
        pt = sb("pt", [P, ST, P])
        ring = [ps(f"ring{b}", [P, W]) for b in range(2)]
        s_ps = ps("s", [P, ST, P])
        t_ps = ps("t", [P, ST, P])
        c_in = [sem(f"c_in{k}") for k in range(2)]
        (w_in, w_high, w_ready, const_set, full, high, free, s_full, link, shifted, ex_done, probs_ready,
         t_full, pt_ready) = map(sem, (
             "w_in", "w_high", "w_ready", "const", "full", "high", "free", "s_full", "link", "shifted",
             "ex", "probs", "t_full", "pt"))
        RING = 2 * KC + ST
        block = ctx.enter_context(nc.Block())

        @block.sync
        def _(sp):
            sp.dma_start(w_f[:, 0], d["a1_wq"]).then_inc(w_in, 16)
            sp.dma_start(w_f[:, 1], d["a1_wk"]).then_inc(w_in, 16)
            sp.dma_start(bias[:], d["a1_bias"]).then_inc(w_in, 16)
            rows = d["ctx"].rearrange("(t p) d -> p t d", p=P)
            for k in range(2):
                sp.dma_start(c_rows[:, k], rows[:, k * ST:(k + 1) * ST, :]).then_inc(c_in[k], 16)
            for k in range(2):
                sp.wait_ge(full, RING * (k + 1))
                sp.dma_start(c_rows[:, k], rows[:, (k + 2) * ST:(k + 3) * ST, :]).then_inc(c_in[k], 16)
            for k in range(2):
                sp.wait_ge(c_in[k], 32)

        @block.gpsimd
        def _(pool):
            norm.pool_start(pool)
            nc.gpsimd.memset(probs[:], 0.0).then_inc(const_set, 1)
            norm.pool(pool, 0)
            pool.wait_ge(w_in, 48)
            for i in range(2):
                for c in range(KC):
                    nc.gpsimd.tensor_copy(w[0][:, i, c, :], w_f[:, i, c, :]).then_inc(w_high, 1)
                    pool.wait_ge(w_high, i * KC + c + 1)
                    nc.gpsimd.tensor_tensor(w[1][:, i, c, :], w_f[:, i, c, :], w[0][:, i, c, :],
                                            ALU.subtract).then_inc(w_ready, 1)
            with pool.Fori(0, NS // 2) as j:
                for k in range(2):
                    norm.pool(pool, 2 * j + k + 1)

        @block.tensor
        def _(pe):
            def project(n, par, i):
                for m in range(KC):
                    it = i * KC + m
                    pe.wait_ge(free, RING * n + it - 1 if it else RING * n)
                    for c in range(KC):
                        for p, (a, b) in enumerate(PASSES):
                            moving = norm.xt[b][:, par, c, :] if i == 0 else env.ct[b][:, c, bass.ds(n * W, W)]
                            last = nc.tensor.matmul(ring[it % 2][:], w[a][:, i, c, m * P:(m + 1) * P], moving,
                                                    start=(c == 0 and p == 0), stop=(c == KC - 1 and p == 2))
                    last.then_inc(full, 1)

            norm.pe(pe, 0)
            pe.wait_ge(w_ready, 2 * KC)
            with pe.Fori(0, NS // 2) as j:
                for k in range(2):
                    n = 2 * j + k
                    pe.wait_ge(norm.low_done, ST * n + ST)
                    project(n, k, 0)
                    project(n, k, 1)
                    norm.pe(pe, n + 1)
                    pe.wait_ge(free, RING * n + 2 * KC)
                    for t in range(ST):
                        cols = slice(t * P, (t + 1) * P)
                        for m in range(KC):
                            for p, (a, b) in enumerate(PASSES):
                                last = nc.tensor.matmul(s_ps[:, t, :], qk[a][:, 0, m, cols], qk[b][:, 1, m, cols],
                                                        start=(m == 0 and p == 0), stop=(m == KC - 1 and p == 2))
                    last.then_inc(s_full, 1)
                    pe.wait_ge(probs_ready, n + 1)
                    for t in range(ST):
                        last = nc.tensor.transpose(t_ps[:, t, :], probs[:, t, :], env.ident[:])
                    last.then_inc(t_full, 1)
                    pe.wait_ge(c_in[k], j * 16 + 16)
                    pe.wait_ge(pt_ready, n + 1)
                    for t in range(ST):
                        it = 2 * KC + t
                        pe.wait_ge(free, RING * n + it - 1)
                        nc.tensor.matmul(ring[it % 2][:], pt[:, t, :], c_rows[:, k, t, :],
                                         start=True, stop=True).then_inc(full, 1)

        @block.scalar
        def _(act):
            norm.act(act, 0, 0)
            act.wait_ge(w_in, 48)
            with act.Fori(0, NS // 2) as j:
                for k in range(2):
                    n = 2 * j + k
                    for it in range(2 * KC):
                        act.wait_ge(full, RING * n + it + 1)
                        nc.scalar.activation(qk[0][:, it // KC, it % KC, :], ring[it % 2][:], ACT.Identity,
                                             bias=bias[:, it // KC, it % KC:it % KC + 1]).then_inc(high, 1)
                    norm.act(act, n + 1, 1 - k)
                    act.wait_ge(shifted, n + 1)
                    nc.scalar.activation(sc[:], sc[:], ACT.Exp, scale=scale).then_inc(ex_done, 1)
                    act.wait_ge(t_full, n + 1)
                    nc.scalar.activation(pt[:], t_ps[:], ACT.Copy).then_inc(pt_ready, 1)

        @block.vector
        def _(dve):
            dve.wait_ge(const_set, 1)
            wide = lambda a: a[:].unsqueeze(2).broadcast_to([P, ST, S])
            halves = [slice(0, S), slice(S, P)]
            norm.dve(dve, 0, 0, 0)
            norm.dve_low(dve, 0, 0)
            with dve.Fori(0, NS // 2) as j:
                for k in range(2):
                    n = 2 * j + k
                    norm.dve(dve, n + 1, 1 - k, first_tile(j, k, True))
                    for it in range(2 * KC):
                        dve.wait_ge(high, 2 * KC * n + it + 1)
                        nc.vector.scalar_tensor_tensor(
                            qk[1][:, it // KC, it % KC, :], ring[it % 2][:], bias[:, it // KC, it % KC:it % KC + 1],
                            qk[0][:, it // KC, it % KC, :], ALU.add, ALU.subtract).then_inc(free, 1)
                    norm.dve_low(dve, n + 1, 1 - k)
                    dve.wait_ge(s_full, n + 1)
                    for rows in halves:
                        nc.vector.tensor_copy(sc[rows], s_ps[rows, :, rows]).then_inc(link, 1)
                    dve.wait_ge(link, 5 * n + 2)
                    nc.vector.tensor_reduce(mx[:], sc[:], AX.X, ALU.max).then_inc(link, 1)
                    dve.wait_ge(link, 5 * n + 3)
                    nc.vector.tensor_tensor(sc[:], sc[:], wide(mx), ALU.subtract).then_inc(shifted, 1)
                    dve.wait_ge(ex_done, n + 1)
                    nc.vector.tensor_reduce(den[:], sc[:], AX.X, ALU.add).then_inc(link, 1)
                    dve.wait_ge(link, 5 * n + 4)
                    nc.vector.reciprocal(rden[:], den[:]).then_inc(link, 1)
                    dve.wait_ge(link, 5 * n + 5)
                    for rows in halves:
                        last = nc.vector.tensor_tensor(probs[rows, :, rows], sc[rows], wide(rden)[rows], ALU.mult)
                    last.then_inc(probs_ready, 1)
                    for t in range(ST):
                        it = 2 * KC + t
                        dve.wait_ge(full, RING * n + it + 1)
                        tile = env.x[:, first_tile(j, k, False) + t, :]
                        nc.vector.scalar_tensor_tensor(tile, ring[it % 2][:], env.tg[:, 1:2], tile,
                                                       ALU.mult, ALU.add).then_inc(free, 1)



G2, J2, HD2 = 8, 4, 16
KV2 = G2 * HD2


def attention2_phase(nc, env, d):
    scale = float(HD2) ** -0.5
    NB = 2 * ST
    with ExitStack() as ctx:
        sem = semaphores(nc, ctx, "a2_")
        sb = lambda n, shape, dt=F32: ctx.enter_context(nc.sbuf_tensor(f"a2_{n}", shape, dt))
        ps = lambda n, shape: ctx.enter_context(nc.psum_tensor(f"a2_{n}", shape, F32))
        norm = StepNorm(nc, env, ctx, "a2", "split")
        WCOLS = D + 2 * KV2
        w_f = sb("w_f", [P, KC, WCOLS])
        w = [sb(f"w{part}", [P, KC, WCOLS], BF16) for part in range(2)]
        wo = sb("wo", [P, J2, D])
        bo = sb("bo", [1, D])
        qk_bias = sb("qk_bias", [P, J2 + 1])
        v_bias = sb("v_bias", [P, KV2])
        g_mask = sb("g_mask", [P, G2])
        v_mask = sb("v_mask", [P, KV2])
        q = sb("q", [P, NB, J2, S])
        kt = sb("kt", [P, W])
        k_block = sb("k_block", [P, 4, G2, S])
        v = sb("v", [P, ST, KV2])
        v_swap = sb("v_swap", [P, ST, KV2])
        v_block = sb("v_block", [P, NB, KV2])
        sc = sb("sc", [P, 3, 2 * G2, S])
        mx = sb("mx", [P, 2 * G2])
        den = sb("den", [P, 2, 2 * G2])
        rden = sb("rden", [P, 2, 2 * G2])
        pt = sb("pt", [P, 2, 4, 2 * P])
        y = sb("y", [P, J2, W])
        ring = [ps(f"ring{b}", [P, W]) for b in range(2)]
        s_ps = ps("s", [P, 2 * G2, S])
        t_ps = ps("t", [P, 4, 2, P])
        (w_in, w_high, w_ready, full, act_free, dve_free, v_moved, v_block_ready, k_block_ready, s_full, link, shifted,
         ex_done, rden_ready, probs_ready, t_full, pt_ready, summed) = map(sem, (
             "w_in", "w_high", "w_ready", "full", "act_free", "dve_free", "v_moved", "v_block", "k_block", "s_full", "link",
             "shifted", "ex", "rden", "probs", "t_full", "pt", "summed"))
        LOADS = 7
        RING = J2 + 2 + 2 * ST
        KI, VI = J2, J2 + 1
        HI = lambda t: J2 + 2 + 2 * t
        block = ctx.enter_context(nc.Block())
        ACT_READS = [*range(J2 + 1), *(HI(t) for t in range(ST))]
        DVE_READS = [VI, *(HI(t) + 1 for t in range(ST))]

        def is_read(n, it):
            prev = (it - 2) % RING
            sem_, reads = (act_free, ACT_READS) if prev in ACT_READS else (dve_free, DVE_READS)
            return sem_, n * len(reads) + (reads.index(prev) + 1) % (len(reads) if it < 2 else RING)

        @block.sync
        def _(sp):
            for tile, name in ((w_f, "a2_w"), (wo, "a2_wo"), (bo, "a2_bo"), (qk_bias, "a2_qk_bias"),
                               (v_bias, "a2_v_bias"), (g_mask, "g_mask"), (v_mask, "v_mask")):
                sp.dma_start(tile[:], d[name]).then_inc(w_in, 16)
            with sp.Fori(0, NS) as n:
                sp.wait_ge(dve_free, len(DVE_READS) * n + 1)
                sp.dma_start(v_swap[S:P], v[0:S]).then_inc(v_moved, 16)
                sp.dma_start(v_swap[0:S], v[S:P]).then_inc(v_moved, 16)
            sp.wait_ge(v_moved, 32 * NS)

        @block.gpsimd
        def _(pool):
            norm.pool_start(pool)
            norm.pool(pool, 0)
            pool.wait_ge(w_in, 16 * LOADS)
            for c in range(KC):
                nc.gpsimd.tensor_copy(w[0][:, c, :], w_f[:, c, :]).then_inc(w_high, 1)
                pool.wait_ge(w_high, c + 1)
                nc.gpsimd.tensor_tensor(w[1][:, c, :], w_f[:, c, :], w[0][:, c, :], ALU.subtract).then_inc(w_ready, 1)

            def block_keys(n, b):
                if b == 0:
                    pool.wait_ge(act_free, len(ACT_READS) * n + J2 + 1)
                if b >= 4:
                    pool.wait_ge(s_full, NB * n + b - 3)
                nc.gpsimd.tensor_tensor(k_block[:, b % 4], kt[:, b * S:(b + 1) * S].unsqueeze(1).broadcast_to([P, G2, S]),
                                        g_mask[:].unsqueeze(2).broadcast_to([P, G2, S]), ALU.mult)\
                    .then_inc(k_block_ready, 1)

            with pool.Fori(0, NS // 2) as j:
                for k in range(2):
                    n = 2 * j + k
                    norm.pool(pool, n + 1)
                    for b in range(3):
                        block_keys(n, b)
                    for b in range(NB):
                        if b + 3 < NB:
                            block_keys(n, b + 3)
                        pool.wait_ge(rden_ready, NB * n + b + 1)
                        nc.gpsimd.tensor_tensor(sc[:, b % 3], sc[:, b % 3],
                                                rden[:, b % 2].unsqueeze(2).broadcast_to([P, 2 * G2, S]), ALU.mult)\
                            .then_inc(probs_ready, 1)

        @block.tensor
        def _(pe):
            def score(n, b):
                pe.wait_ge(k_block_ready, NB * n + b + 1)
                if b:
                    pe.wait_ge(shifted, NB * n + b)
                for jp in range(2):
                    last = nc.tensor.matmul(s_ps[:, jp * G2:(jp + 1) * G2, :], q[:, b, 2 * jp:2 * jp + 2, :],
                                            k_block[:, b % 4], start=True, stop=True)
                last.then_inc(s_full, 1)

            def turn(n, b):
                if b:
                    pe.wait_ge(pt_ready, NB * n + b)
                pe.wait_ge(probs_ready, NB * n + b + 1)
                for jp in range(2):
                    for gp in range(4):
                        at = jp * G2 + 2 * gp
                        last = nc.tensor.transpose(t_ps[:, gp, jp, :], sc[:, b % 3, at:at + 2, :], env.ident[:])
                last.then_inc(t_full, 1)

            def mix(n, b):
                it = HI(b // 2)
                if b % 2 == 0:
                    pe.wait_ge(*is_read(n, it))
                if b == 0:
                    pe.wait_ge(v_block_ready, n + 1)
                pe.wait_ge(pt_ready, NB * n + b + 1)
                for gp in range(4):
                    rows = slice(32 * gp, 32 * gp + 32)
                    last = nc.tensor.matmul(ring[it % 2][rows, (b % 2) * 256:(b % 2) * 256 + 256], v_block[:, b, rows],
                                            pt[:, b % 2, gp, :], start=True, stop=True, tile_position=(0, 32 * gp))
                if b % 2:
                    last.then_inc(full, 1)

            def project_out(n, t):
                it = HI(t) + 1
                pe.wait_ge(*is_read(n, it))
                nc.tensor.matmul(ring[it % 2][:], env.ones[0:1, :], bo[:], start=True, stop=False)
                pe.wait_ge(act_free, len(ACT_READS) * n + J2 + 1 + t + 1)
                for j in range(J2):
                    last = nc.tensor.matmul(ring[it % 2][:], y[:, j, t * P:(t + 1) * P], wo[:, j, :],
                                            start=False, stop=(j == J2 - 1))
                last.then_inc(full, 1)

            norm.pe(pe, 0)
            pe.wait_ge(w_ready, KC)
            with pe.Fori(0, NS // 2) as jj:
                for k in range(2):
                    n = 2 * jj + k
                    pe.wait_ge(norm.low_done, ST * n + ST)
                    for it in range(J2 + 1):
                        pe.wait_ge(*is_read(n, it))
                        for c in range(KC):
                            for p, (a, b) in enumerate(PASSES):
                                moving = norm.xt[b][:, k, c, :] if it < J2 else env.ct[b][:, c, bass.ds(n * W, W)]
                                last = nc.tensor.matmul(ring[it % 2][:], w[a][:, c, it * P:(it + 1) * P], moving,
                                                        start=(c == 0 and p == 0), stop=(c == KC - 1 and p == 2))
                        last.then_inc(full, 1)
                    pe.wait_ge(*is_read(n, VI))
                    for t in range(ST):
                        for c in range(KC):
                            for p, (a, b) in enumerate(PASSES):
                                last = nc.tensor.matmul(
                                    ring[VI % 2][:, t * P:(t + 1) * P], env.ct[a][:, c, bass.ds(n * W + t * P, P)],
                                    w[b][:, c, D + KV2:WCOLS], start=(c == 0 and p == 0), stop=(c == KC - 1 and p == 2))
                    last.then_inc(full, 1)
                    norm.pe(pe, n + 1)
                    score(n, 0)
                    for b in range(NB + 3):
                        if b + 1 < NB:
                            score(n, b + 1)
                        if 1 <= b <= NB:
                            turn(n, b - 1)
                        if b >= 4 and b % 2 == 0:
                            project_out(n, b // 2 - 2)
                        if 2 <= b <= NB + 1:
                            mix(n, b - 2)

        def heads_out(act, n, t):
            act.wait_ge(full, RING * n + HI(t) + 1)
            nc.scalar.activation(y[:].rearrange("p j (t r q) -> p t r j q", t=ST, r=2)[:, t],
                                 ring[HI(t) % 2][:].rearrange("p (r j q) -> p r j q", r=2, j=J2), ACT.Copy)\
                .then_inc(act_free, 1)

        @block.scalar
        def _(act):
            norm.act(act, 0, 0)
            act.wait_ge(w_in, 16 * LOADS)

            def exponent(n, b):
                act.wait_ge(shifted, NB * n + b + 1)
                nc.scalar.activation(sc[:, b % 3], sc[:, b % 3], ACT.Exp, scale=scale).then_inc(ex_done, 1)

            with act.Fori(0, NS // 2) as jj:
                for k in range(2):
                    n = 2 * jj + k
                    for it in range(J2 + 1):
                        act.wait_ge(full, RING * n + it + 1)
                        src = ring[it % 2][:]
                        if it < J2:
                            nc.scalar.activation(q[:, :, it, :], src.rearrange("p (b s) -> p b s", s=S), ACT.Identity,
                                                 bias=qk_bias[:, it:it + 1]).then_inc(act_free, 1)
                        else:
                            nc.scalar.activation(kt[:], src, ACT.Identity,
                                                 bias=qk_bias[:, it:it + 1]).then_inc(act_free, 1)
                    norm.act(act, n + 1, 1 - k)
                    exponent(n, 0)
                    for b in range(NB + 2):
                        if b + 1 < NB:
                            exponent(n, b + 1)
                        if 1 <= b <= NB:
                            act.wait_ge(t_full, NB * n + b)
                            nc.scalar.activation(pt[:, (b - 1) % 2].rearrange("p g n -> p (g n)"),
                                                 t_ps[:].rearrange("p g j n -> p (g j n)"), ACT.Copy)\
                                .then_inc(pt_ready, 1)
                        if b >= 3 and b % 2:
                            heads_out(act, n, b // 2 - 1)

        def add(dve, n, t, tile0):
            dve.wait_ge(full, RING * n + HI(t) + 2)
            tile = env.x[:, tile0 + t, :]
            nc.vector.scalar_tensor_tensor(tile, ring[(HI(t) + 1) % 2][:], env.tg[:, 2:3], tile, ALU.mult, ALU.add)\
                .then_inc(dve_free, 1)


        @block.vector
        def _(dve):
            dve.wait_ge(w_in, 16 * LOADS)
            wide = lambda a: a[:].unsqueeze(2).broadcast_to([P, 2 * G2, S])
            norm.dve(dve, 0, 0, 0)
            norm.dve_low(dve, 0, 0)

            def front(n, b):
                dve.wait_ge(s_full, NB * n + b + 1)
                nc.vector.tensor_reduce(mx[:], s_ps[:], AX.X, ALU.max).then_inc(link, 1)
                dve.wait_ge(link, NB * n + b + 1)
                nc.vector.tensor_tensor(sc[:, b % 3], s_ps[:], wide(mx), ALU.subtract).then_inc(shifted, 1)

            def total(n, b):
                dve.wait_ge(ex_done, NB * n + b + 1)
                nc.vector.tensor_reduce(den[:, b % 2], sc[:, b % 3], AX.X, ALU.add).then_inc(summed, 1)
                dve.wait_ge(summed, NB * n + b + 1)
                if b >= 2:
                    dve.wait_ge(probs_ready, NB * n + b - 1)
                nc.vector.reciprocal(rden[:, b % 2], den[:, b % 2]).then_inc(rden_ready, 1)

            with dve.Fori(0, NS // 2) as jj:
                for k in range(2):
                    n = 2 * jj + k
                    norm.dve(dve, n + 1, 1 - k, first_tile(jj, k, True))
                    dve.wait_ge(full, RING * n + VI + 1)
                    nc.vector.tensor_tensor(v[:], ring[VI % 2][:].rearrange("p (t c) -> p t c", t=ST),
                                            v_bias[:].unsqueeze(1).broadcast_to([P, ST, KV2]), ALU.add)\
                        .then_inc(dve_free, 1)
                    norm.dve_low(dve, n + 1, 1 - k)
                    front(n, 0)
                    dve.wait_ge(v_moved, 32 * n + 32)
                    for rows, r in ((slice(0, S), 0), (slice(S, P), 1)):
                        for own in (0, 1):
                            src = (v if own == r else v_swap)[rows]
                            out = v_block[rows].rearrange("p (t r) c -> p t r c", r=2)[:, :, own, :]
                            last = nc.vector.tensor_tensor(out, src, v_mask[rows].unsqueeze(1).broadcast_to(
                                [S, ST, KV2]), ALU.mult)
                    last.then_inc(v_block_ready, 1)
                    for b in range(NB + 4):
                        if b + 1 < NB:
                            front(n, b + 1)
                        if b < NB:
                            total(n, b)
                        if b >= 5 and b % 2:
                            add(dve, n, b // 2 - 2, first_tile(jj, k, False))



QMAX = 127.0
ROUND = 1.5 * 2.0 ** 23


def quantized_phase(nc, env, d):
    with ExitStack() as ctx:
        sem = semaphores(nc, ctx, "f2_")
        sb = lambda n, shape, dt=F32: ctx.enter_context(nc.sbuf_tensor(f"f2_{n}", shape, dt))
        norm = StepNorm(nc, env, ctx, "f2", "plain")
        reps = sb("reps", [P, 4, D])
        GAMMA, BETA, B1, B3 = range(4)
        w_f = sb("w_f", [P, 2, KC, D])
        w_am = sb("w_am", [P, 2 * KC])
        w_s = sb("w_s", [P, 2 * KC])
        w_inv = sb("w_inv", [P, 2 * KC])
        w_q = sb("w_q", [P, 2, KC, D], BF16)
        w_t = sb("w_t", [P, 2, KC, D], BF16)
        w_srow = sb("w_srow", [P, 2, D])
        h = sb("h", [P, 2, ST, D])
        am = sb("am", [P, 2, ST])
        s = sb("s", [P, 2, 2, ST])
        inv = sb("inv", [P, 2, ST])
        st2 = sb("st2", [P, ST, 6])
        mv2 = sb("mv2", [P, ST, 2])
        ve2 = sb("ve2", [P, ST])
        rstd2 = sb("rstd2", [P, ST])
        pace = sb("pace", [P, 1])
        qx = sb("qx", [P, 2, ST, D], BF16)
        qt = sb("qt", [P, 2, KC, W], BF16)
        o = sb("o", [P, ST, D])
        ident16 = sb("ident16", [P, P], BF16)
        t_ps = [ctx.enter_context(nc.psum_tensor(f"f2_t{b}", [P, KC, P], BF16)) for b in range(2)]
        out_ps = [ctx.enter_context(nc.psum_tensor(f"f2_o{b}", [P, D], F32)) for b in range(2)]
        row_ps = [ctx.enter_context(nc.psum_tensor(f"f2_r{b}", [P, D], F32)) for b in range(2)]
        (in_, id_set, wl, w_rounded, w_q_ready, w_t_full, w_t_ready, row_full, row_ready) = map(sem, (
            "in", "id", "wl", "w_rounded", "w_q", "w_t_full", "w_t", "row_full", "row"))
        (l_front, ve_ready, r2_ready, fr_rounded, mid_rounded, fr_q, mid_q, t_full, qt_ready, o_full, h1,
         h1b, h1g, l_mid, oo, oob) = map(sem, (
             "l_front", "ve", "r2", "fr_rounded", "mid_rounded", "fr_q", "mid_q", "t_full", "qt", "o_full",
             "h1", "h1b", "h1g", "l_mid", "oo", "oob"))
        added = sem("added")
        block = ctx.enter_context(nc.Block())

        @block.sync
        def _(sp):
            sp.dma_start(w_f[:], d["f2_w"]).then_inc(in_, 16)
            sp.dma_start(reps[:], d["f2_reps"]).then_inc(in_, 16)
            sp.wait_ge(in_, 32)

        @block.gpsimd
        def _(pool):
            norm.pool_start(pool)
            nc.gpsimd.tensor_copy(ident16[:], env.ident[:]).then_inc(id_set, 1)

            def front(n):
                norm.pool(pool, n)
                pool.wait_ge(ve_ready, n + 1)
                nc.gpsimd.tensor_tensor(rstd2[:], ve2[:], norm.minus_half[:], ALU.pow).then_inc(r2_ready, 1)

            front(0)
            pool.wait_ge(in_, 32)
            with pool.Fori(0, NS // 2) as j:
                for k in range(2):
                    n = 2 * j + k
                    for t in range(ST):
                        pool.wait_ge(h1, ST * n + t + 1)
                        nc.gpsimd.tensor_tensor(o[:, t, :], o[:, t, :], reps[:, B1, :], ALU.add).then_inc(h1b, 1)
                    front(n + 1)
                    for t in range(ST):
                        pool.wait_ge(oo, ST * n + t + 1)
                        nc.gpsimd.tensor_tensor(o[:, t, :], o[:, t, :], reps[:, B3, :], ALU.add).then_inc(oob, 1)

        @block.tensor
        def _(pe):
            pe.wait_ge(id_set, 1)
            for i in range(2 * KC):
                pe.wait_ge(w_q_ready, i + 1)
                if i >= 2:
                    pe.wait_ge(w_t_ready, i - 1)
                for c in range(KC):
                    last = nc.tensor.transpose(t_ps[i % 2][:, c, :], w_q[:, i // KC, i % KC, c * P:(c + 1) * P],
                                               ident16[:])
                last.then_inc(w_t_full, 1)
            for i in range(2):
                for m in range(KC):
                    at = i * KC + m
                    last = nc.tensor.matmul(row_ps[i][:, m * P:(m + 1) * P], w_s[:, at:at + 1].broadcast_to([P, P]),
                                            env.ident[:], start=True, stop=True)
                last.then_inc(row_full, 1)
            pe.wait_ge(w_t_ready, 2 * KC)

            def product(n, i, par):
                at = 2 * ST * n + ST * i
                for t in range(ST):
                    pe.wait_ge(fr_q if i == 0 else mid_q, ST * n + t + 1)
                    pe.wait_ge(qt_ready, at + t - 1 if (t or i) else at)
                    for c in range(KC):
                        last = nc.tensor.transpose(t_ps[t % 2][:, c, :], qx[:, i, t, c * P:(c + 1) * P], ident16[:])
                    last.then_inc(t_full, 1)
                for t in range(ST):
                    pe.wait_ge(qt_ready, at + t + 1)
                    if t >= 2:
                        pe.wait_ge((h1, oo)[i], ST * n + t - 1)
                    else:
                        pe.wait_ge((oo, h1)[i], ST * n + ST * i)
                    for c in range(KC):
                        last = nc.tensor.matmul(out_ps[t % 2][:], qt[:, i, c, t * P:(t + 1) * P], w_t[:, i, c, :],
                                                start=(c == 0), stop=(c == KC - 1))
                    last.then_inc(o_full, 1)

            with pe.Fori(0, NS // 2) as j:
                for k in range(2):
                    product(2 * j + k, 0, k)
                    product(2 * j + k, 1, k)

        @block.scalar
        def _(act):
            for i in range(2 * KC):
                act.wait_ge(w_rounded, i + 1)
                nc.scalar.activation(w_q[:, i // KC, i % KC, :], w_f[:, i // KC, i % KC, :], ACT.Copy,
                                     bias=-ROUND).then_inc(w_q_ready, 1)
            for i in range(2 * KC):
                act.wait_ge(w_t_full, i + 1)
                nc.scalar.activation(w_t[:, i // KC, :, (i % KC) * P:(i % KC + 1) * P], t_ps[i % 2][:], ACT.Copy)\
                    .then_inc(w_t_ready, 1)

            def whole(n, i, t):
                act.wait_ge(fr_rounded if i == 0 else mid_rounded, ST * n + t + 1)
                nc.scalar.activation(qx[:, i, t, :], h[:, i, t, :], ACT.Copy, bias=-ROUND)\
                    .then_inc(fr_q if i == 0 else mid_q, 1)

            def turned(n, i):
                for t in range(ST):
                    act.wait_ge(t_full, 2 * ST * n + ST * i + t + 1)
                    nc.scalar.activation(qt[:, i, :, t * P:(t + 1) * P], t_ps[t % 2][:], ACT.Copy)\
                        .then_inc(qt_ready, 1)

            for t in range(ST):
                whole(0, 0, t)
            with act.Fori(0, NS // 2) as j:
                for k in range(2):
                    n = 2 * j + k
                    turned(n, 0)
                    for t in range(ST):
                        act.wait_ge(h1b, ST * n + t + 1)
                        nc.scalar.activation(h[:, 1, t, :], o[:, t, :], ACT.Gelu).then_inc(h1g, 1)
                    for t in range(ST):
                        whole(n + 1, 0, t)
                    for t in range(ST):
                        whole(n, 1, t)
                    turned(n, 1)

        @block.vector
        def _(dve):
            def scales(am_ap, s_ap, inv_ap, chain, at):
                nc.vector.tensor_scalar(s_ap, am_ap, 1.0 / QMAX, 1e-8, ALU.mult, ALU.max).then_inc(chain, 1)
                dve.wait_ge(chain, at)
                nc.vector.reciprocal(inv_ap, s_ap).then_inc(chain, 1)
                dve.wait_ge(chain, at + 1)

            def rounded(tile, inv_col, chain, at, done):
                nc.vector.tensor_scalar(tile, tile, inv_col, QMAX, ALU.mult, ALU.min).then_inc(chain, 1)
                dve.wait_ge(chain, at)
                nc.vector.tensor_scalar(tile, tile, -QMAX, ROUND, ALU.max, ALU.add).then_inc(done, 1)

            FR = 7 + ST
            MID = 3 + ST

            def front(n, par, tile):
                at = FR * n
                norm.dve(dve, n, par, tile)
                dve.wait_ge(norm.tile_ready, ST * n + ST)
                for t in range(ST):
                    last = nc.vector.bn_stats(st2[:, t, :], norm.tiles[:, par, t, :])
                last.then_inc(l_front, 1)
                dve.wait_ge(l_front, at + 1)
                nc.vector.memset(pace[:], 0.0)
                for t in range(ST):
                    last = nc.vector.bn_aggr(mv2[:, t, :], st2[:, t, :])
                last.then_inc(l_front, 1)
                dve.wait_ge(l_front, at + 2)
                nc.vector.tensor_scalar(ve2[:], mv2[:, :, 1], EPS, None, ALU.add).then_inc(ve_ready, 1)
                dve.wait_ge(fr_q, ST * n)
                for t in range(ST):
                    last = nc.vector.scalar_tensor_tensor(h[:, 0, t, :], norm.tiles[:, par, t, :], mv2[:, t, 0:1],
                                                          reps[:, GAMMA, :], ALU.subtract, ALU.mult)
                last.then_inc(l_front, 1)
                dve.wait_ge(l_front, at + 3)
                dve.wait_ge(r2_ready, n + 1)
                for t in range(ST):
                    last = nc.vector.scalar_tensor_tensor(h[:, 0, t, :], h[:, 0, t, :], rstd2[:, t:t + 1],
                                                          reps[:, BETA, :], ALU.mult, ALU.add)
                last.then_inc(l_front, 1)
                dve.wait_ge(l_front, at + 4)
                nc.vector.tensor_reduce(am[:, 0, :], h[:, 0], AX.X, ALU.max, apply_absolute_value=True)\
                    .then_inc(l_front, 1)
                dve.wait_ge(l_front, at + 5)
                scales(am[:, 0, :], s[:, 0, par, :], inv[:, 0, :], l_front, at + 6)
                for t in range(ST):
                    nc.vector.tensor_scalar(h[:, 0, t, :], h[:, 0, t, :], inv[:, 0, t:t + 1], QMAX, ALU.mult,
                                            ALU.min).then_inc(l_front, 1)
                for t in range(ST):
                    dve.wait_ge(l_front, at + 7 + t + 1)
                    nc.vector.tensor_scalar(h[:, 0, t, :], h[:, 0, t, :], -QMAX, ROUND, ALU.max, ALU.add)\
                        .then_inc(fr_rounded, 1)

            dve.wait_ge(in_, 32)
            nc.vector.tensor_reduce(w_am[:], w_f[:].rearrange("p i c d -> p (i c) d"), AX.X, ALU.max,
                                    apply_absolute_value=True).then_inc(wl, 1)
            dve.wait_ge(wl, 1)
            scales(w_am[:], w_s[:], w_inv[:], wl, 2)
            for i in range(2 * KC):
                rounded(w_f[:, i // KC, i % KC, :], w_inv[:, i:i + 1], wl, 4 + i, w_rounded)
            front(0, 0, 0)
            dve.wait_ge(row_full, 1)
            nc.vector.tensor_copy(w_srow[:, 0, :], row_ps[0][:]).then_inc(row_ready, 1)
            dve.wait_ge(row_full, 2)
            nc.vector.tensor_scalar(w_srow[:, 1, :], row_ps[1][:], env.tg[:, 6:7], None, ALU.mult)\
                .then_inc(row_ready, 1)
            nc.vector.tensor_scalar(reps[:, B3, :], reps[:, B3, :], env.tg[:, 6:7], None, ALU.mult)\
                .then_inc(row_ready, 1)
            dve.wait_ge(row_ready, 3)
            with dve.Fori(0, NS // 2) as j:
                for k in range(2):
                    n = 2 * j + k
                    dve.wait_ge(added, ST * n)
                    for t in range(ST):
                        dve.wait_ge(o_full, 2 * ST * n + t + 1)
                        nc.vector.scalar_tensor_tensor(o[:, t, :], out_ps[t % 2][:], s[:, 0, k, t:t + 1],
                                                       w_srow[:, 0, :], ALU.mult, ALU.mult).then_inc(h1, 1)
                    front(n + 1, 1 - k, first_tile(j, k, True))
                    dve.wait_ge(h1g, ST * n + ST)
                    nc.vector.tensor_reduce(am[:, 1, :], h[:, 1], AX.X, ALU.max, apply_absolute_value=True)\
                        .then_inc(l_mid, 1)
                    dve.wait_ge(l_mid, MID * n + 1)
                    scales(am[:, 1, :], s[:, 1, k, :], inv[:, 1, :], l_mid, MID * n + 2)
                    for t in range(ST):
                        nc.vector.tensor_scalar(h[:, 1, t, :], h[:, 1, t, :], inv[:, 1, t:t + 1], QMAX, ALU.mult,
                                                ALU.min).then_inc(l_mid, 1)
                    for t in range(ST):
                        dve.wait_ge(l_mid, MID * n + 3 + t + 1)
                        nc.vector.tensor_scalar(h[:, 1, t, :], h[:, 1, t, :], -QMAX, ROUND, ALU.max, ALU.add)\
                            .then_inc(mid_rounded, 1)
                    for t in range(ST):
                        dve.wait_ge(o_full, 2 * ST * n + ST + t + 1)
                        nc.vector.scalar_tensor_tensor(o[:, t, :], out_ps[t % 2][:], s[:, 1, k, t:t + 1],
                                                       w_srow[:, 1, :], ALU.mult, ALU.mult).then_inc(oo, 1)
                    for t in range(ST):
                        dve.wait_ge(oob, ST * n + t + 1)
                        tile = env.x[:, first_tile(j, k, False) + t, :]
                        nc.vector.tensor_tensor(tile, tile, o[:, t, :], ALU.add).then_inc(added, 1)



H3, HD3 = 8, 64
M3 = H3 * HD3 // P
NC = D // P


def attention3_phase(nc, env, d):
    with ExitStack() as ctx:
        sem = semaphores(nc, ctx, "a3_")
        sb = lambda n, shape, dt=F32: ctx.enter_context(nc.sbuf_tensor(f"a3_{n}", shape, dt))
        ps = lambda n, shape: ctx.enter_context(nc.psum_tensor(f"a3_{n}", shape, F32))
        w_f = sb("w_f", [P, 2, H3 * HD3])
        w = [sb(f"w{part}", [P, 2, H3 * HD3], BF16) for part in range(2)]
        wv = sb("wv", [P, M3, P])
        wo = sb("wo", [P, M3, HD3])
        u_t = sb("u_t", [P, H3, HD3])
        cols = sb("cols", [P, 2])
        gain = sb("gain", [P, 1])
        half_ones = sb("half_ones", [P, 2])
        minus_half = sb("minus_half", [P, 2 * NC])
        stats = sb("stats", [P, 6])
        mv = sb("mv", [P, 2])
        pace = sb("pace", [P, 1])
        var_eps = sb("var_eps", [P, 1])
        rstd = sb("rstd", [P, 1])
        rows_f = sb("rows_f", [P, 2, 2, D])
        rows = [sb(f"rows{part}", [P, 2, 2, D], BF16) for part in range(2)]
        nmax = sb("nmax", [P, 2, M3])
        ksum = sb("ksum", [P, 2, M3])
        rksum = sb("rksum", [P, M3])
        kexp = sb("kexp", [P, M3, D])
        kt = [sb(f"kt{part}", [P, NC, M3 * P], BF16) for part in range(2)]
        g = sb("g", [P, H3 * HD3])
        m_t = sb("m_t", [P, M3, HD3])
        qmax = sb("qmax", [P, NC, H3])
        qe = sb("qe", [P, 2, NC, H3 * HD3])
        qsum = sb("qsum", [P, NC * H3])
        rqsum = sb("rqsum", [P, NC * H3])
        qt = sb("qt", [P, M3, D])
        u = sb("u", [P, 2, D])
        sq = sb("sq", [P, 2, D])
        ssm = sb("ssm", [P, 2 * NC])
        rn = sb("rn", [P, 2 * NC])
        rn_rows = sb("rn_rows", [P, 2 * NC, HD3])
        vec = sb("vec", [P, D])
        proj = [ps(f"proj{b}", [P, 512]) for b in range(4)]
        turn = [ps(f"turn{b}", [P, 512]) for b in range(2)]
        small = ps("small", [P, 512])
        o_ps = ps("o", [P, D])
        in_, c_in0, c_in1 = map(sem, ("in", "c_in0", "c_in1"))
        c_in = (c_in0, c_in1)
        const_set, w_high, w_ready, u_full, u_ready, gain_ready = map(
            sem, ("const", "w_high", "w_ready", "u_full", "u_ready", "gain"))
        ln_link, var_ready, rstd_ready, xn_ready, split_link, c_ready, x_ready = map(
            sem, ("ln_link", "var", "rstd", "xn", "split_link", "c_ready", "x_ready"))
        (proj_full, kmax_ready, k_free, q_link, q_free, qe_done, sum_link, qr_ready, qp_ready) = map(sem, (
            "proj_full", "kmax", "k_free", "q_link", "q_free", "qe", "sum_link", "qr", "qp"))
        (kt_full, kt_high, kt_ready, qt_full, qt_ready, g_full, g_ready, m_full, rk_done, m_ready, o_full) = map(sem, (
            "kt_full", "kt_high", "kt_ready", "qt_full", "qt_ready", "g_full", "g_ready", "m_full", "rk", "m_ready",
            "o_full"))
        u_ready2, ss_full, ss_read, rn_link, rn_ready, rep_full, rep_read, x_done = map(
            sem, ("u", "ss_full", "ss_read", "rn_link", "rn", "rep_full", "rep_read", "x_done"))
        LOADS = 5
        CTX, XN = 0, 1

        class At:

            def __init__(self, j, c):
                self.b, self.c, self.j = 4 * j + c, c, j
                self.first = isinstance(j, int) and self.b == 0
                self.second = isinstance(j, int) and self.b == 1
                self.old = not isinstance(j, int) or self.b >= 4

            def tile(self, back=0):
                return 2 * self.j + (self.c - back) // 2

        def run(eng, steps):
            for c in range(4):
                steps(At(0, c), True, c >= 1, c == 3, False, c % 2 == 0)
            with eng.Fori(1, B // 4 - 1) as j:
                for c in range(4):
                    steps(At(j, c), True, True, c % 2 == 1, c % 2 == 0, c % 2 == 0)
            for c in range(4):
                steps(At(B // 4 - 1, c), True, True, c % 2 == 1, c % 2 == 0, c == 0)
            steps(At(B // 4, 0), False, True, False, True, False)
            steps(At(B // 4, 1), False, False, True, False, False)
            steps(At(B // 4, 2), False, False, False, True, False)

        block = ctx.enter_context(nc.Block())

        @block.sync
        def _(sp):
            for tile, name in ((w_f, "a3_w"), (wv, "a3_wv"), (wo, "a3_wo"), (cols, "a3_cols"),
                               (half_ones, "half_ones")):
                sp.dma_start(tile[:], d[name]).then_inc(in_, 16)
            rows_d = d["ctx"].rearrange("(t p) n -> p t n", p=P)
            for k in range(2):
                sp.dma_start(rows_f[:, k, CTX, :], rows_d[:, k, :]).then_inc(c_in[k], 16)
            with sp.Fori(0, NT // 2 - 1) as j:
                for k in range(2):
                    sp.wait_ge(c_ready, 2 * j + k + 1)
                    sp.dma_start(rows_f[:, k, CTX, :], rows_d[:, bass.ds(2 * j + k + 2, 1), :].rearrange(
                        "p t n -> p (t n)")).then_inc(c_in[k], 16)
            for k in range(2):
                sp.wait_ge(c_in[k], 16 * NT // 2)

        @block.gpsimd
        def _(pool):
            nc.gpsimd.memset(minus_half[:], -0.5).then_inc(const_set, 1)
            pool.wait_ge(const_set, 1)
            pool.wait_ge(in_, 16 * LOADS)
            for i in range(2):
                nc.gpsimd.tensor_copy(w[0][:, i, :], w_f[:, i, :]).then_inc(w_high, 1)
                pool.wait_ge(w_high, i + 1)
                nc.gpsimd.tensor_tensor(w[1][:, i, :], w_f[:, i, :], w[0][:, i, :], ALU.subtract).then_inc(w_ready, 1)

            def norm(t):
                pool.wait_ge(var_ready, t + 1)
                nc.gpsimd.tensor_tensor(rstd[:], var_eps[:], minus_half[:, 0:1], ALU.pow).then_inc(rstd_ready, 1)

            def split(t, k, which, ready, value, source_ready):
                pool.wait_ge(source_ready, value)
                if not (isinstance(t, int) and t < 2):
                    pool.wait_ge(proj_full, 16 * (t - 1))
                nc.gpsimd.tensor_tensor(rows[0][:, k, which, :], rows_f[:, k, which, :], ones_row(), ALU.mult)\
                    .then_inc(split_link, 1)
                pool.wait_ge(split_link, 2 * t + (1 if which == CTX else 2))
                nc.gpsimd.tensor_tensor(rows[1][:, k, which, :], rows_f[:, k, which, :], rows[0][:, k, which, :],
                                        ALU.subtract).then_inc(ready, 1)

            ones_row = lambda: env.ones[:, 0:1].broadcast_to([P, D])

            def split_tile(t, k, j):
                split(t, k, CTX, c_ready, 16 * (j + 1), c_in[k])
                split(t, k, XN, x_ready, t + 1, xn_ready)

            norm(0)
            split_tile(0, 0, 0)

            def steps(at, main, prev, ss, rep, ahead):
                b, c = at.b, at.c
                t = at.tile()
                if ahead:
                    norm(t + 1)
                if main:
                    pool.wait_ge(qr_ready, b + 1)
                    shape = [P, NC * H3, HD3]
                    e = qe[:, c % 2].rearrange("p n (h d) -> p (n h) d", h=H3)
                    nc.gpsimd.tensor_tensor(e, e, rqsum[:].unsqueeze(2).broadcast_to(shape), ALU.mult)\
                        .then_inc(qp_ready, 1)
                if ahead:
                    split_tile(t + 1, (c // 2 + 1) % 2, at.j + c // 2)
                if ss:
                    t = at.tile(3)
                    pool.wait_ge(ss_read, t + 1)
                    nc.gpsimd.tensor_tensor(rn[:], ssm[:], minus_half[:], ALU.pow).then_inc(rn_link, 1)
                    pool.wait_ge(rn_link, t + 1)
                    wide = [P, 2 * NC, HD3]
                    nc.gpsimd.tensor_tensor(rn_rows[:], rn[:].unsqueeze(2).broadcast_to(wide),
                                            env.ones[:, 0:1].unsqueeze(2).broadcast_to(wide), ALU.mult)\
                        .then_inc(rn_ready, 1)

            run(pool, steps)

        @block.tensor
        def _(pe):
            pe.wait_ge(in_, 16 * LOADS)
            for h in range(H3):
                r = slice((h % 2) * HD3, (h % 2 + 1) * HD3)
                last = nc.tensor.matmul(turn[h % 2][:, (h // 2) * HD3:(h // 2 + 1) * HD3], wv[r, h // 2, :],
                                        wo[r, h // 2, :], start=True, stop=True)
            last.then_inc(u_full, 1)
            pe.wait_ge(u_ready, 2)
            pe.wait_ge(w_ready, 2)

            def steps(at, main, prev, ss, rep, ahead):
                b, c = at.b, at.c
                k, r = c // 2, slice((c % 2) * S, (c % 2 + 1) * S)
                t = at.tile()
                first = at.first
                if main:
                    if c % 2 == 0:
                        pe.wait_ge(c_ready, t + 1)
                    for m in range(M3):
                        if not first:
                            pe.wait_ge(q_free, 4 * (b - 1) + m + 1)
                        for i, (a, bb) in enumerate(PASSES):
                            mm = nc.tensor.matmul(proj[m][:], w[a][r, 0, m * P:(m + 1) * P], rows[bb][r, k, CTX, :],
                                                  start=(i == 0), stop=(i == 2))
                        mm.then_inc(proj_full, 1)
                    if c % 2 == 0:
                        pe.wait_ge(x_ready, t + 1)
                    for n in range(NC):
                        pe.wait_ge(k_free, 4 * b + n + 1)
                        for i, (a, bb) in enumerate(PASSES):
                            mm = nc.tensor.matmul(proj[n][:], rows[a][r, k, XN, n * P:(n + 1) * P], w[bb][r, 1, :],
                                                  start=(i == 0), stop=(i == 2))
                        mm.then_inc(proj_full, 1)
                if prev:
                    if at.old:
                        pe.wait_ge(rep_read if c % 2 else ss_read, at.tile(5 if c % 2 else 4) + 1)
                    elif not at.second:
                        pe.wait_ge(m_ready, 2 * (b - 1))
                    pe.wait_ge(kt_ready, 4 * b)
                    for n in range(NC):
                        for i, (a, bb) in enumerate(PASSES):
                            mm = nc.tensor.matmul(small[:], env.ct[a][:, n, bass.ds(at.tile(1) * P, P)],
                                                  kt[bb][:, n, :], start=(n == 0 and i == 0),
                                                  stop=(n == NC - 1 and i == 2))
                    mm.then_inc(g_full, 1)
                if prev:
                    pr = slice(((c - 1) % 2) * S, ((c - 1) % 2 + 1) * S)
                    for m in range(M3):
                        if m == 0:
                            pe.wait_ge(qp_ready, b)
                        if m >= 2:
                            pe.wait_ge(qt_ready, 4 * (b - 1) + m - 1)
                        for n in range(NC):
                            mm = nc.tensor.transpose(turn[m % 2][:, n * P:(n + 1) * P],
                                                     qe[:, (c - 1) % 2, n, m * P:(m + 1) * P], env.ident[:])
                        mm.then_inc(qt_full, 1)
                    pe.wait_ge(g_ready, b)
                    for m in range(M3):
                        mm = nc.tensor.matmul(small[:, m * P:(m + 1) * P], g[pr, m * P:(m + 1) * P],
                                              u_t[pr, 2 * m:2 * m + 2, :].rearrange("p h o -> p (h o)"),
                                              start=True, stop=True)
                    mm.then_inc(m_full, 1)
                if main:
                    for n in range(NC):
                        if n >= 2:
                            pe.wait_ge(kt_ready, 4 * b + n - 1)
                        elif prev:
                            pe.wait_ge(qt_ready, 4 * (b - 1) + n + 3)
                        for m in range(M3):
                            mm = nc.tensor.transpose(turn[n % 2][:, m * P:(m + 1) * P], kexp[:, m, n * P:(n + 1) * P],
                                                     env.ident[:])
                        mm.then_inc(kt_full, 1)
                if (ss or rep) and (main or prev):
                    pe.wait_ge(m_ready, 2 * b)
                if ss:
                    t3 = at.tile(3)
                    pe.wait_ge(u_ready2, t3 + 1)
                    if not main:
                        pe.wait_ge(rep_read, t3)
                    for n in range(NC):
                        mm = nc.tensor.matmul(small[:, 2 * n:2 * n + 2], sq[:, ((c - 3) // 2) % 2, n * P:(n + 1) * P],
                                              half_ones[:], start=True, stop=True)
                    mm.then_inc(ss_full, 1)
                if rep:
                    t4 = at.tile(4)
                    pe.wait_ge(rn_ready, t4 + 1)
                    for n in range(NC):
                        mm = nc.tensor.matmul(small[:, n * P:(n + 1) * P],
                                              rn_rows[:, 2 * n:2 * n + 2, :].rearrange("p s o -> p (s o)"),
                                              env.ident[:], start=True, stop=True)
                    mm.then_inc(rep_full, 1)
                if prev:
                    if (c - 1) % 2 == 0 and not at.second:
                        pe.wait_ge(u_ready2, at.tile(1))
                    pe.wait_ge(qt_ready, 4 * (b - 1) + 4)
                    pe.wait_ge(m_ready, 2 * b)
                    for m in range(M3):
                        mm = nc.tensor.matmul(o_ps[pr, :], m_t[:, m, :], qt[:, m, :], start=(m == 0),
                                              stop=(m == M3 - 1))
                    mm.then_inc(o_full, 1)

            run(pe, steps)

        @block.scalar
        def _(act):
            act.wait_ge(in_, 16 * LOADS)

            def query_exps(b, c, which):
                for n in which:
                    act.wait_ge(q_free, 4 * b + n + 1)
                    nc.scalar.activation(qe[:, c % 2, n, :], qe[:, c % 2, n, :], ACT.Exp).then_inc(qe_done, 1)

            def steps(at, main, prev, ss, rep, ahead):
                b, c = at.b, at.c
                if main:
                    for m in range(M3):
                        act.wait_ge(kmax_ready, 4 * b + m + 1)
                        nc.scalar.activation(kexp[:, m, :], proj[m][:], ACT.Exp, bias=nmax[:, c % 2, m:m + 1],
                                             accum_out=ksum[:, c % 2, m:m + 1]).then_inc(k_free, 1)
                    query_exps(b, c, range(0, 2))
                if prev:
                    act.wait_ge(g_full, b)
                    pr = slice(((c - 1) % 2) * S, ((c - 1) % 2 + 1) * S)
                    nc.scalar.activation(g[pr, :], small[pr, :], ACT.Copy).then_inc(g_ready, 1)
                    for m in range(M3):
                        act.wait_ge(qt_full, 4 * (b - 1) + m + 1)
                        nc.scalar.activation(qt[:, m, :], turn[m % 2][:], ACT.Copy).then_inc(qt_ready, 1)
                if main:
                    for n in range(NC):
                        act.wait_ge(kt_full, 4 * b + n + 1)
                        nc.scalar.activation(kt[0][:, n, :], turn[n % 2][:], ACT.Copy).then_inc(kt_high, 1)
                    query_exps(b, c, range(2, NC))
                if prev and (c - 1) % 2 == 1:
                    act.wait_ge(o_full, b)
                    k = ((c - 1) // 2) % 2
                    nc.scalar.activation(u[:, k, :], o_ps[:], ACT.Identity, bias=cols[:, 0:1])
                    nc.scalar.activation(sq[:, k, :], o_ps[:], ACT.Square, bias=cols[:, 0:1]).then_inc(u_ready2, 1)

            run(act, steps)

        @block.vector
        def _(dve):
            dve.wait_ge(in_, 16 * LOADS)
            nc.vector.tensor_scalar(gain[:], cols[:, 1:2], env.tg[:, 3:4], float(np.sqrt(S)), ALU.mult, ALU.mult)\
                .then_inc(gain_ready, 1)

            def norm(t, k):
                nc.vector.bn_stats(stats[:], env.x[:, t, :]).then_inc(ln_link, 1)
                dve.wait_ge(ln_link, 2 * t + 1)
                nc.vector.memset(pace[:], 0.0)
                nc.vector.bn_aggr(mv[:], stats[:]).then_inc(ln_link, 1)
                dve.wait_ge(ln_link, 2 * t + 2)
                nc.vector.tensor_scalar(var_eps[:], mv[:, 1:2], EPS, None, ALU.add).then_inc(var_ready, 1)
                if not (isinstance(t, int) and t < 2):
                    dve.wait_ge(x_ready, t - 1)
                dve.wait_ge(rstd_ready, t + 1)
                nc.vector.tensor_scalar(rows_f[:, k, XN, :], env.x[:, t, :], mv[:, 0:1], rstd[:, 0:1],
                                        ALU.subtract, ALU.mult).then_inc(xn_ready, 1)

            norm(0, 0)
            dve.wait_ge(u_full, 1)
            for hh in range(2):
                nc.vector.tensor_copy(u_t[:].rearrange("p (m two) o -> p m two o", two=2)[:, :, hh, :],
                                      turn[hh][:, 0:M3 * HD3].rearrange("p (m o) -> p m o", m=M3)).then_inc(u_ready, 1)

            def steps(at, main, prev, ss, rep, ahead):
                b, c = at.b, at.c
                t = at.tile()
                if main:
                    for m in range(M3):
                        dve.wait_ge(proj_full, 8 * b + m + 1)
                        nc.vector.tensor_reduce(nmax[:, c % 2, m:m + 1], proj[m][:], AX.X, ALU.max, negate=True)\
                            .then_inc(kmax_ready, 1)
                    for n in range(NC):
                        dve.wait_ge(proj_full, 8 * b + 4 + n + 1)
                        by_head = proj[n][:].rearrange("p (h d) -> p h d", h=H3)
                        nc.vector.tensor_reduce(qmax[:, n, :], by_head, AX.X, ALU.max).then_inc(q_link, 1)
                        dve.wait_ge(q_link, 4 * b + n + 1)
                        nc.vector.tensor_tensor(qe[:, c % 2, n, :].rearrange("p (h d) -> p h d", h=H3), by_head,
                                                qmax[:, n, :].unsqueeze(2).broadcast_to([P, H3, HD3]), ALU.subtract)\
                            .then_inc(q_free, 1)
                    if ahead:
                        norm(t + 1, (c // 2 + 1) % 2)
                if prev:
                    dve.wait_ge(k_free, 4 * b)
                    nc.vector.reciprocal(rksum[:], ksum[:, (c - 1) % 2, :]).then_inc(rk_done, 1)
                    dve.wait_ge(rk_done, b)
                    dve.wait_ge(m_full, b)
                    for hh in range(2):
                        rr = slice(hh * HD3, (hh + 1) * HD3)
                        nc.vector.scalar_tensor_tensor(
                            m_t[rr], small[rr, :].rearrange("p (m two o) -> p m two o", m=M3, two=2)[:, :, hh, :],
                            float(HD3) ** -0.5, rksum[rr].unsqueeze(2).broadcast_to([HD3, M3, HD3]),
                            ALU.mult, ALU.mult).then_inc(m_ready, 1)
                if main:
                    for n in range(NC):
                        dve.wait_ge(kt_high, 4 * b + n + 1)
                        nc.vector.tensor_tensor(kt[1][:, n, :], turn[n % 2][:], kt[0][:, n, :], ALU.subtract)\
                            .then_inc(kt_ready, 1)
                if ss:
                    dve.wait_ge(ss_full, at.tile(3) + 1)
                    nc.vector.tensor_scalar(ssm[:], small[:, 0:2 * NC], 1e-24, None, ALU.max).then_inc(ss_read, 1)
                if rep:
                    t4 = at.tile(4)
                    dve.wait_ge(rep_full, t4 + 1)
                    nc.vector.tensor_tensor(vec[:], small[:], u[:, ((c - 4) // 2) % 2, :], ALU.mult)\
                        .then_inc(rep_read, 1)
                    dve.wait_ge(rep_read, t4 + 1)
                    nc.vector.scalar_tensor_tensor(env.x[:, t4, :], vec[:], gain[:, 0:1], env.x[:, t4, :],
                                                   ALU.mult, ALU.add).then_inc(x_done, 1)
                if main:
                    dve.wait_ge(qe_done, 4 * b + 4)
                    nc.vector.tensor_reduce(qsum[:], qe[:, c % 2].rearrange("p n (h d) -> p (n h) d", h=H3), AX.X,
                                            ALU.add).then_inc(sum_link, 1)
                    dve.wait_ge(sum_link, b + 1)
                    if not at.first:
                        dve.wait_ge(qp_ready, b)
                    nc.vector.reciprocal(rqsum[:], qsum[:]).then_inc(qr_ready, 1)

            run(dve, steps)



I3 = 1792
C3 = I3 // P
UNITS = 3 * C3
CH3 = 3 * D
GATE_ROWS, SCALE_ROWS = 0, 64


def gated_phase(nc, env, d):
    with ExitStack() as ctx:
        sem = semaphores(nc, ctx, "f3_")
        sb = lambda n, shape, dt=F32: ctx.enter_context(nc.sbuf_tensor(f"f3_{n}", shape, dt))
        ps = lambda n, shape: ctx.enter_context(nc.psum_tensor(f"f3_{n}", shape, F32))
        norm = StepNorm(nc, env, ctx, "f3", "split")
        w = [sb(f"w{part}", [P, C3 * CH3], BF16) for part in range(2)]
        w_int = sb("w_int", [P, 2, 3, D], I32)
        zeros = sb("zeros", [UNITS, D], I32)
        rows_f = sb("rows_f", [P, D])
        parts = [sb(f"part{i}", [P, D], BF16) for i in range(3)]
        pick = sb("pick", [P, P], BF16)
        centred = sb("centred", [P, D])
        w_f = sb("w_f", [P, 3, D])
        sg = sb("sg", [P, 2, W])
        hf = sb("hf", [P, 2, W])
        h = [sb(f"h{part}", [P, 2, W], BF16) for part in range(2)]
        gate_ps, up_ps = ps("gate", [P, W]), ps("up", [P, W])
        out_ps = [ps(f"out{t}", [P, D]) for t in range(ST)]
        zero_ps, scale_ps = (b[:].rearrange("p k c -> p (k c)") for b in norm.turned)
        w_in = [sem(f"w_in{k}") for k in range(2)]
        (rows_in, blank, rows_ready, part_link, rep_full, sub_done, mul_done, w_high, w_ready) = map(sem, (
            "rows_in", "blank", "rows_ready", "part_link", "rep_full", "sub", "mul", "w_high", "w_ready"))
        (gate_full, up_full, sg_done, hf_done, h_high, h_ready, down_done, out_free) = map(sem, (
            "gate_full", "up_full", "sg", "hf", "h_high", "h_ready", "down_done", "out_free"))
        PARTS = 5
        block = ctx.enter_context(nc.Block())

        @block.sync
        def _(sp):
            sp.dma_start(zeros[:], d["f3_zeros"]).then_inc(rows_in, 16)
            sp.wait_ge(blank, 1)
            sp.dma_start(rows_f[SCALE_ROWS:SCALE_ROWS + UNITS, :], d["f3_scales"]).then_inc(rows_in, 16)
            for k in range(2):
                sp.dma_start(w_int[:, k].rearrange("p u c -> p (u c)"), d["f3_w"][:, k, :]).then_inc(w_in[k], 16)
            with sp.Fori(1, C3 // 2) as i:
                for k in range(2):
                    sp.wait_ge(sub_done, 3 * (2 * i + k) - 3)
                    sp.dma_start(w_int[:, k].rearrange("p u c -> p (u c)"),
                                 d["f3_w"][:, bass.ds(2 * i + k, 1), :].rearrange("p c n -> p (c n)"))\
                        .then_inc(w_in[k], 16)
            for k in range(2):
                sp.wait_ge(w_in[k], 16 * C3 // 2)

        @block.gpsimd
        def _(pool):
            nc.gpsimd.memset(rows_f[:], 0.0).then_inc(blank, 1)
            norm.pool_start(pool)
            norm.pool(pool, 0)
            pool.wait_ge(blank, 1)
            pool.wait_ge(rows_in, 32)
            nc.gpsimd.tensor_copy(rows_f[0:UNITS, :], zeros[:]).then_inc(rows_ready, 1)
            norm.pool(pool, 1)

            def low(c, i):
                u = 3 * c + i
                pool.wait_ge(w_high, u + 1)
                cols = bass.ds(u * D, D)
                nc.gpsimd.tensor_tensor(w[1][:, cols], w_f[:, i, :], w[0][:, cols], ALU.subtract)\
                    .then_inc(w_ready, 1)

            with pool.Fori(0, C3) as c:
                for i in range(3):
                    low(c, i)
            for n in range(1, NS - 1):
                norm.pool(pool, n + 1)

        @block.tensor
        def _(pe):
            def repeat(c, i):
                u = 3 * c + i
                if not (isinstance(u, int) and u == 0):
                    pe.wait_ge(mul_done, u)
                for row, bank in ((0, zero_ps), (SCALE_ROWS, scale_ps)):
                    for p in range(3):
                        mm = nc.tensor.matmul(bank, pick[:, bass.ds(u + row, 1)].broadcast_to([P, P]), parts[p][:],
                                              start=(p == 0), stop=(p == 2))
                mm.then_inc(rep_full, 1)

            def product(bank, c, i, par, full):
                for k in range(KC):
                    for p, (a, b) in enumerate(PASSES):
                        mm = nc.tensor.matmul(bank[:], w[a][:, bass.ds(c * CH3 + i * D + k * P, P)],
                                              norm.xt[b][:, par, k, :], start=(k == 0 and p == 0),
                                              stop=(k == KC - 1 and p == 2))
                mm.then_inc(full, 1)

            def down(n, c, k, start, stop):
                pe.wait_ge(h_ready, C3 * n + c + 1)
                for t in range(ST):
                    for p, (a, b) in enumerate(PASSES):
                        mm = nc.tensor.matmul(out_ps[t][:], h[a][:, k, t * P:(t + 1) * P],
                                              w[b][:, bass.ds(c * CH3 + 2 * D, D)], start=(start and p == 0),
                                              stop=(stop and p == 2))
                mm.then_inc(down_done, 1)

            norm.pe(pe, 0)
            pe.wait_ge(part_link, PARTS)
            pe.wait_ge(norm.low_done, ST)
            for i in range(3):
                repeat(0, i)
            for n in range(NS):
                def chunk(c, k, last=False):
                    static = isinstance(c, int)
                    N = C3 * n + c
                    ahead = n == 0 and not last
                    if ahead:
                        repeat(c + 1, 0)
                    if n == 0:
                        pe.wait_ge(w_ready, 3 * c + 3)
                    if not (static and N == 0):
                        pe.wait_ge(sg_done, N)
                    product(gate_ps, c, 0, n % 2, gate_full)
                    if ahead:
                        repeat(c + 1, 1)
                    if not (static and N == 0):
                        pe.wait_ge(hf_done, N)
                    product(up_ps, c, 1, n % 2, up_full)
                    if ahead:
                        repeat(c + 1, 2)
                    if static and c == 1 and n:
                        pe.wait_ge(out_free, ST * n)
                    if not (static and c == 0):
                        down(n, c - 1, 1 - k, static and c == 1, False)

                chunk(0, 0)
                chunk(1, 1)
                with pe.Fori(1, C3 // 2 - 1) as i:
                    for k in range(2):
                        chunk(2 * i + k, k)
                chunk(C3 - 2, 0)
                chunk(C3 - 1, 1, last=True)
                if n < NS - 1:
                    if n == 0:
                        pe.wait_ge(mul_done, UNITS)
                    norm.pe(pe, n + 1)
                down(n, C3 - 1, 1, False, True)
                if n < NS - 1:
                    pe.wait_ge(norm.low_done, ST * (n + 2))

        @block.scalar
        def _(act):
            def w_part(c, i):
                u = 3 * c + i
                act.wait_ge(mul_done, u + 1)
                nc.scalar.activation(w[0][:, bass.ds(u * D, D)], w_f[:, i, :], ACT.Copy).then_inc(w_high, 1)

            norm.act(act, 0, 0)
            for i in range(3):
                w_part(0, i)
            for n in range(NS):
                def chunk(c, k, last=False):
                    static = isinstance(c, int)
                    N = C3 * n + c
                    ahead = n == 0 and not last
                    if ahead:
                        w_part(c + 1, 0)
                    act.wait_ge(gate_full, N + 1)
                    if not (static and N < 2):
                        act.wait_ge(hf_done, N - 1)
                    nc.scalar.activation(sg[:, k, :], gate_ps[:], ACT.Silu).then_inc(sg_done, 1)
                    if ahead:
                        w_part(c + 1, 1)
                    act.wait_ge(hf_done, N + 1)
                    if not (static and N < 2):
                        act.wait_ge(down_done, N - 1)
                    nc.scalar.activation(h[0][:, k, :], hf[:, k, :], ACT.Copy).then_inc(h_high, 1)
                    if ahead:
                        w_part(c + 1, 2)

                chunk(0, 0)
                chunk(1, 1)
                with act.Fori(1, C3 // 2 - 1) as i:
                    for k in range(2):
                        chunk(2 * i + k, k)
                chunk(C3 - 2, 0)
                chunk(C3 - 1, 1, last=True)
                if n < NS - 1:
                    norm.act(act, n + 1, (n + 1) % 2)

        @block.vector
        def _(dve):
            def weights(c, i, k):
                u = 3 * c + i
                if i == 0:
                    dve.wait_ge(w_in[k], 16 if isinstance(c, int) and c < 2 else (c - k) * 8 + 16)
                dve.wait_ge(rep_full, u + 1)
                nc.vector.tensor_tensor(centred[:], w_int[:, k, i, :], zero_ps, ALU.subtract).then_inc(sub_done, 1)
                if not (isinstance(u, int) and u < 3):
                    dve.wait_ge(w_ready, u - 2)
                dve.wait_ge(sub_done, u + 1)
                nc.vector.tensor_tensor(w_f[:, i, :], centred[:], scale_ps, ALU.mult).then_inc(mul_done, 1)

            norm.dve(dve, 0, 0, 0)
            dve.wait_ge(rows_ready, 1)
            nc.vector.tensor_copy(pick[:], env.ident[:]).then_inc(part_link, 1)
            nc.vector.tensor_copy(parts[0][:], rows_f[:]).then_inc(part_link, 1)
            dve.wait_ge(part_link, 2)
            nc.vector.tensor_tensor(rows_f[:], rows_f[:], parts[0][:], ALU.subtract).then_inc(part_link, 1)
            dve.wait_ge(part_link, 3)
            nc.vector.tensor_copy(parts[1][:], rows_f[:]).then_inc(part_link, 1)
            dve.wait_ge(part_link, 4)
            nc.vector.tensor_tensor(parts[2][:], rows_f[:], parts[1][:], ALU.subtract).then_inc(part_link, 1)
            norm.dve_low(dve, 0, 0)
            for i in range(3):
                weights(0, i, 0)
            for n in range(NS):
                def chunk(c, k, last=False):
                    static = isinstance(c, int)
                    N = C3 * n + c
                    ahead = n == 0 and not last
                    if ahead:
                        weights(c + 1, 0, 1 - k)
                        weights(c + 1, 1, 1 - k)
                    dve.wait_ge(up_full, N + 1)
                    dve.wait_ge(sg_done, N + 1)
                    if not (static and N < 2):
                        dve.wait_ge(h_ready, N - 1)
                    nc.vector.tensor_tensor(hf[:, k, :], sg[:, k, :], up_ps[:], ALU.mult).then_inc(hf_done, 1)
                    if ahead:
                        weights(c + 1, 2, 1 - k)
                    dve.wait_ge(h_high, N + 1)
                    nc.vector.tensor_tensor(h[1][:, k, :], hf[:, k, :], h[0][:, k, :], ALU.subtract)\
                        .then_inc(h_ready, 1)

                if n < NS - 1:
                    norm.dve(dve, n + 1, (n + 1) % 2, (n + 1) * ST)
                chunk(0, 0)
                chunk(1, 1)
                with dve.Fori(1, C3 // 2 - 1) as i:
                    for k in range(2):
                        chunk(2 * i + k, k)
                chunk(C3 - 2, 0)
                chunk(C3 - 1, 1, last=True)
                if n < NS - 1:
                    norm.dve_low(dve, n + 1, (n + 1) % 2)
                dve.wait_ge(down_done, C3 * (n + 1))
                for t in range(ST):
                    tile = env.x[:, n * ST + t, :]
                    nc.vector.scalar_tensor_tensor(tile, out_ps[t][:], env.tg[:, 7:8], tile,
                                                   ALU.mult, ALU.add).then_inc(out_free, 1)



PHASES = ("a0", "f0", "a1", "f1", "a2", "f2", "a3", "f3")


def build(nc, d, out, phases=PHASES):
    with ExitStack() as ctx:
        sb = lambda n, shape, dt: ctx.enter_context(nc.sbuf_tensor(n, shape, dt))
        env = Env()
        env.x = sb("x_res", [P, NT, D], F32)
        env.ident = sb("ident", [P, P], F32)
        env.ones = sb("ones", [P, P], F32)
        env.tg = sb("tanh_gates", [P, 8], F32)
        with nc.sbuf_tensor("ctx_high", [P, KC, T], BF16) as high, nc.sbuf_tensor("ctx_low", [P, KC, T], BF16) as low:
            env.ct = env.cth, env.ctl = high, low
            load_phase(nc, env, d)
            if "a0" in phases:
                with nc.sbuf_tensor("x_high", [P, KC, T], BF16) as high, \
                        nc.sbuf_tensor("x_low", [P, KC, T], BF16) as low:
                    env.xt = env.xth, env.xtl = high, low
                    layer_norm_phase(nc, env, "ln0", "split")
                    attention0_phase(nc, env, d)
            if "f0" in phases:
                experts_phase(nc, env, d, "f0", 16, True, 4.0, 4)
            if "a1" in phases:
                attention1_phase(nc, env, d)
            if "f1" in phases:
                experts_phase(nc, env, d, "f1", 8, False, 2.0, 5)
            if "a2" in phases:
                attention2_phase(nc, env, d)
            if "f2" in phases:
                quantized_phase(nc, env, d)
            if "a3" in phases:
                attention3_phase(nc, env, d)
        if "f3" in phases:
            gated_phase(nc, env, d)
        store_phase(nc, env, out)


def store_phase(nc, env, out):
    with ExitStack() as ctx:
        stored = ctx.enter_context(nc.semaphore("stored"))
        block = ctx.enter_context(nc.Block())

        @block.sync
        def _(sp):
            sp.dma_start(out.rearrange("(t p) d -> p t d", p=P), env.x[:]).then_inc(stored, 16)
            sp.wait_ge(stored, 16)


def layouts(inputs, np):
    i = {k: np.asarray(v) for k, v in inputs.items()}
    out = {}
    out["x"] = i["x"].reshape(T, D)
    out["ctxT"] = i["ctx_4096"].reshape(T, D).T
    gates = np.concatenate([i["g_xattn"], i["g_ffn"]])
    out["gates"] = np.broadcast_to(gates, (P, 8))
    out["mask"] = i["mask_1x1xSxS2_ff0"].reshape(S, S)
    out["qk_norm_w"] = np.stack([i["L0_xattn_q_norm_w"], i["L0_xattn_k_norm_w"]], 1)
    wq = i["L0_xattn_Wq"].reshape(G0, QCOLS, KC, P).transpose(0, 3, 2, 1)
    wk = i["L0_xattn_Wk"].reshape(G0, HD0, KC, P).transpose(0, 3, 2, 1)
    wv = i["L0_xattn_Wv"].reshape(G0, HD0, KC, P).transpose(0, 3, 2, 1)
    wo = i["L0_xattn_Wo"].reshape(D, G0, H0, P).transpose(1, 3, 2, 0)
    w0 = np.concatenate([wq.reshape(G0, P, -1), np.concatenate([wk, wv], 3).reshape(G0, P, -1),
                         wo.reshape(G0, P, -1)], 2)
    out["w0"] = w0
    out["ctx"] = i["ctx_4096"].reshape(T, D)
    chunks = lambda w: w.reshape(KC, P, -1).transpose(1, 0, 2)
    out["f0_down"] = chunks(np.concatenate([i["L0_ffn_A"].reshape(-1, D), i["L0_ffn_router_w"]]).T)
    out["f0_up"] = i["L0_ffn_B"].transpose(0, 2, 1).reshape(-1, D)
    out["a1_wq"] = chunks(i["L1_xattn_Wq"].T)
    out["a1_wk"] = chunks(i["L1_xattn_Wk"].T)
    out["a1_bias"] = np.stack([i["L1_xattn_bq"].reshape(KC, P).T, i["L1_xattn_bk"].reshape(KC, P).T], 1)
    out["f1_down"] = chunks(np.concatenate([i["L1_ffn_A"].reshape(-1, D), i["L1_ffn_Wr"]]).T)
    out["f1_up"] = np.concatenate([i["L1_ffn_Bm"].transpose(0, 2, 1).reshape(-1, D), i["L1_ffn_b"][None]])
    out["f1_dense"] = chunks(i["L1_ffn_W"].T)
    by_j = lambda w: w.reshape(-1, G2, J2, HD2).transpose(0, 2, 1, 3).reshape(-1, D)
    out["a2_w"] = chunks(np.concatenate([by_j(i["L2_xattn_Wq"]), i["L2_xattn_Wk"], i["L2_xattn_Wv"]], 1))
    out["a2_wo"] = i["L2_xattn_Wo"].reshape(G2, J2, HD2, D).transpose(0, 2, 1, 3).reshape(KV2, J2, D)
    out["a2_bo"] = i["L2_xattn_bo"][None]
    out["a2_qk_bias"] = np.concatenate([by_j(i["L2_xattn_bq"]).reshape(J2, KV2).T, i["L2_xattn_bk"][:, None]], 1)
    out["a2_v_bias"] = np.broadcast_to(i["L2_xattn_bv"], (P, KV2))
    row = np.arange(P)
    out["g_mask"] = (row[:, None] // HD2 == np.arange(G2)).astype(np.float32)
    out["v_mask"] = (row[:, None] // S == (row // HD2) % 2).astype(np.float32)
    out["f2_w"] = np.stack([i[f"L2_ffn_{n}"].reshape(KC, P, D).transpose(1, 0, 2) for n in ("w1", "w3")], 1)
    out["f2_reps"] = np.stack([np.broadcast_to(i[f"L2_ffn_{n}"], (P, D)) for n in ("gamma", "beta", "b1", "b3")], 1)
    twice = lambda w: np.concatenate([w, w])
    out["a3_w"] = np.stack([twice(i["L3_xattn_Wk"].T), twice(i["L3_xattn_Wq"].T)], 1)
    wv3 = i["L3_xattn_Wv"].reshape(M3, P, S).transpose(1, 0, 2)
    out["a3_wv"] = np.concatenate([wv3, wv3], 2)
    out["a3_wo"] = i["L3_xattn_Wo"].reshape(S, M3, P).transpose(2, 1, 0)
    out["a3_cols"] = np.stack([twice(i["L3_xattn_bo"]), twice(i["L3_xattn_g"].reshape(S))], 1)
    out["half_ones"] = (row[:, None] // S == np.arange(2)).astype(np.float32)
    by_column = lambda w: w.reshape(KC, -1, C3, P).transpose(1, 2, 0, 3).reshape(-1, C3, D)
    units = lambda gate, up, down: np.stack([by_column(i[f"L3_ffn_{gate}"]), by_column(i[f"L3_ffn_{up}"]),
                                             i[f"L3_ffn_{down}"].reshape(C3, -1, D).transpose(1, 0, 2)], 2)
    out["f3_w"] = units("gate_w", "up_w", "down_w").reshape(P, C3, CH3)
    out["f3_zeros"] = units("gate_z", "up_z", "down_z").reshape(UNITS, D)
    out["f3_scales"] = units("gate_s", "up_s", "down_s").reshape(UNITS, D)
    return {k: np.ascontiguousarray(v) for k, v in out.items()}


def kernel(**inputs):
    import numpy as _np
    import concourse.bacc as _bacc
    from concourse import mybir as _mybir
    from concourse.bass_utils import run_bass_kernel_spmd as _run

    nc = _bacc.Bacc("TRN2", target_bir_lowering=False, num_devices=1)
    arrays = layouts(inputs, _np)
    d = {k: nc.dram_tensor(f"in_{k}", a.shape, _mybir.dt.from_np(a.dtype), kind="ExternalInput").ap()
         for k, a in arrays.items()}
    out = nc.dram_tensor("out_x", (T, D), _mybir.dt.float32, kind="ExternalOutput").ap()
    build(nc, d, out)
    r = _run(nc, [{f"in_{k}": a for k, a in arrays.items()}], core_ids=[0])
    return r.results[0]["out_x"].reshape(B, S, D)
```

```python
import numpy as np

import concourse.bass as bass
from concourse import mybir
from contextlib import ExitStack

F32 = mybir.dt.float32
BF16 = mybir.dt.bfloat16
I32 = mybir.dt.int32
ALU = mybir.AluOpType
ACT = mybir.ActivationFunctionType
AX = mybir.AxisListType

P = 128
B, S, D = 32, 64, 512
T = B * S
NT = T // P
KC = D // P
ST = 4
NS = NT // ST
W = ST * P
EPS = 1e-5
PASSES = ((0, 0), (0, 1), (1, 0))


class Env:
    pass


def semaphores(nc, ctx, prefix):
    taken = []

    def sem(name):
        taken.append(nc.alloc_semaphore(name=f"{prefix}{name}"))
        return taken[-1]

    def give_back():
        nc.clear_and_free_semaphores(taken)
        nc.all_engine_barrier()

    ctx.callback(give_back)
    return sem



class StepNorm:

    def __init__(self, nc, env, ctx, name, mode):
        sem = semaphores(nc, ctx, f"{name}_norm_")
        sb = lambda n, shape, dt: ctx.enter_context(nc.sbuf_tensor(f"{name}_norm_{n}", shape, dt))
        self.nc, self.env, self.mode = nc, env, mode
        self.stats = sb("stats", [P, ST, 6], F32)
        self.mv = sb("mv", [P, ST, 2], F32)
        self.var_eps = sb("var_eps", [P, ST], F32)
        self.rstd = sb("rstd", [P, ST], F32)
        self.pace = sb("pace", [P, 1], F32)
        self.minus_half = sb("minus_half", [P, ST], F32)
        copies = 2 if mode == "plain" else 1
        self.tiles = sb("tiles", [P, copies, ST, D], F32)
        if mode == "f32":
            self.xt32 = sb("xt", [P, 2, KC, W], F32)
        if mode == "split":
            self.xt = [sb(f"xt{part}", [P, 2, KC, W], BF16) for part in range(2)]
        if mode != "plain":
            self.turned = [ctx.enter_context(nc.psum_tensor(f"{name}_norm_turned{b}", [P, KC, P], F32))
                           for b in range(2)]
        self.const_set, self.stats_done, self.mv_done, self.var_ready, self.rstd_ready = map(
            sem, ("const", "stats", "mv", "var", "rstd"))
        self.tile_ready, self.turned_ready, self.high_done, self.low_done = map(
            sem, ("tile", "turned", "high", "low"))
        self.evacuated = self.high_done if mode == "f32" else self.low_done

    def turned_out(self, part, n, par, t):
        if self.mode == "whole":
            return self.env.xt[part][:, :, (n * ST + t) * P:(n * ST + t + 1) * P]
        out = self.xt32 if self.mode == "f32" else self.xt[part]
        return out[:, par, :, t * P:(t + 1) * P]

    def pool_start(self, pool):
        self.nc.gpsimd.memset(self.minus_half[:], -0.5).then_inc(self.const_set, 1)
        pool.wait_ge(self.const_set, 1)

    def pool(self, pool, n):
        pool.wait_ge(self.var_ready, n + 1)
        self.nc.gpsimd.tensor_tensor(self.rstd[:], self.var_eps[:], self.minus_half[:], ALU.pow)\
            .then_inc(self.rstd_ready, 1)

    def dve(self, dve, n, par, tile):
        self.dve_moments(dve, n, tile)
        self.dve_tiles(dve, n, par, tile)

    def dve_moments(self, dve, n, tile):
        nc = self.nc
        for t in range(ST):
            last = nc.vector.bn_stats(self.stats[:, t, :], self.env.x[:, tile + t, :])
        last.then_inc(self.stats_done, 1)
        dve.wait_ge(self.stats_done, n + 1)
        nc.vector.memset(self.pace[:], 0.0)
        for t in range(ST):
            last = nc.vector.bn_aggr(self.mv[:, t, :], self.stats[:, t, :])
        last.then_inc(self.mv_done, 1)
        dve.wait_ge(self.mv_done, n + 1)
        nc.vector.tensor_scalar(self.var_eps[:], self.mv[:, :, 1], EPS, None, ALU.add).then_inc(self.var_ready, 1)

    def dve_tiles(self, dve, n, par, tile):
        nc = self.nc
        if self.mode != "plain" and not (isinstance(n, int) and n == 0):
            dve.wait_ge(self.turned_ready, ST * n)
        dve.wait_ge(self.rstd_ready, n + 1)
        for t in range(ST):
            nc.vector.tensor_scalar(self.tiles[:, par if self.mode == "plain" else 0, t, :],
                                    self.env.x[:, tile + t, :], self.mv[:, t, 0:1], self.rstd[:, t:t + 1],
                                    ALU.subtract, ALU.mult).then_inc(self.tile_ready, 1)

    def dve_low(self, dve, n, par):
        for t in range(ST):
            dve.wait_ge(self.high_done, ST * n + t + 1)
            self.nc.vector.tensor_tensor(self.turned_out(1, n, par, t), self.turned[t % 2][:],
                                         self.turned_out(0, n, par, t), ALU.subtract).then_inc(self.low_done, 1)

    def pe(self, pe, n, t0=0, t1=ST):
        for t in range(t0, t1):
            pe.wait_ge(self.tile_ready, ST * n + t + 1)
            if t >= 2 or not (isinstance(n, int) and n == 0):
                pe.wait_ge(self.evacuated, ST * n + t - 1 if t >= 1 else ST * n)
            for c in range(KC):
                last = self.nc.tensor.transpose(self.turned[t % 2][:, c, :], self.tiles[:, 0, t, c * P:(c + 1) * P],
                                                self.env.ident[:])
            last.then_inc(self.turned_ready, 1)

    def act(self, act, n, par):
        for t in range(ST):
            act.wait_ge(self.turned_ready, ST * n + t + 1)
            self.nc.scalar.activation(self.turned_out(0, n, par, t), self.turned[t % 2][:], ACT.Copy)\
                .then_inc(self.high_done, 1)


class Staged:

    def __init__(self, nc, ctx, d, names):
        self.tile = ctx.enter_context(nc.sbuf_tensor("staged", [P, WALL0], F32))
        self.loaded = {n: ctx.enter_context(nc.semaphore(f"{n}_loaded")) for n in names}
        self.d, self.waiting = d, list(names)

    def load_next(self, sp):
        if self.waiting:
            name = self.waiting.pop(0)
            source = self.d["w0"][0] if name == "a0" else self.d[f"{name}_w"]
            sp.dma_start(self.tile[:, 0:source.shape[1]], source).then_inc(self.loaded[name], 16)



def load_phase(nc, env, d, normalize):
    with ExitStack() as ctx:
        sem = semaphores(nc, ctx, "load_")
        norm = StepNorm(nc, env, ctx, "a0", "whole") if normalize else None
        ctx_f = ctx.enter_context(nc.sbuf_tensor("ctx_f", [P, KC, T], F32))
        gates = ctx.enter_context(nc.sbuf_tensor("gates", [P, 8], F32))
        x_in = [sem(f"x_in{n}") for n in range(NS)]
        ctx_in = [sem(f"ctx_in{c}") for c in range(KC)]
        gates_in, zeroed, made, high_done, pool_low, dve_low, tanh_done = map(
            sem, ("gates_in", "zeroed", "made", "high", "pool_low", "dve_low", "tanh"))
        block = ctx.enter_context(nc.Block())

        @block.sync
        def _(sp):
            sp.dma_start(gates[:], d["gates"]).then_inc(gates_in, 16)
            rows = d["x"].rearrange("(t p) d -> p t d", p=P)
            for n in range(NS):
                tiles = slice(n * ST, (n + 1) * ST)
                sp.dma_start(env.x[:, tiles, :], rows[:, tiles, :]).then_inc(x_in[n], 16)
            for c in range(KC):
                sp.dma_start(ctx_f[:, c, :], d["ctxT"][c * P:(c + 1) * P, :]).then_inc(ctx_in[c], 16)
            env.staged.load_next(sp)
            for n in range(NS):
                sp.wait_ge(x_in[n], 16)

        @block.gpsimd
        def _(pool):
            nc.gpsimd.memset(env.ident[:], 0.0).then_inc(zeroed, 1)
            nc.gpsimd.memset(env.ones[:], 1.0).then_inc(made, 1)
            pool.wait_ge(zeroed, 1)
            nc.gpsimd.affine_select(out=env.ident[:], in_=env.ident[:], compare_op=ALU.not_equal, fill=1.0, base=0,
                                    pattern=[[-1, P]], channel_multiplier=1).then_inc(made, 1)
            if normalize:
                norm.pool_start(pool)
                for n in range(NS):
                    norm.pool(pool, n)
            for c in range(0, KC // 2):
                pool.wait_ge(high_done, c + 1)
                nc.gpsimd.tensor_tensor(env.ctl[:, c, :], ctx_f[:, c, :], env.cth[:, c, :], ALU.subtract)\
                    .then_inc(pool_low, 1)

        if normalize:
            @block.tensor
            def _(pe):
                pe.wait_ge(made, 2)
                for n in range(NS):
                    norm.pe(pe, n)

        @block.scalar
        def _(act):
            act.wait_ge(gates_in, 16)
            nc.scalar.activation(env.tg[:], gates[:], ACT.Tanh).then_inc(tanh_done, 1)
            order = [("x", 0), ("x", 1), ("x", 2), ("c", 0), ("x", 3), ("c", 1), ("c", 2), ("c", 3)]
            for what, i in order:
                if what == "c":
                    act.wait_ge(ctx_in[i], 16)
                    nc.scalar.activation(env.cth[:, i, :], ctx_f[:, i, :], ACT.Copy).then_inc(high_done, 1)
                elif normalize:
                    norm.act(act, i, 0)

        @block.vector
        def _(dve):
            if normalize:
                for n in range(NS + 1):
                    if n < NS:
                        dve.wait_ge(x_in[n], 16)
                        if n:
                            dve.wait_ge(norm.tile_ready, ST * n)
                        norm.dve_moments(dve, n, n * ST)
                    if n:
                        norm.dve_low(dve, n - 1, 0)
                    if n < NS:
                        norm.dve_tiles(dve, n, 0, n * ST)
            for c in range(KC // 2, KC):
                dve.wait_ge(high_done, c + 1)
                nc.vector.tensor_tensor(env.ctl[:, c, :], ctx_f[:, c, :], env.cth[:, c, :],
                                        ALU.subtract).then_inc(dve_low, 1)



G0, H0, HD0 = 8, 4, 128
QCOLS, KVCOLS = H0 * HD0, 2 * HD0
WQ0, WKV0, WO0 = 0, KC * QCOLS, KC * (QCOLS + KVCOLS)
WALL0 = WO0 + H0 * D
CHUNK0 = 512


def attention0_phase(nc, env, d):
    per = 2 * NS
    with ExitStack() as ctx:
        sem = semaphores(nc, ctx, "a0_")
        sb = lambda n, shape, dt: ctx.enter_context(nc.sbuf_tensor(f"a0_{n}", shape, dt))
        ps = lambda n, shape: ctx.enter_context(nc.psum_tensor(f"a0_{n}", shape, F32))
        w_f = env.staged.tile
        w_split = [[sb(f"w{g}{part}", [P, WALL0], BF16) for part in range(2)] for g in range(2)]
        mask = sb("mask", [P, S], F32)
        qkw_in = sb("qkw_in", [P, 2], F32)
        qkw = sb("qkw", [P, 1], F32)
        minus_half = sb("minus_half", [P, 16], F32)
        k_f = sb("k_f", [P, ST, HD0], F32)
        k_sq = sb("k_sq", [P, ST, HD0], F32)
        k_ss = sb("k_ss", [P, ST], F32)
        k_se = sb("k_se", [P, ST], F32)
        k_r = sb("k_r", [P, ST], F32)
        k_n = sb("k_n", [P, ST, HD0], F32)
        v = [sb(f"v{part}", [P, 2, ST, HD0], BF16) for part in range(2)]
        kt = [sb(f"kt{part}", [P, W], BF16) for part in range(2)]
        q = [sb(f"q{part}", [P, 2 * ST, H0, S], BF16) for part in range(2)]
        q_sq = sb("q_sq", [P, 2, 2 * ST, S], F32)
        q_sq16 = [sb(f"q_sq{part}", [P, 2 * ST, H0, S], BF16) for part in range(2)]
        ones16 = sb("ones16", [P, 1], BF16)
        q_se = sb("q_se", [P, 16], F32)
        q_r = sb("q_r", [P, 16], F32)
        sc = sb("sc", [P, 16, S], F32)
        mx = sb("mx", [P, 16], F32)
        den = sb("den", [P, 16], F32)
        rden = sb("rden", [P, 16], F32)
        pt = [sb(f"pt{part}", [P, ST, 2, P], BF16) for part in range(2)]
        ot = [sb(f"ot{part}", [P, H0, W], BF16) for part in range(2)]
        ring = [ps(f"ring{b}", [P, 512]) for b in range(2)]
        scores = ps("scores", [P, 16, S])
        heads = [ps(f"heads{b}", [P, 2, H0, S]) for b in range(2)]
        q_ss = ps("q_ss", [P, 512])
        k_turned = ps("k_turned", [P, 512])

        const_in, const_set, w_in, w_high, w_ready = map(sem, ("const_in", "const_set", "w_in", "w_high", "w_ready"))
        qkw_ready = sem("qkw_ready")
        full, free, act_out = map(sem, ("ring_full", "ring_free", "act_out"))
        ssk_ready, sek_ready, rk_ready, kn_ready = map(sem, ("ssk", "sek", "rk", "kn"))
        kt_full, kt_high, kt_ready = map(sem, ("kt_full", "kt_high", "kt_ready"))
        sq_high, sq_ready, ssq_ready, seq_ready, rq_ready = map(sem, ("sq_high", "sq", "ssq", "seq", "rq"))
        scores_ready, chain, shifted, exp_done, rden_ready, probs_ready = map(
            sem, ("scores", "chain", "shifted", "exp", "rden", "probs"))
        pt_full, pt_high, pt_ready = map(sem, ("pt_full", "pt_high", "pt_ready"))
        heads_full, ot_high, ot_ready = map(sem, ("heads_full", "ot_high", "ot_ready"))
        RING = 10
        KV, QI, OI = 0, 2, 6
        PASSES0 = G0 // 2
        first_high, first_ready = map(sem, ("first_high", "first_ready"))

        block = ctx.enter_context(nc.Block())

        def item(n, k, which):
            m = n * per + k
            if which < OI:
                return which if isinstance(m, int) and m == 0 else m * RING - 4 + which
            last = isinstance(m, int) and m == PASSES0 * per - 1
            return m * RING + (0 if last else 6) + which

        def run(eng, body):
            with eng.Fori(0, PASSES0 - 1) as n:
                for k in range(per):
                    body(n, k, True)
            for k in range(per):
                body(PASSES0 - 1, k, k < per - 1)

        def head_out(part, tp, par):
            return ot[part][:].rearrange("p h (t r q) -> p t r h q", t=ST, r=2)[:, 2 * tp:2 * tp + 2, par, :, :]

        def bank(k, which):
            return ring[which % 2]

        @block.sync
        def _(sp):
            sp.dma_start(mask[0:S, :], d["mask"]).then_inc(const_in, 16)
            sp.dma_start(mask[S:P, :], d["mask"]).then_inc(const_in, 16)
            sp.dma_start(qkw_in[:], d["qk_norm_w"]).then_inc(const_in, 16)
            sp.wait_ge(first_ready, 10)
            sp.dma_start(w_f[:], d["w0"][1]).then_inc(w_in, 16)
            with sp.Fori(2, G0) as g:
                sp.wait_ge(w_ready, g - 1)
                sp.dma_start(w_f[:], d["w0"][bass.ds(g, 1)].rearrange("a p n -> (a p) n")).then_inc(w_in, 16)
            sp.wait_ge(w_in, 16 * (G0 - 1))
            sp.wait_ge(w_ready, G0 - 1)
            env.staged.load_next(sp)

        @block.gpsimd
        def _(pool):
            nc.gpsimd.memset(minus_half[:], -0.5).then_inc(const_set, 1)
            nc.gpsimd.memset(ones16[:], 1.0).then_inc(const_set, 1)
            pool.wait_ge(const_set, 1)

            def split_weights(g, par, chunks):
                for c in chunks:
                    cols = slice(c * CHUNK0, (c + 1) * CHUNK0)
                    nc.gpsimd.tensor_copy(w_split[par][0][:, cols], w_f[:, cols]).then_inc(w_high, 1)
                    pool.wait_ge(w_high, (g - 1) * 10 + c + 1)
                    last = nc.gpsimd.tensor_tensor(w_split[par][1][:, cols], w_f[:, cols],
                                                   w_split[par][0][:, cols], ALU.subtract)
                    if c == 9:
                        last.then_inc(w_ready, 1)

            def normalize(n):
                pool.wait_ge(rden_ready, n + 1)
                nc.gpsimd.tensor_tensor(sc[:], sc[:], rden[:].unsqueeze(2).broadcast_to([P, 16, S]), ALU.mult)\
                    .then_inc(probs_ready, 1)

            def key_factor(m):
                pool.wait_ge(sek_ready, m + 1)
                nc.gpsimd.tensor_tensor(k_r[:], k_se[:], minus_half[:, 0:ST], ALU.pow).then_inc(rk_ready, 1)

            def query_factor(m):
                pool.wait_ge(seq_ready, m + 1)
                nc.gpsimd.tensor_tensor(q_r[:], q_se[:], minus_half[:], ALU.pow).then_inc(rq_ready, 1)

            def body(n, k, front):
                m = n * per + k
                if front:
                    key_factor(m + 1)
                g = 2 * n + k // NS + 1
                more = not (isinstance(g, int) and g == G0)
                if k % NS == 0 and more:
                    pool.wait_ge(w_in, 16 * g)
                    pool.wait_ge(full, (m - 1) * RING + 6 + OI + 4)
                normalize(m)
                if k % NS < NS - 1 and more:
                    split_weights(g, (k // NS + 1) % 2, (range(0, 4), range(4, 7), range(7, 10))[k % NS])
                if front:
                    query_factor(m + 1)

            key_factor(0)
            query_factor(0)
            run(pool, body)

        @block.tensor
        def _(pe):
            def parts(g, k):
                return w_split[(k // NS) % 2]

            def project_kv(n, k):
                wg = parts(n, k)
                first = isinstance(n, int) and n == k == 0
                if first:
                    pe.wait_ge(first_ready, 10)
                elif k % NS == 0:
                    pe.wait_ge(w_ready, 2 * n + k // NS)
                for h in range(2):
                    out = bank(k, KV + h)
                    it = item(n, k, KV + h)
                    if not first:
                        pe.wait_ge(free, it - 1)
                    for j in range(2):
                        t = (k % NS) * ST + 2 * h + j
                        for c in range(KC):
                            for i, (a, b) in enumerate(PASSES):
                                last = nc.tensor.matmul(
                                    out[:, j * KVCOLS:(j + 1) * KVCOLS], env.ct[a][:, c, t * P:(t + 1) * P],
                                    wg[b][:, WKV0 + c * KVCOLS:WKV0 + (c + 1) * KVCOLS],
                                    start=(c == 0 and i == 0), stop=(c == KC - 1 and i == 2))
                    last.then_inc(full, 1)

            def project_q(n, k, which):
                wg = parts(n, k)
                for h in which:
                    out = bank(k, QI + h)
                    pe.wait_ge(free, item(n, k, QI + h) - 1)
                    for c in range(KC):
                        cols = WQ0 + c * QCOLS + h * HD0
                        for i, (a, b) in enumerate(PASSES):
                            last = nc.tensor.matmul(
                                out[:], wg[a][:, cols:cols + HD0], env.xt[b][:, c, (k % NS) * W:(k % NS + 1) * W],
                                start=(c == 0 and i == 0), stop=(c == KC - 1 and i == 2))
                    last.then_inc(full, 1)

            def turn_k(n, k):
                pe.wait_ge(kn_ready, n * per + k + 1)
                for t in range(ST):
                    last = nc.tensor.transpose(k_turned[:, t * P:(t + 1) * P], k_n[:, t, :], env.ident[:])
                last.then_inc(kt_full, 1)

            def q_squares(n, k):
                pe.wait_ge(sq_ready, (n * per + k + 1) * H0)
                for t in range(ST):
                    for pair in range(2):
                        for par in range(2):
                            at = 4 * t + 2 * pair + par
                            for p in range(2):
                                rows = q_sq16[p][:, 2 * t + par, 2 * pair:2 * pair + 2, :]
                                last = nc.tensor.matmul(q_ss[:, at:at + 1], rows, ones16[:], start=(p == 0),
                                                        stop=(p == 1))
                last.then_inc(ssq_ready, 1)

            def score(n, k):
                pe.wait_ge(kt_ready, n * per + k + 1)
                pe.wait_ge(free, item(n, k, QI + 3) + 1)
                for t in range(ST):
                    for pair in range(2):
                        for par in range(2):
                            at = 4 * t + 2 * pair + par
                            cols = slice(t * P + par * S, t * P + (par + 1) * S)
                            for i, (a, b) in enumerate(PASSES):
                                rows = q[a][:, 2 * t + par, 2 * pair:2 * pair + 2, :]
                                last = nc.tensor.matmul(scores[:, at, :], rows, kt[b][:, cols],
                                                        start=(i == 0), stop=(i == 2))
                last.then_inc(scores_ready, 1)

            def turn_probs(n, k):
                pe.wait_ge(probs_ready, n * per + k + 1)
                turned = scores[:].rearrange("p (t u) s -> p t (u s)", t=8)
                source = sc[:].rearrange("p (t u) s -> p t (u s)", t=8)
                for at in range(8):
                    last = nc.tensor.transpose(turned[:, at, :], source[:, at, :], env.ident[:])
                    if at % 4 == 3:
                        last.then_inc(pt_full, 1)

            def mix_values(n, k, tp):
                pe.wait_ge(pt_ready, 2 * (n * per + k) + tp + 1)
                if tp == 1:
                    pe.wait_ge(ot_ready, 4 * (n * per + k) + 2)
                for par in range(2):
                    rows = slice(par * S, (par + 1) * S)
                    for j in range(2):
                        t = 2 * tp + j
                        for i, (a, b) in enumerate(PASSES):
                            last = nc.tensor.matmul(
                                heads[par][:, j, :, :], v[a][rows, k % 2, t, :], pt[b][rows, t, :, :],
                                start=(i == 0), stop=(i == 2))
                    last.then_inc(heads_full, 1)

            def project_out(n, k):
                wg = parts(n, k)
                for t in range(ST):
                    if t % 2 == 0:
                        pe.wait_ge(ot_ready, 4 * (n * per + k) + 2 * (t // 2) + 2)
                    out = bank(k, OI + t)
                    pe.wait_ge(free, item(n, k, OI + t) - 1)
                    for h in range(H0):
                        for i, (a, b) in enumerate(PASSES):
                            last = nc.tensor.matmul(
                                out[:], ot[a][:, h, t * P:(t + 1) * P], wg[b][:, WO0 + h * D:WO0 + (h + 1) * D],
                                start=(h == 0 and i == 0), stop=(h == H0 - 1 and i == 2))
                    last.then_inc(full, 1)

            def body(n, k, front):
                ahead = (n, k + 1) if k < per - 1 else (n + 1, 0)
                score(n, k)
                if front:
                    project_kv(*ahead)
                    project_q(*ahead, range(0, 2))
                turn_probs(n, k)
                if front:
                    project_q(*ahead, range(2, 3))
                mix_values(n, k, 0)
                if front:
                    project_q(*ahead, range(3, 4))
                mix_values(n, k, 1)
                if front:
                    turn_k(*ahead)
                    q_squares(*ahead)
                project_out(n, k)

            pe.wait_ge(const_set, 2)
            project_kv(0, 0)
            project_q(0, 0, range(H0))
            turn_k(0, 0)
            q_squares(0, 0)
            run(pe, body)

        @block.scalar
        def _(act):
            def kv_out(n, k, h):
                act.wait_ge(full, item(n, k, KV + h) + 1)
                src = bank(k, KV + h)[:].rearrange("p (j c) -> p j c", j=2)
                nc.scalar.activation(k_f[:, 2 * h:2 * h + 2, :], src[:, :, 0:HD0], ACT.Copy)
                for j in range(2):
                    last = nc.scalar.activation(k_sq[:, 2 * h + j, :], src[:, j, 0:HD0], ACT.Square,
                                                accum_out=k_ss[:, 2 * h + j:2 * h + j + 1])
                last.then_inc(ssk_ready, 1)
                nc.scalar.activation(v[0][:, k % 2, 2 * h:2 * h + 2, :], src[:, :, HD0:KVCOLS], ACT.Copy)\
                    .then_inc(act_out, 1)

            def q_out(n, k, h):
                act.wait_ge(full, item(n, k, QI + h) + 1)
                src = bank(k, QI + h)[:].rearrange("p (b s) -> p b s", s=S)
                if h >= 2:
                    act.wait_ge(sq_ready, H0 * (n * per + k) + h - 1)
                nc.scalar.activation(q_sq[:, h % 2], src, ACT.Square)
                nc.scalar.activation(q[0][:, :, h, :], src, ACT.Copy).then_inc(act_out, 1)
                act.wait_ge(act_out, 6 * (n * per + k) + 2 + h + 1)
                nc.scalar.activation(q_sq16[0][:, :, h, :], q_sq[:, h % 2], ACT.Copy).then_inc(sq_high, 1)

            def exponent(n, k):
                act.wait_ge(shifted, n * per + k + 1)
                nc.scalar.activation(sc[:], sc[:], ACT.Exp).then_inc(exp_done, 1)

            def probs_out(n, k):
                for h in range(2):
                    act.wait_ge(pt_full, 2 * (n * per + k) + h + 1)
                    nc.scalar.activation(pt[0][:, 2 * h:2 * h + 2, :, :].rearrange("p t u s -> p (t u s)"),
                                         scores[:, 8 * h:8 * h + 8, :].rearrange("p a s -> p (a s)"), ACT.Copy)\
                        .then_inc(pt_high, 1)

            def heads_out(n, k, tp):
                for par in range(2):
                    act.wait_ge(heads_full, 4 * (n * per + k) + 2 * tp + par + 1)
                    nc.scalar.activation(head_out(0, tp, par), heads[par][:], ACT.Copy).then_inc(ot_high, 1)

            def keys_out(n, k):
                act.wait_ge(kt_full, n * per + k + 1)
                nc.scalar.activation(kt[0][:], k_turned[:], ACT.Copy, scale=qkw[:, 0:1]).then_inc(kt_high, 1)

            def body(n, k, front):
                ahead = (n, k + 1) if k < per - 1 else (n + 1, 0)
                if front:
                    for h in range(2):
                        kv_out(*ahead, h)
                exponent(n, k)
                if front:
                    for h in range(2):
                        q_out(*ahead, h)
                probs_out(n, k)
                if front:
                    q_out(*ahead, 2)
                heads_out(n, k, 0)
                if front:
                    q_out(*ahead, 3)
                heads_out(n, k, 1)
                if front:
                    keys_out(*ahead)

            act.wait_ge(env.staged.loaded["a0"], 16)
            for c in range(10):
                cols = slice(c * CHUNK0, (c + 1) * CHUNK0)
                nc.scalar.activation(w_split[0][0][:, cols], w_f[:, cols], ACT.Copy).then_inc(first_high, 1)
            act.wait_ge(qkw_ready, 1)
            for h in range(2):
                kv_out(0, 0, h)
            for h in range(H0):
                q_out(0, 0, h)
            keys_out(0, 0)
            run(act, body)

        @block.vector
        def _(dve):
            dve.wait_ge(const_in, 48)
            nc.vector.tensor_scalar(qkw[:], qkw_in[:, 0:1], qkw_in[:, 1:2], float(np.sqrt(HD0)),
                                    ALU.mult, ALU.mult).then_inc(qkw_ready, 1)
            wide = lambda a: a[:].unsqueeze(2).broadcast_to([P, 16, S])
            LINKS = 4

            def softmax_front(n, k):
                at = (n * per + k) * LINKS
                dve.wait_ge(rq_ready, n * per + k + 1)
                dve.wait_ge(scores_ready, n * per + k + 1)
                nc.vector.tensor_tensor(sc[:], scores[:], wide(q_r), ALU.mult).then_inc(chain, 1)
                dve.wait_ge(chain, at + 1)
                nc.vector.tensor_tensor(sc[:], sc[:], mask[:].unsqueeze(1).broadcast_to([P, 16, S]), ALU.add)\
                    .then_inc(chain, 1)
                dve.wait_ge(chain, at + 2)
                nc.vector.tensor_reduce(mx[:], sc[:], AX.X, ALU.max).then_inc(chain, 1)
                dve.wait_ge(chain, at + 3)
                nc.vector.tensor_tensor(sc[:], sc[:], wide(mx), ALU.subtract).then_inc(shifted, 1)

            def softmax_sum(n, k):
                at = (n * per + k) * LINKS
                dve.wait_ge(exp_done, n * per + k + 1)
                nc.vector.tensor_reduce(den[:], sc[:], AX.X, ALU.add).then_inc(chain, 1)
                dve.wait_ge(chain, at + 4)
                nc.vector.reciprocal(rden[:], den[:]).then_inc(rden_ready, 1)

            def kv_low(n, k, h):
                dve.wait_ge(act_out, 6 * (n * per + k) + h + 1)
                src = bank(k, KV + h)[:].rearrange("p (j c) -> p j c", j=2)
                tiles = slice(2 * h, 2 * h + 2)
                nc.vector.tensor_tensor(v[1][:, k % 2, tiles, :], src[:, :, HD0:KVCOLS], v[0][:, k % 2, tiles, :],
                                        ALU.subtract).then_inc(free, 1)

            def q_low(n, k, h):
                dve.wait_ge(act_out, 6 * (n * per + k) + 2 + h + 1)
                nc.vector.tensor_tensor(q[1][:, :, h, :], bank(k, QI + h)[:].rearrange("p (b s) -> p b s", s=S),
                                        q[0][:, :, h, :], ALU.subtract)\
                    .then_inc(free, 1)
                dve.wait_ge(sq_high, H0 * (n * per + k) + h + 1)
                nc.vector.tensor_tensor(q_sq16[1][:, :, h, :], q_sq[:, h % 2], q_sq16[0][:, :, h, :],
                                        ALU.subtract).then_inc(sq_ready, 1)

            def probs_low(n, k):
                for h in range(2):
                    dve.wait_ge(pt_high, 2 * (n * per + k) + h + 1)
                    flat = [pt[part][:, 2 * h:2 * h + 2, :, :].rearrange("p t u s -> p (t u s)") for part in range(2)]
                    nc.vector.tensor_tensor(flat[1], scores[:, 8 * h:8 * h + 8, :].rearrange("p a s -> p (a s)"),
                                            flat[0], ALU.subtract).then_inc(pt_ready, 1)

            def heads_low(n, k, tp):
                for par in range(2):
                    dve.wait_ge(ot_high, 4 * (n * per + k) + 2 * tp + par + 1)
                    nc.vector.tensor_tensor(head_out(1, tp, par), heads[par][:], head_out(0, tp, par),
                                            ALU.subtract).then_inc(ot_ready, 1)

            def keys_squared(n, k):
                dve.wait_ge(ssk_ready, 2 * (n * per + k) + 2)
                nc.vector.tensor_scalar(k_se[:], k_ss[:], HD0 * EPS, None, ALU.add).then_inc(sek_ready, 1)

            def keys_scaled(n, k):
                dve.wait_ge(rk_ready, n * per + k + 1)
                for t in range(ST):
                    last = nc.vector.tensor_scalar(k_n[:, t, :], k_f[:, t, :], k_r[:, t:t + 1], None, ALU.mult)
                last.then_inc(kn_ready, 1)

            def norms_out(n, k):
                dve.wait_ge(kt_high, n * per + k + 1)
                nc.vector.scalar_tensor_tensor(kt[1][:], k_turned[:], qkw[:, 0:1], kt[0][:],
                                               ALU.mult, ALU.subtract).then_inc(kt_ready, 1)
                dve.wait_ge(ssq_ready, n * per + k + 1)
                nc.vector.tensor_scalar(q_se[:], q_ss[:, 0:16], HD0 * EPS, None, ALU.add).then_inc(seq_ready, 1)

            def add_out(n, k):
                for t in range(ST):
                    dve.wait_ge(full, item(n, k, OI + t) + 1)
                    tile = env.x[:, (k % NS) * ST + t, :]
                    nc.vector.scalar_tensor_tensor(tile, bank(k, OI + t)[:], env.tg[:, 0:1], tile,
                                                   ALU.mult, ALU.add).then_inc(free, 1)

            def body(n, k, front):
                ahead = (n, k + 1) if k < per - 1 else (n + 1, 0)
                softmax_front(n, k)
                if front:
                    for h in range(2):
                        kv_low(*ahead, h)
                    keys_squared(*ahead)
                softmax_sum(n, k)
                if front:
                    keys_scaled(*ahead)
                    for h in range(2):
                        q_low(*ahead, h)
                probs_low(n, k)
                if front:
                    q_low(*ahead, 2)
                heads_low(n, k, 0)
                if front:
                    q_low(*ahead, 3)
                heads_low(n, k, 1)
                if front:
                    norms_out(*ahead)
                add_out(n, k)

            for c in range(10):
                cols = slice(c * CHUNK0, (c + 1) * CHUNK0)
                dve.wait_ge(first_high, c + 1)
                nc.vector.tensor_tensor(w_split[0][1][:, cols], w_f[:, cols], w_split[0][0][:, cols], ALU.subtract)\
                    .then_inc(first_ready, 1)
            for h in range(2):
                kv_low(0, 0, h)
            keys_squared(0, 0)
            keys_scaled(0, 0)
            for h in range(H0):
                q_low(0, 0, h)
            norms_out(0, 0)
            run(dve, body)


def first_tile(j, k, ahead):
    if not ahead:
        return j * (2 * ST) + k * ST
    return j * (2 * ST) + ST if k == 0 else j * (-2 * ST) + 2 * ST



E_ = 4


def experts_phase(nc, env, d, name, rank, top2, lora_scale, gate):
    R = E_ * rank
    RB = R if top2 else R + 1
    with ExitStack() as ctx:
        sem = semaphores(nc, ctx, f"{name}_")
        sb = lambda n, shape, dt=F32: ctx.enter_context(nc.sbuf_tensor(f"{name}_{n}", shape, dt))
        ps = lambda n, shape: ctx.enter_context(nc.psum_tensor(f"{name}_{n}", shape, F32))
        norm = StepNorm(nc, env, ctx, name, "f32" if top2 else "split")
        down = sb("down", [P, KC, R + E_])
        up = sb("up", [RB, D])
        if not top2:
            dense_f = sb("dense_f", [P, KC, D])
            dense = [sb(f"dense{part}", [P, KC, D], BF16) for part in range(2)]
            downs = [sb(f"down{part}", [P, KC, R + E_], BF16) for part in range(2)]
        earlier = sb("earlier", [P, E_, E_])
        lg = sb("lg", [P, ST, E_])
        greater = sb("greater", [P, ST, E_, E_])
        equal = sb("equal", [P, ST, E_, E_])
        rank_of = sb("rank", [P, ST, E_])
        mx = sb("mx", [P, ST])
        den = sb("den", [P, ST])
        rden = sb("rden", [P, ST])
        ex = sb("ex", [P, ST, E_])
        gates = sb("gates", [P, ST, E_])
        mid = sb("mid", [P, ST, P])
        mid_t = sb("mid_t", [RB, W])
        a_ps = [ps(f"a{b}", [P, ST, P]) for b in range(2)]
        m_ps = ps("m", [P, W])
        out_ps = [ps(f"out{b}", [P, D]) for b in range(2)]
        w_in, const_set, a_full, link, shifted, ex_done, mid_ready, m_full, mid_t_ready, out_full, out_free = map(
            sem, ("w_in", "const", "a_full", "link", "shifted", "ex", "mid", "m_full", "mid_t", "out_full",
                  "out_free"))
        rden_done = sem("rden_done")
        w_high, w_ready = map(sem, ("w_high", "w_ready"))
        LINKS = 9 if top2 else 3
        block = ctx.enter_context(nc.Block())

        @block.sync
        def _(sp):
            sp.dma_start(down[:], d[f"{name}_down"]).then_inc(w_in, 16)
            sp.dma_start(up[:], d[f"{name}_up"]).then_inc(w_in, 16)
            if not top2:
                sp.dma_start(dense_f[:], d[f"{name}_dense"]).then_inc(w_in, 16)
            sp.wait_ge(w_in, 32 if top2 else 48)

        @block.gpsimd
        def _(pool):
            norm.pool_start(pool)
            nc.gpsimd.memset(mid[:, :, RB:P], 0.0).then_inc(const_set, 1)
            if top2:
                for e in range(E_):
                    nc.gpsimd.memset(earlier[:, e, 0:e] if e else earlier[:, 0, 0:1], 1.0 if e else 0.0)\
                        .then_inc(const_set, 1)
                    if e:
                        nc.gpsimd.memset(earlier[:, e, e:E_], 0.0).then_inc(const_set, 1)
                nc.gpsimd.memset(earlier[:, 0, 1:E_], 0.0).then_inc(const_set, 1)
            else:
                nc.gpsimd.memset(mid[:, :, R:RB], 1.0).then_inc(const_set, 1)
            for n in range(2):
                norm.pool(pool, n)
            if not top2:
                pool.wait_ge(w_high, 1)
                nc.gpsimd.tensor_tensor(downs[1][:], down[:], downs[0][:], ALU.subtract).then_inc(w_ready, 1)
                for c in range(KC):
                    pool.wait_ge(w_high, c + 2)
                    nc.gpsimd.tensor_tensor(dense[1][:, c, :], dense_f[:, c, :], dense[0][:, c, :], ALU.subtract)\
                        .then_inc(w_ready, 1)
            with pool.Fori(0, NS // 2) as j:
                for k in range(2):
                    norm.pool(pool, 2 * j + k + 2)

        @block.tensor
        def _(pe):
            def rest(n, par):
                pe.wait_ge(mid_ready, n + 1)
                for t in range(ST):
                    last = nc.tensor.transpose(m_ps[:, t * P:(t + 1) * P], mid[:, t, :], env.ident[:])
                last.then_inc(m_full, 1)
                for t in range(ST):
                    pe.wait_ge(out_free, 1 + (ST * n + t - 1 if t else ST * n))
                    if not top2:
                        for c in range(KC):
                            for p, (a, b) in enumerate(PASSES):
                                nc.tensor.matmul(out_ps[t % 2][:], norm.xt[a][:, par, c, t * P:(t + 1) * P],
                                                 dense[b][:, c, :], start=(c == 0 and p == 0), stop=False)
                    if t == 0:
                        pe.wait_ge(mid_t_ready, n + 1)
                    nc.tensor.matmul(out_ps[t % 2][:], mid_t[:, t * P:(t + 1) * P], up[:],
                                     start=top2, stop=True).then_inc(out_full, 1)

            def first(n, par):
                pe.wait_ge(norm.evacuated, ST * n + ST)
                for t in range(ST):
                    cols = slice(t * P, (t + 1) * P)
                    for c in range(KC):
                        if top2:
                            last = nc.tensor.matmul(a_ps[par][:, t, 0:R + E_], norm.xt32[:, par, c, cols],
                                                    down[:, c, :], start=(c == 0), stop=(c == KC - 1))
                            continue
                        for p, (a, b) in enumerate(PASSES):
                            last = nc.tensor.matmul(a_ps[par][:, t, 0:R + E_], norm.xt[a][:, par, c, cols],
                                                    downs[b][:, c, :], start=(c == 0 and p == 0),
                                                    stop=(c == KC - 1 and p == 2))
                last.then_inc(a_full, 1)

            norm.pe(pe, 0)
            pe.wait_ge(w_in, 32 if top2 else 48)
            if not top2:
                pe.wait_ge(w_ready, KC + 1)
            first(0, 0)
            with pe.Fori(0, NS // 2) as j:
                for k in range(2):
                    n = 2 * j + k
                    norm.pe(pe, n + 1)
                    first(n + 1, 1 - k)
                    rest(n, k)

        @block.scalar
        def _(act):
            norm.act(act, 0, 0)
            if not top2:
                act.wait_ge(w_in, 48)
                nc.scalar.activation(downs[0][:], down[:], ACT.Copy).then_inc(w_high, 1)
                for c in range(KC):
                    nc.scalar.activation(dense[0][:, c, :], dense_f[:, c, :], ACT.Copy).then_inc(w_high, 1)
            with act.Fori(0, NS // 2) as j:
                for k in range(2):
                    n = 2 * j + k
                    norm.act(act, n + 1, 1 - k)
                    act.wait_ge(shifted, n + 1)
                    nc.scalar.activation(ex[:], ex[:], ACT.Exp).then_inc(ex_done, 1)
                    act.wait_ge(m_full, n + 1)
                    nc.scalar.activation(mid_t[:], m_ps[0:RB, :], ACT.Copy).then_inc(mid_t_ready, 1)

        @block.vector
        def _(dve):
            dve.wait_ge(const_set, 9 if top2 else 2)
            wide = lambda a: a.unsqueeze(2).broadcast_to([P, ST, E_])
            nc.vector.memset(norm.pace[:], 0.0).then_inc(out_free, 1)
            norm.dve(dve, 0, 0, 0)
            if not top2:
                norm.dve_low(dve, 0, 0)
            norm.dve(dve, 1, 1, ST)
            with dve.Fori(0, NS // 2) as j:
                for k in range(2):
                    n = 2 * j + k
                    at = n * LINKS
                    if not top2:
                        norm.dve_low(dve, n + 1, 1 - k)
                    dve.wait_ge(a_full, n + 1)
                    nc.vector.tensor_copy(lg[:], a_ps[k][:, :, R:R + E_]).then_inc(link, 1)
                    dve.wait_ge(link, at + 1)
                    nc.vector.tensor_reduce(mx[:], lg[:], AX.X, ALU.max).then_inc(link, 1)
                    dve.wait_ge(link, at + 2)
                    nc.vector.tensor_tensor(ex[:], lg[:], wide(mx[:]), ALU.subtract).then_inc(shifted, 1)
                    if top2:
                        mine = lg[:].unsqueeze(3).broadcast_to([P, ST, E_, E_])
                        other = lg[:].unsqueeze(2).broadcast_to([P, ST, E_, E_])
                        nc.vector.tensor_tensor(greater[:], other, mine, ALU.is_gt).then_inc(link, 1)
                        nc.vector.tensor_tensor(equal[:], other, mine, ALU.is_equal).then_inc(link, 1)
                        dve.wait_ge(link, at + 4)
                        nc.vector.tensor_tensor(equal[:], equal[:], earlier[:].unsqueeze(1).broadcast_to(
                            [P, ST, E_, E_]), ALU.mult).then_inc(link, 1)
                        dve.wait_ge(link, at + 5)
                        nc.vector.tensor_tensor(greater[:], greater[:], equal[:], ALU.add).then_inc(link, 1)
                        dve.wait_ge(link, at + 6)
                        nc.vector.tensor_reduce(rank_of[:], greater[:], AX.X, ALU.add).then_inc(link, 1)
                        dve.wait_ge(link, at + 7)
                        dve.wait_ge(ex_done, n + 1)
                        nc.vector.scalar_tensor_tensor(ex[:], rank_of[:], 1.5, ex[:], ALU.is_lt, ALU.mult)\
                            .then_inc(link, 1)
                        dve.wait_ge(link, at + 8)
                    dve.wait_ge(ex_done, n + 1)
                    nc.vector.tensor_reduce(den[:], ex[:], AX.X, ALU.add).then_inc(link, 1)
                    dve.wait_ge(link, at + LINKS)
                    nc.vector.reciprocal(rden[:], den[:]).then_inc(rden_done, 1)
                    dve.wait_ge(rden_done, 2 * n + 1)
                    nc.vector.scalar_tensor_tensor(gates[:], ex[:], lora_scale, wide(rden[:]), ALU.mult, ALU.mult)\
                        .then_inc(rden_done, 1)
                    dve.wait_ge(rden_done, 2 * n + 2)
                    nc.vector.tensor_tensor(
                        mid[:, :, 0:R].rearrange("p t (e r) -> p t e r", e=E_),
                        a_ps[k][:, :, 0:R].rearrange("p t (e r) -> p t e r", e=E_),
                        gates[:].unsqueeze(3).broadcast_to([P, ST, E_, rank]), ALU.mult).then_inc(mid_ready, 1)
                    norm.dve(dve, n + 2, k, j * (-2 * ST) + (k + 2) * ST)
                    for t in range(ST):
                        dve.wait_ge(out_full, ST * n + t + 1)
                        tile = env.x[:, first_tile(j, k, False) + t, :]
                        nc.vector.scalar_tensor_tensor(tile, out_ps[t % 2][:], env.tg[:, gate:gate + 1], tile,
                                                       ALU.mult, ALU.add).then_inc(out_free, 1)



def attention1_phase(nc, env, d):
    scale = float(D) ** -0.5
    with ExitStack() as ctx:
        sem = semaphores(nc, ctx, "a1_")
        sb = lambda n, shape, dt=F32: ctx.enter_context(nc.sbuf_tensor(f"a1_{n}", shape, dt))
        ps = lambda n, shape: ctx.enter_context(nc.psum_tensor(f"a1_{n}", shape, F32))
        norm = StepNorm(nc, env, ctx, "a1", "split")
        w_f = env.staged.tile[:, 0:2 * KC * D].rearrange("p (i c d) -> p i c d", i=2, c=KC)
        w = [sb(f"w{part}", [P, 2, KC, D], BF16) for part in range(2)]
        bias = sb("bias", [P, 2, KC])
        c_rows = sb("c_rows", [P, 2, ST, D])
        qk = [sb(f"qk{part}", [P, 2, KC, W], BF16) for part in range(2)]
        sc = sb("sc", [P, ST, S])
        mx = sb("mx", [P, ST])
        den = sb("den", [P, ST])
        rden = sb("rden", [P, ST])
        probs = sb("probs", [P, ST, P])
        pt = sb("pt", [P, ST, P])
        ring = [ps(f"ring{b}", [P, W]) for b in range(2)]
        s_ps = ps("s", [P, ST, P])
        t_ps = ps("t", [P, ST, P])
        c_in = [sem(f"c_in{k}") for k in range(2)]
        (w_in, w_high, w_ready, const_set, full, high, free, s_full, link, shifted, ex_done, probs_ready,
         t_full, pt_ready) = map(sem, (
             "w_in", "w_high", "w_ready", "const", "full", "high", "free", "s_full", "link", "shifted",
             "ex", "probs", "t_full", "pt"))
        RING = 2 * KC + ST
        block = ctx.enter_context(nc.Block())

        @block.sync
        def _(sp):
            sp.dma_start(bias[:], d["a1_bias"]).then_inc(w_in, 16)
            rows = d["ctx"].rearrange("(t p) d -> p t d", p=P)
            for k in range(2):
                sp.dma_start(c_rows[:, k], rows[:, k * ST:(k + 1) * ST, :]).then_inc(c_in[k], 16)
            sp.wait_ge(w_ready, 2 * KC)
            env.staged.load_next(sp)
            for k in range(2):
                sp.wait_ge(full, RING * (k + 1))
                sp.dma_start(c_rows[:, k], rows[:, (k + 2) * ST:(k + 3) * ST, :]).then_inc(c_in[k], 16)
            for k in range(2):
                sp.wait_ge(c_in[k], 32)

        @block.gpsimd
        def _(pool):
            norm.pool_start(pool)
            nc.gpsimd.memset(probs[:], 0.0).then_inc(const_set, 1)
            norm.pool(pool, 0)
            for i in range(2):
                for c in range(KC):
                    pool.wait_ge(w_high, i * KC + c + 1)
                    nc.gpsimd.tensor_tensor(w[1][:, i, c, :], w_f[:, i, c, :], w[0][:, i, c, :],
                                            ALU.subtract).then_inc(w_ready, 1)
            with pool.Fori(0, NS // 2) as j:
                for k in range(2):
                    norm.pool(pool, 2 * j + k + 1)

        @block.tensor
        def _(pe):
            def project(n, par, i):
                for m in range(KC):
                    it = i * KC + m
                    pe.wait_ge(free, 1 + (RING * n + it - 1 if it else RING * n))
                    for c in range(KC):
                        for p, (a, b) in enumerate(PASSES):
                            moving = norm.xt[b][:, par, c, :] if i == 0 else env.ct[b][:, c, bass.ds(n * W, W)]
                            last = nc.tensor.matmul(ring[it % 2][:], w[a][:, i, c, m * P:(m + 1) * P], moving,
                                                    start=(c == 0 and p == 0), stop=(c == KC - 1 and p == 2))
                    last.then_inc(full, 1)

            norm.pe(pe, 0)
            pe.wait_ge(w_ready, 2 * KC)
            with pe.Fori(0, NS // 2) as j:
                for k in range(2):
                    n = 2 * j + k
                    pe.wait_ge(norm.low_done, ST * n + ST)
                    project(n, k, 0)
                    project(n, k, 1)
                    norm.pe(pe, n + 1)
                    pe.wait_ge(free, 1 + RING * n + 2 * KC)
                    for t in range(ST):
                        cols = slice(t * P, (t + 1) * P)
                        for m in range(KC):
                            for p, (a, b) in enumerate(PASSES):
                                last = nc.tensor.matmul(s_ps[:, t, :], qk[a][:, 0, m, cols], qk[b][:, 1, m, cols],
                                                        start=(m == 0 and p == 0), stop=(m == KC - 1 and p == 2))
                    last.then_inc(s_full, 1)
                    pe.wait_ge(probs_ready, n + 1)
                    for t in range(ST):
                        last = nc.tensor.transpose(t_ps[:, t, :], probs[:, t, :], env.ident[:])
                    last.then_inc(t_full, 1)
                    pe.wait_ge(c_in[k], j * 16 + 16)
                    pe.wait_ge(pt_ready, n + 1)
                    for t in range(ST):
                        it = 2 * KC + t
                        pe.wait_ge(free, 1 + RING * n + it - 1)
                        nc.tensor.matmul(ring[it % 2][:], pt[:, t, :], c_rows[:, k, t, :],
                                         start=True, stop=True).then_inc(full, 1)

        @block.scalar
        def _(act):
            act.wait_ge(env.staged.loaded["a1"], 16)
            for i in range(2):
                for c in range(KC):
                    nc.scalar.activation(w[0][:, i, c, :], w_f[:, i, c, :], ACT.Copy).then_inc(w_high, 1)
            norm.act(act, 0, 0)
            act.wait_ge(w_in, 16)
            with act.Fori(0, NS // 2) as j:
                for k in range(2):
                    n = 2 * j + k
                    for it in range(2 * KC):
                        act.wait_ge(full, RING * n + it + 1)
                        nc.scalar.activation(qk[0][:, it // KC, it % KC, :], ring[it % 2][:], ACT.Identity,
                                             bias=bias[:, it // KC, it % KC:it % KC + 1]).then_inc(high, 1)
                    norm.act(act, n + 1, 1 - k)
                    act.wait_ge(shifted, n + 1)
                    nc.scalar.activation(sc[:], sc[:], ACT.Exp, scale=scale).then_inc(ex_done, 1)
                    act.wait_ge(t_full, n + 1)
                    nc.scalar.activation(pt[:], t_ps[:], ACT.Copy).then_inc(pt_ready, 1)

        @block.vector
        def _(dve):
            dve.wait_ge(const_set, 1)
            wide = lambda a: a[:].unsqueeze(2).broadcast_to([P, ST, S])
            halves = [slice(0, S), slice(S, P)]
            nc.vector.memset(norm.pace[:], 0.0).then_inc(free, 1)
            norm.dve(dve, 0, 0, 0)
            norm.dve_low(dve, 0, 0)
            with dve.Fori(0, NS // 2) as j:
                for k in range(2):
                    n = 2 * j + k
                    norm.dve(dve, n + 1, 1 - k, first_tile(j, k, True))
                    for it in range(2 * KC):
                        dve.wait_ge(high, 2 * KC * n + it + 1)
                        nc.vector.scalar_tensor_tensor(
                            qk[1][:, it // KC, it % KC, :], ring[it % 2][:], bias[:, it // KC, it % KC:it % KC + 1],
                            qk[0][:, it // KC, it % KC, :], ALU.add, ALU.subtract).then_inc(free, 1)
                    norm.dve_low(dve, n + 1, 1 - k)
                    dve.wait_ge(s_full, n + 1)
                    for rows in halves:
                        nc.vector.tensor_copy(sc[rows], s_ps[rows, :, rows]).then_inc(link, 1)
                    dve.wait_ge(link, 5 * n + 2)
                    nc.vector.tensor_reduce(mx[:], sc[:], AX.X, ALU.max).then_inc(link, 1)
                    dve.wait_ge(link, 5 * n + 3)
                    nc.vector.tensor_tensor(sc[:], sc[:], wide(mx), ALU.subtract).then_inc(shifted, 1)
                    dve.wait_ge(ex_done, n + 1)
                    nc.vector.tensor_reduce(den[:], sc[:], AX.X, ALU.add).then_inc(link, 1)
                    dve.wait_ge(link, 5 * n + 4)
                    nc.vector.reciprocal(rden[:], den[:]).then_inc(link, 1)
                    dve.wait_ge(link, 5 * n + 5)
                    for rows in halves:
                        last = nc.vector.tensor_tensor(probs[rows, :, rows], sc[rows], wide(rden)[rows], ALU.mult)
                    last.then_inc(probs_ready, 1)
                    for t in range(ST):
                        it = 2 * KC + t
                        dve.wait_ge(full, RING * n + it + 1)
                        tile = env.x[:, first_tile(j, k, False) + t, :]
                        nc.vector.scalar_tensor_tensor(tile, ring[it % 2][:], env.tg[:, 1:2], tile,
                                                       ALU.mult, ALU.add).then_inc(free, 1)



G2, J2, HD2 = 8, 4, 16
KV2 = G2 * HD2


def attention2_phase(nc, env, d):
    scale = float(HD2) ** -0.5
    NB = 2 * ST
    with ExitStack() as ctx:
        sem = semaphores(nc, ctx, "a2_")
        sb = lambda n, shape, dt=F32: ctx.enter_context(nc.sbuf_tensor(f"a2_{n}", shape, dt))
        ps = lambda n, shape: ctx.enter_context(nc.psum_tensor(f"a2_{n}", shape, F32))
        norm = StepNorm(nc, env, ctx, "a2", "split")
        WCOLS = D + 2 * KV2
        w_f = env.staged.tile[:, 0:KC * WCOLS].rearrange("p (c n) -> p c n", c=KC)
        w = [sb(f"w{part}", [P, KC, WCOLS], BF16) for part in range(2)]
        wo = sb("wo", [P, J2, D])
        bo = sb("bo", [1, D])
        qk_bias = sb("qk_bias", [P, J2 + 1])
        v_bias = sb("v_bias", [P, KV2])
        g_mask = sb("g_mask", [P, G2])
        v_mask = sb("v_mask", [P, KV2])
        q = sb("q", [P, NB, J2, S])
        kt = sb("kt", [P, W])
        k_block = sb("k_block", [P, 4, G2, S])
        v = sb("v", [P, ST, KV2])
        v_swap = sb("v_swap", [P, ST, KV2])
        v_block = sb("v_block", [P, NB, KV2])
        sc = sb("sc", [P, 3, 2 * G2, S])
        mx = sb("mx", [P, 2 * G2])
        den = sb("den", [P, 2, 2 * G2])
        rden = sb("rden", [P, 2, 2 * G2])
        pt = sb("pt", [P, 2, 4, 2 * P])
        y = sb("y", [P, J2, W])
        ring = [ps(f"ring{b}", [P, W]) for b in range(2)]
        s_ps = ps("s", [P, 2 * G2, S])
        t_ps = ps("t", [P, 4, 2, P])
        (w_in, w_high, w_ready, full, act_free, dve_free, v_moved, v_block_ready, k_block_ready, s_full, link, shifted,
         ex_done, rden_ready, probs_ready, t_full, pt_ready, summed) = map(sem, (
             "w_in", "w_high", "w_ready", "full", "act_free", "dve_free", "v_moved", "v_block", "k_block", "s_full",
             "link", "shifted", "ex", "rden", "probs", "t_full", "pt", "summed"))
        LOADS = 6
        RING = J2 + 2 + 2 * ST
        VI = J2 + 1
        HI = lambda t: J2 + 2 + 2 * t
        block = ctx.enter_context(nc.Block())
        ACT_READS = [*range(J2 + 1), *(HI(t) for t in range(ST))]
        DVE_READS = [VI, *(HI(t) + 1 for t in range(ST))]

        def is_read(n, it):
            prev = (it - 2) % RING
            sem_, reads, base = (act_free, ACT_READS, 0) if prev in ACT_READS else (dve_free, DVE_READS, 1)
            return sem_, base + n * len(reads) + (reads.index(prev) + 1) % (len(reads) if it < 2 else RING)

        @block.sync
        def _(sp):
            for tile, name in ((wo, "a2_wo"), (bo, "a2_bo"), (qk_bias, "a2_qk_bias"),
                               (v_bias, "a2_v_bias"), (g_mask, "g_mask"), (v_mask, "v_mask")):
                sp.dma_start(tile[:], d[name]).then_inc(w_in, 16)
            sp.wait_ge(w_ready, KC)
            env.staged.load_next(sp)
            with sp.Fori(0, NS) as n:
                sp.wait_ge(dve_free, len(DVE_READS) * n + 2)
                sp.dma_start(v_swap[S:P], v[0:S]).then_inc(v_moved, 16)
                sp.dma_start(v_swap[0:S], v[S:P]).then_inc(v_moved, 16)
            sp.wait_ge(v_moved, 32 * NS)

        @block.gpsimd
        def _(pool):
            norm.pool_start(pool)
            norm.pool(pool, 0)
            for c in range(KC):
                pool.wait_ge(w_high, c + 1)
                nc.gpsimd.tensor_tensor(w[1][:, c, :], w_f[:, c, :], w[0][:, c, :], ALU.subtract).then_inc(w_ready, 1)

            def block_keys(n, b):
                if b == 0:
                    pool.wait_ge(act_free, len(ACT_READS) * n + J2 + 1)
                if b >= 4:
                    pool.wait_ge(s_full, NB * n + b - 3)
                keys = kt[:, b * S:(b + 1) * S].unsqueeze(1)
                nc.gpsimd.tensor_tensor(k_block[:, b % 4], keys.broadcast_to([P, G2, S]),
                                        g_mask[:].unsqueeze(2).broadcast_to([P, G2, S]), ALU.mult)\
                    .then_inc(k_block_ready, 1)

            pool.wait_ge(w_in, 16 * LOADS)
            with pool.Fori(0, NS // 2) as j:
                for k in range(2):
                    n = 2 * j + k
                    norm.pool(pool, n + 1)
                    for b in range(3):
                        block_keys(n, b)
                    for b in range(NB):
                        if b + 3 < NB:
                            block_keys(n, b + 3)
                        pool.wait_ge(rden_ready, NB * n + b + 1)
                        nc.gpsimd.tensor_tensor(sc[:, b % 3], sc[:, b % 3],
                                                rden[:, b % 2].unsqueeze(2).broadcast_to([P, 2 * G2, S]), ALU.mult)\
                            .then_inc(probs_ready, 1)

        @block.tensor
        def _(pe):
            def score(n, b):
                pe.wait_ge(k_block_ready, NB * n + b + 1)
                if b:
                    pe.wait_ge(shifted, NB * n + b)
                for jp in range(2):
                    last = nc.tensor.matmul(s_ps[:, jp * G2:(jp + 1) * G2, :], q[:, b, 2 * jp:2 * jp + 2, :],
                                            k_block[:, b % 4], start=True, stop=True)
                last.then_inc(s_full, 1)

            def turn(n, b):
                if b:
                    pe.wait_ge(pt_ready, NB * n + b)
                pe.wait_ge(probs_ready, NB * n + b + 1)
                for jp in range(2):
                    for gp in range(4):
                        at = jp * G2 + 2 * gp
                        last = nc.tensor.transpose(t_ps[:, gp, jp, :], sc[:, b % 3, at:at + 2, :], env.ident[:])
                last.then_inc(t_full, 1)

            def mix(n, b):
                it = HI(b // 2)
                if b % 2 == 0:
                    pe.wait_ge(*is_read(n, it))
                if b == 0:
                    pe.wait_ge(v_block_ready, n + 1)
                pe.wait_ge(pt_ready, NB * n + b + 1)
                for gp in range(4):
                    rows = slice(32 * gp, 32 * gp + 32)
                    last = nc.tensor.matmul(ring[it % 2][rows, (b % 2) * 256:(b % 2) * 256 + 256], v_block[:, b, rows],
                                            pt[:, b % 2, gp, :], start=True, stop=True, tile_position=(0, 32 * gp))
                if b % 2:
                    last.then_inc(full, 1)

            def project_out(n, t):
                it = HI(t) + 1
                pe.wait_ge(*is_read(n, it))
                nc.tensor.matmul(ring[it % 2][:], env.ones[0:1, :], bo[:], start=True, stop=False)
                pe.wait_ge(act_free, len(ACT_READS) * n + J2 + 1 + t + 1)
                for j in range(J2):
                    last = nc.tensor.matmul(ring[it % 2][:], y[:, j, t * P:(t + 1) * P], wo[:, j, :],
                                            start=False, stop=(j == J2 - 1))
                last.then_inc(full, 1)

            norm.pe(pe, 0)
            pe.wait_ge(w_ready, KC)
            pe.wait_ge(w_in, 16 * LOADS)
            with pe.Fori(0, NS // 2) as jj:
                for k in range(2):
                    n = 2 * jj + k
                    pe.wait_ge(norm.low_done, ST * n + ST)
                    for it in range(J2 + 1):
                        if it:
                            pe.wait_ge(*is_read(n, it))
                        for c in range(KC):
                            for p, (a, b) in enumerate(PASSES):
                                moving = norm.xt[b][:, k, c, :] if it < J2 else env.ct[b][:, c, bass.ds(n * W, W)]
                                last = nc.tensor.matmul(ring[it % 2][:], w[a][:, c, it * P:(it + 1) * P], moving,
                                                        start=(c == 0 and p == 0), stop=(c == KC - 1 and p == 2))
                        last.then_inc(full, 1)
                    pe.wait_ge(*is_read(n, VI))
                    for t in range(ST):
                        for c in range(KC):
                            for p, (a, b) in enumerate(PASSES):
                                last = nc.tensor.matmul(
                                    ring[VI % 2][:, t * P:(t + 1) * P], env.ct[a][:, c, bass.ds(n * W + t * P, P)],
                                    w[b][:, c, D + KV2:WCOLS], start=(c == 0 and p == 0), stop=(c == KC - 1 and p == 2))
                    last.then_inc(full, 1)
                    norm.pe(pe, n + 1)
                    score(n, 0)
                    for b in range(NB + 3):
                        if b + 1 < NB:
                            score(n, b + 1)
                        if 1 <= b <= NB:
                            turn(n, b - 1)
                        if b >= 4 and b % 2 == 0:
                            project_out(n, b // 2 - 2)
                        if 2 <= b <= NB + 1:
                            mix(n, b - 2)

        def heads_out(act, n, t):
            act.wait_ge(full, RING * n + HI(t) + 1)
            nc.scalar.activation(y[:].rearrange("p j (t r q) -> p t r j q", t=ST, r=2)[:, t],
                                 ring[HI(t) % 2][:].rearrange("p (r j q) -> p r j q", r=2, j=J2), ACT.Copy)\
                .then_inc(act_free, 1)

        @block.scalar
        def _(act):
            act.wait_ge(env.staged.loaded["a2"], 16)
            for c in range(KC):
                nc.scalar.activation(w[0][:, c, :], w_f[:, c, :], ACT.Copy).then_inc(w_high, 1)
            norm.act(act, 0, 0)
            act.wait_ge(w_in, 16 * LOADS)

            def exponent(n, b):
                act.wait_ge(shifted, NB * n + b + 1)
                nc.scalar.activation(sc[:, b % 3], sc[:, b % 3], ACT.Exp, scale=scale).then_inc(ex_done, 1)

            with act.Fori(0, NS // 2) as jj:
                for k in range(2):
                    n = 2 * jj + k
                    for it in range(J2 + 1):
                        act.wait_ge(full, RING * n + it + 1)
                        src = ring[it % 2][:]
                        if it < J2:
                            nc.scalar.activation(q[:, :, it, :], src.rearrange("p (b s) -> p b s", s=S), ACT.Identity,
                                                 bias=qk_bias[:, it:it + 1]).then_inc(act_free, 1)
                        else:
                            nc.scalar.activation(kt[:], src, ACT.Identity,
                                                 bias=qk_bias[:, it:it + 1]).then_inc(act_free, 1)
                    norm.act(act, n + 1, 1 - k)
                    exponent(n, 0)
                    for b in range(NB + 2):
                        if b + 1 < NB:
                            exponent(n, b + 1)
                        if 1 <= b <= NB:
                            act.wait_ge(t_full, NB * n + b)
                            nc.scalar.activation(pt[:, (b - 1) % 2].rearrange("p g n -> p (g n)"),
                                                 t_ps[:].rearrange("p g j n -> p (g j n)"), ACT.Copy)\
                                .then_inc(pt_ready, 1)
                        if b >= 3 and b % 2:
                            heads_out(act, n, b // 2 - 1)

        def add(dve, n, t, tile0):
            dve.wait_ge(full, RING * n + HI(t) + 2)
            tile = env.x[:, tile0 + t, :]
            nc.vector.scalar_tensor_tensor(tile, ring[(HI(t) + 1) % 2][:], env.tg[:, 2:3], tile, ALU.mult, ALU.add)\
                .then_inc(dve_free, 1)


        @block.vector
        def _(dve):
            dve.wait_ge(w_in, 16 * LOADS)
            wide = lambda a: a[:].unsqueeze(2).broadcast_to([P, 2 * G2, S])
            nc.vector.memset(norm.pace[:], 0.0).then_inc(dve_free, 1)
            norm.dve(dve, 0, 0, 0)
            norm.dve_low(dve, 0, 0)

            def front(n, b):
                dve.wait_ge(s_full, NB * n + b + 1)
                nc.vector.tensor_reduce(mx[:], s_ps[:], AX.X, ALU.max).then_inc(link, 1)
                dve.wait_ge(link, NB * n + b + 1)
                nc.vector.tensor_tensor(sc[:, b % 3], s_ps[:], wide(mx), ALU.subtract).then_inc(shifted, 1)

            def total(n, b):
                dve.wait_ge(ex_done, NB * n + b + 1)
                nc.vector.tensor_reduce(den[:, b % 2], sc[:, b % 3], AX.X, ALU.add).then_inc(summed, 1)
                dve.wait_ge(summed, NB * n + b + 1)
                if b >= 2:
                    dve.wait_ge(probs_ready, NB * n + b - 1)
                nc.vector.reciprocal(rden[:, b % 2], den[:, b % 2]).then_inc(rden_ready, 1)

            with dve.Fori(0, NS // 2) as jj:
                for k in range(2):
                    n = 2 * jj + k
                    norm.dve(dve, n + 1, 1 - k, first_tile(jj, k, True))
                    dve.wait_ge(full, RING * n + VI + 1)
                    nc.vector.tensor_tensor(v[:], ring[VI % 2][:].rearrange("p (t c) -> p t c", t=ST),
                                            v_bias[:].unsqueeze(1).broadcast_to([P, ST, KV2]), ALU.add)\
                        .then_inc(dve_free, 1)
                    norm.dve_low(dve, n + 1, 1 - k)
                    front(n, 0)
                    dve.wait_ge(v_moved, 32 * n + 32)
                    for rows, r in ((slice(0, S), 0), (slice(S, P), 1)):
                        for own in (0, 1):
                            src = (v if own == r else v_swap)[rows]
                            out = v_block[rows].rearrange("p (t r) c -> p t r c", r=2)[:, :, own, :]
                            last = nc.vector.tensor_tensor(out, src, v_mask[rows].unsqueeze(1).broadcast_to(
                                [S, ST, KV2]), ALU.mult)
                    last.then_inc(v_block_ready, 1)
                    for b in range(NB + 4):
                        if b + 1 < NB:
                            front(n, b + 1)
                        if b < NB:
                            total(n, b)
                        if b >= 5 and b % 2:
                            add(dve, n, b // 2 - 2, first_tile(jj, k, False))



QMAX = 127.0
ROUND = 1.5 * 2.0 ** 23


def quantized_phase(nc, env, d):
    with ExitStack() as ctx:
        sem = semaphores(nc, ctx, "f2_")
        sb = lambda n, shape, dt=F32: ctx.enter_context(nc.sbuf_tensor(f"f2_{n}", shape, dt))
        norm = StepNorm(nc, env, ctx, "f2", "plain")
        reps = sb("reps", [P, 4, D])
        GAMMA, BETA, B1, B3 = range(4)
        w_f = env.staged.tile[:, 0:2 * KC * D].rearrange("p (i c d) -> p i c d", i=2, c=KC)
        w_am = sb("w_am", [P, 2 * KC])
        w_s = sb("w_s", [P, 2 * KC])
        w_inv = sb("w_inv", [P, 2 * KC])
        w_q = sb("w_q", [P, 2, KC, D], BF16)
        w_t = sb("w_t", [P, 2, KC, D], BF16)
        w_srow = sb("w_srow", [P, 2, D])
        h = sb("h", [P, 2, ST, D])
        am = sb("am", [P, 2, ST])
        s = sb("s", [P, 2, 2, ST])
        inv = sb("inv", [P, 2, ST])
        st2 = sb("st2", [P, ST, 6])
        mv2 = sb("mv2", [P, ST, 2])
        ve2 = sb("ve2", [P, ST])
        rstd2 = sb("rstd2", [P, ST])
        pace = sb("pace", [P, 1])
        qx = sb("qx", [P, 2, ST, D], BF16)
        qt = sb("qt", [P, 2, KC, W], BF16)
        o = sb("o", [P, 2, ST, D])
        pool_pace = sb("pool_pace", [P, 1])
        act_pace = sb("act_pace", [P, 1])
        ident16 = sb("ident16", [P, P], BF16)
        t_ps = [ctx.enter_context(nc.psum_tensor(f"f2_t{b}", [P, KC, P], BF16)) for b in range(2)]
        out_ps = [ctx.enter_context(nc.psum_tensor(f"f2_o{b}", [P, D], F32)) for b in range(2)]
        row_ps = [ctx.enter_context(nc.psum_tensor(f"f2_r{b}", [P, D], F32)) for b in range(2)]
        (in_, id_set, wl, w_rounded, w_q_ready, w_t_full, w_t_ready, row_full, row_ready) = map(sem, (
            "in", "id", "wl", "w_rounded", "w_q", "w_t_full", "w_t", "row_full", "row"))
        (l_front, ve_ready, r2_ready, fr_rounded, mid_rounded, fr_q, mid_q, t_full, qt_ready, o_full, h1,
         h1b, h1g, l_mid, oo, oob) = map(sem, (
             "l_front", "ve", "r2", "fr_rounded", "mid_rounded", "fr_q", "mid_q", "t_full", "qt", "o_full",
             "h1", "h1b", "h1g", "l_mid", "oo", "oob"))
        added, scaled = map(sem, ("added", "scaled"))
        block = ctx.enter_context(nc.Block())

        @block.sync
        def _(sp):
            sp.dma_start(reps[:], d["f2_reps"]).then_inc(in_, 16)
            sp.wait_ge(w_q_ready, 2 * KC)
            env.staged.load_next(sp)
            sp.wait_ge(in_, 16)

        @block.gpsimd
        def _(pool):
            norm.pool_start(pool)
            nc.gpsimd.tensor_copy(ident16[:], env.ident[:]).then_inc(id_set, 1)

            def front(n):
                norm.pool(pool, n)
                pool.wait_ge(ve_ready, n + 1)
                nc.gpsimd.tensor_tensor(rstd2[:], ve2[:], norm.minus_half[:], ALU.pow).then_inc(r2_ready, 1)

            def scale_and_shift(i, bias, t, link, done):
                tile = o[:, i, t, :]
                nc.gpsimd.tensor_tensor(tile, tile, w_srow[:, i, :], ALU.mult).then_inc(scaled, 1)
                pool.wait_ge(scaled, link)
                nc.gpsimd.tensor_tensor(tile, tile, reps[:, bias, :], ALU.add).then_inc(done, 1)

            nc.gpsimd.memset(pool_pace[:], 0.0).then_inc(added, 1)
            front(0)
            pool.wait_ge(in_, 16)
            pool.wait_ge(row_ready, 3)
            def last_product(n):
                for t in range(ST):
                    pool.wait_ge(oo, ST * n + t + 2)
                    link = ST * (2 * n + 1) + (ST if n < NS - 1 else 0) + t + 1
                    scale_and_shift(1, B3, t, link, oob)
                    pool.wait_ge(oob, ST * n + t + 1)
                    tile = env.x[:, n * ST + t, :]
                    nc.gpsimd.tensor_tensor(tile, tile, o[:, 1, t, :], ALU.add).then_inc(added, 1)

            for n in range(NS):
                front(n + 1)
                for t in range(ST):
                    pool.wait_ge(h1, ST * n + t + 1)
                    scale_and_shift(0, B1, t, ST * max(2 * n - 1, 0) + t + 1, h1b)
                if n:
                    last_product(n - 1)
            last_product(NS - 1)

        @block.tensor
        def _(pe):
            pe.wait_ge(id_set, 1)
            for i in range(2 * KC):
                pe.wait_ge(w_q_ready, i + 1)
                if i >= 2:
                    pe.wait_ge(w_t_ready, i - 1)
                for c in range(KC):
                    last = nc.tensor.transpose(t_ps[i % 2][:, c, :], w_q[:, i // KC, i % KC, c * P:(c + 1) * P],
                                               ident16[:])
                last.then_inc(w_t_full, 1)
            for i in range(2):
                for m in range(KC):
                    at = i * KC + m
                    last = nc.tensor.matmul(row_ps[i][:, m * P:(m + 1) * P], w_s[:, at:at + 1].broadcast_to([P, P]),
                                            env.ident[:], start=True, stop=True)
                last.then_inc(row_full, 1)
            pe.wait_ge(w_t_ready, 2 * KC)

            def product(n, i, par):
                at = 2 * ST * n + ST * i
                for t in range(ST):
                    pe.wait_ge(fr_q if i == 0 else mid_q, ST * n + t + 1)
                    if t >= 2:
                        pe.wait_ge(qt_ready, at + t - 1)
                    for c in range(KC):
                        last = nc.tensor.transpose(t_ps[t % 2][:, c, :], qx[:, i, t, c * P:(c + 1) * P], ident16[:])
                    last.then_inc(t_full, 1)
                for t in range(ST):
                    pe.wait_ge(qt_ready, at + t + 1)
                    if t >= 2:
                        pe.wait_ge((h1, oo)[i], ST * n + t - 1 + i)
                    else:
                        pe.wait_ge((oo, h1)[i], ST * n + (ST if i else 1))
                    for c in range(KC):
                        last = nc.tensor.matmul(out_ps[t % 2][:], qt[:, i, c, t * P:(t + 1) * P], w_t[:, i, c, :],
                                                start=(c == 0), stop=(c == KC - 1))
                    last.then_inc(o_full, 1)

            with pe.Fori(0, NS // 2) as j:
                for k in range(2):
                    product(2 * j + k, 0, k)
                    product(2 * j + k, 1, k)

        @block.scalar
        def _(act):
            for i in range(2 * KC):
                act.wait_ge(w_rounded, i + 1)
                nc.scalar.activation(w_q[:, i // KC, i % KC, :], w_f[:, i // KC, i % KC, :], ACT.Copy,
                                     bias=-ROUND).then_inc(w_q_ready, 1)
            for i in range(2 * KC):
                act.wait_ge(w_t_full, i + 1)
                nc.scalar.activation(w_t[:, i // KC, :, (i % KC) * P:(i % KC + 1) * P], t_ps[i % 2][:], ACT.Copy)\
                    .then_inc(w_t_ready, 1)

            def whole(n, i, t):
                act.wait_ge(fr_rounded if i == 0 else mid_rounded, ST * n + t + 1)
                nc.scalar.activation(qx[:, i, t, :], h[:, i, t, :], ACT.Copy, bias=-ROUND)\
                    .then_inc(fr_q if i == 0 else mid_q, 1)

            def turned(n, i):
                for t in range(ST):
                    act.wait_ge(t_full, 2 * ST * n + ST * i + t + 1)
                    nc.scalar.activation(qt[:, i, :, t * P:(t + 1) * P], t_ps[t % 2][:], ACT.Copy)\
                        .then_inc(qt_ready, 1)

            def product_out(n, i, par, done):
                for t in range(ST):
                    act.wait_ge(o_full, 2 * ST * n + ST * i + t + 1)
                    nc.scalar.activation(o[:, i, t, :], out_ps[t % 2][:], ACT.Copy, scale=s[:, i, par, t:t + 1])\
                        .then_inc(done, 1)

            nc.scalar.activation(act_pace[:], env.ones[:, 0:1], ACT.Copy).then_inc(oo, 1)
            for t in range(ST):
                whole(0, 0, t)
            with act.Fori(0, NS // 2) as j:
                for k in range(2):
                    n = 2 * j + k
                    turned(n, 0)
                    product_out(n, 0, k, h1)
                    for t in range(ST):
                        act.wait_ge(h1b, ST * n + t + 1)
                        nc.scalar.activation(h[:, 1, t, :], o[:, 0, t, :], ACT.Gelu).then_inc(h1g, 1)
                    for t in range(ST):
                        whole(n + 1, 0, t)
                    for t in range(ST):
                        whole(n, 1, t)
                    turned(n, 1)
                    act.wait_ge(added, ST * n + 1)
                    product_out(n, 1, k, oo)

        @block.vector
        def _(dve):
            def scales(am_ap, s_ap, inv_ap, chain, at):
                nc.vector.tensor_scalar(s_ap, am_ap, 1.0 / QMAX, 1e-8, ALU.mult, ALU.max).then_inc(chain, 1)
                dve.wait_ge(chain, at)
                nc.vector.reciprocal(inv_ap, s_ap).then_inc(chain, 1)
                dve.wait_ge(chain, at + 1)

            def rounded(tile, inv_col, chain, at, done):
                nc.vector.tensor_scalar(tile, tile, inv_col, QMAX, ALU.mult, ALU.min).then_inc(chain, 1)
                dve.wait_ge(chain, at)
                nc.vector.tensor_scalar(tile, tile, -QMAX, ROUND, ALU.max, ALU.add).then_inc(done, 1)

            FR = 7 + ST
            MID = 3 + ST

            def front(n, par, tile):
                at = FR * n
                norm.dve(dve, n, par, tile)
                dve.wait_ge(norm.tile_ready, ST * n + ST)
                for t in range(ST):
                    last = nc.vector.bn_stats(st2[:, t, :], norm.tiles[:, par, t, :])
                last.then_inc(l_front, 1)
                dve.wait_ge(l_front, at + 1)
                nc.vector.memset(pace[:], 0.0)
                for t in range(ST):
                    last = nc.vector.bn_aggr(mv2[:, t, :], st2[:, t, :])
                last.then_inc(l_front, 1)
                dve.wait_ge(l_front, at + 2)
                nc.vector.tensor_scalar(ve2[:], mv2[:, :, 1], EPS, None, ALU.add).then_inc(ve_ready, 1)
                if not (isinstance(n, int) and n == 0):
                    dve.wait_ge(fr_q, ST * n)
                for t in range(ST):
                    last = nc.vector.scalar_tensor_tensor(h[:, 0, t, :], norm.tiles[:, par, t, :], mv2[:, t, 0:1],
                                                          reps[:, GAMMA, :], ALU.subtract, ALU.mult)
                last.then_inc(l_front, 1)
                dve.wait_ge(l_front, at + 3)
                dve.wait_ge(r2_ready, n + 1)
                for t in range(ST):
                    last = nc.vector.scalar_tensor_tensor(h[:, 0, t, :], h[:, 0, t, :], rstd2[:, t:t + 1],
                                                          reps[:, BETA, :], ALU.mult, ALU.add)
                last.then_inc(l_front, 1)
                dve.wait_ge(l_front, at + 4)
                nc.vector.tensor_reduce(am[:, 0, :], h[:, 0], AX.X, ALU.max, apply_absolute_value=True)\
                    .then_inc(l_front, 1)
                dve.wait_ge(l_front, at + 5)
                scales(am[:, 0, :], s[:, 0, par, :], inv[:, 0, :], l_front, at + 6)
                for t in range(ST):
                    nc.vector.tensor_scalar(h[:, 0, t, :], h[:, 0, t, :], inv[:, 0, t:t + 1], QMAX, ALU.mult,
                                            ALU.min).then_inc(l_front, 1)
                for t in range(ST):
                    dve.wait_ge(l_front, at + 7 + t + 1)
                    nc.vector.tensor_scalar(h[:, 0, t, :], h[:, 0, t, :], -QMAX, ROUND, ALU.max, ALU.add)\
                        .then_inc(fr_rounded, 1)

            dve.wait_ge(env.staged.loaded["f2"], 16)
            nc.vector.tensor_reduce(w_am[:], w_f.rearrange("p i c d -> p (i c) d"), AX.X, ALU.max,
                                    apply_absolute_value=True).then_inc(wl, 1)
            dve.wait_ge(wl, 1)
            scales(w_am[:], w_s[:], w_inv[:], wl, 2)
            for i in range(2 * KC):
                rounded(w_f[:, i // KC, i % KC, :], w_inv[:, i:i + 1], wl, 4 + i, w_rounded)
            dve.wait_ge(in_, 16)
            front(0, 0, 0)
            dve.wait_ge(row_full, 1)
            nc.vector.tensor_copy(w_srow[:, 0, :], row_ps[0][:]).then_inc(row_ready, 1)
            dve.wait_ge(row_full, 2)
            nc.vector.tensor_scalar(w_srow[:, 1, :], row_ps[1][:], env.tg[:, 6:7], None, ALU.mult)\
                .then_inc(row_ready, 1)
            nc.vector.tensor_scalar(reps[:, B3, :], reps[:, B3, :], env.tg[:, 6:7], None, ALU.mult)\
                .then_inc(row_ready, 1)
            dve.wait_ge(row_ready, 3)
            with dve.Fori(0, NS // 2) as j:
                for k in range(2):
                    n = 2 * j + k
                    front(n + 1, 1 - k, first_tile(j, k, True))
                    dve.wait_ge(h1g, ST * n + ST)
                    nc.vector.tensor_reduce(am[:, 1, :], h[:, 1], AX.X, ALU.max, apply_absolute_value=True)\
                        .then_inc(l_mid, 1)
                    dve.wait_ge(l_mid, MID * n + 1)
                    scales(am[:, 1, :], s[:, 1, k, :], inv[:, 1, :], l_mid, MID * n + 2)
                    for t in range(ST):
                        nc.vector.tensor_scalar(h[:, 1, t, :], h[:, 1, t, :], inv[:, 1, t:t + 1], QMAX, ALU.mult,
                                                ALU.min).then_inc(l_mid, 1)
                    for t in range(ST):
                        dve.wait_ge(l_mid, MID * n + 3 + t + 1)
                        nc.vector.tensor_scalar(h[:, 1, t, :], h[:, 1, t, :], -QMAX, ROUND, ALU.max, ALU.add)\
                            .then_inc(mid_rounded, 1)



H3, HD3 = 8, 64
M3 = H3 * HD3 // P
NC = D // P


def attention3_phase(nc, env, d):
    with ExitStack() as ctx:
        sem = semaphores(nc, ctx, "a3_")
        sb = lambda n, shape, dt=F32: ctx.enter_context(nc.sbuf_tensor(f"a3_{n}", shape, dt))
        ps = lambda n, shape: ctx.enter_context(nc.psum_tensor(f"a3_{n}", shape, F32))
        w_f = env.staged.tile[:, 0:2 * H3 * HD3].rearrange("p (i n) -> p i n", i=2)
        w = [sb(f"w{part}", [P, 2, H3 * HD3], BF16) for part in range(2)]
        wv = sb("wv", [P, M3, P])
        wo = sb("wo", [P, M3, HD3])
        u_t = sb("u_t", [P, H3, HD3])
        cols = sb("cols", [P, 2])
        gain = sb("gain", [P, 1])
        half_ones = sb("half_ones", [P, 2])
        minus_half = sb("minus_half", [P, 2 * NC])
        stats = sb("stats", [P, 6])
        mv = sb("mv", [P, 2])
        pace = sb("pace", [P, 1])
        var_eps = sb("var_eps", [P, 1])
        rstd = sb("rstd", [P, 1])
        rows_f = sb("rows_f", [P, 2, 2, D])
        rows = [sb(f"rows{part}", [P, 2, 2, D], BF16) for part in range(2)]
        nmax = sb("nmax", [P, 2, M3])
        ksum = sb("ksum", [P, 2, M3])
        rksum = sb("rksum", [P, M3])
        kexp = sb("kexp", [P, M3, D])
        kt = [sb(f"kt{part}", [P, NC, M3 * P], BF16) for part in range(2)]
        g = sb("g", [P, H3 * HD3])
        m_t = sb("m_t", [P, M3, HD3])
        qmax = sb("qmax", [P, NC, H3])
        qe = sb("qe", [P, 2, NC, H3 * HD3])
        qsum = sb("qsum", [P, NC * H3])
        rqsum = sb("rqsum", [P, NC * H3])
        qt = sb("qt", [P, M3, D])
        u = sb("u", [P, 2, D])
        sq = sb("sq", [P, 2, D])
        ssm = sb("ssm", [P, 2 * NC])
        rn = sb("rn", [P, 2 * NC])
        rn_rows = sb("rn_rows", [P, 2 * NC, HD3])
        vec = sb("vec", [P, D])
        proj = [ps(f"proj{b}", [P, 512]) for b in range(4)]
        turn = [ps(f"turn{b}", [P, 512]) for b in range(2)]
        small = ps("small", [P, 512])
        o_ps = ps("o", [P, D])
        in_, c_in0, c_in1 = map(sem, ("in", "c_in0", "c_in1"))
        c_in = (c_in0, c_in1)
        const_set, w_high, w_ready, u_full, u_ready, gain_ready = map(
            sem, ("const", "w_high", "w_ready", "u_full", "u_ready", "gain"))
        ln_link, var_ready, rstd_ready, xn_ready, split_link, c_ready, x_ready = map(
            sem, ("ln_link", "var", "rstd", "xn", "split_link", "c_ready", "x_ready"))
        (proj_full, kmax_ready, kexp_ready, q_link, q_free, qe_done, sum_link, qr_ready, qp_ready) = map(sem, (
            "proj_full", "kmax", "kexp_ready", "q_link", "q_free", "qe", "sum_link", "qr", "qp"))
        (kt_full, kt_high, kt_ready, qt_full, qt_ready, g_full, g_ready, m_full, rk_done, m_ready, o_full) = map(sem, (
            "kt_full", "kt_high", "kt_ready", "qt_full", "qt_ready", "g_full", "g_ready", "m_full", "rk", "m_ready",
            "o_full"))
        out_ready, ss_full, ss_read, rn_link, rn_ready, rep_full, rep_read, x_done = map(
            sem, ("out", "ss_full", "ss_read", "rn_link", "rn", "rep_full", "rep_read", "x_done"))
        LOADS = 4
        CTX, XN = 0, 1

        class At:

            def __init__(self, j, c):
                self.b, self.c, self.j = 4 * j + c, c, j
                self.first = isinstance(j, int) and self.b == 0
                self.second = isinstance(j, int) and self.b == 1
                self.old = not isinstance(j, int) or self.b >= 4

            def tile(self, back=0):
                return 2 * self.j + (self.c - back) // 2

        def run(eng, steps):
            for c in range(4):
                steps(At(0, c), True, c >= 1, c == 3, False, c % 2 == 0, False, False)
            with eng.Fori(1, B // 4 - 1) as j:
                for c in range(4):
                    steps(At(j, c), True, True, c % 2 == 1, c % 2 == 0, c % 2 == 0, c % 2 == 0, c % 2 == 1)
            for c in range(4):
                steps(At(B // 4 - 1, c), True, True, c % 2 == 1, c % 2 == 0, c == 0, c % 2 == 0, c % 2 == 1)
            steps(At(B // 4, 0), False, True, False, True, False, True, False)
            steps(At(B // 4, 1), False, False, True, False, False, False, True)
            steps(At(B // 4, 2), False, False, False, True, False, True, False)
            steps(At(B // 4, 3), False, False, False, False, False, False, True)

        block = ctx.enter_context(nc.Block())

        @block.sync
        def _(sp):
            for tile, name in ((wv, "a3_wv"), (wo, "a3_wo"), (cols, "a3_cols"),
                               (half_ones, "half_ones")):
                sp.dma_start(tile[:], d[name]).then_inc(in_, 16)
            rows_d = d["ctx"].rearrange("(t p) n -> p t n", p=P)
            for k in range(2):
                sp.dma_start(rows_f[:, k, CTX, :], rows_d[:, k, :]).then_inc(c_in[k], 16)
            with sp.Fori(0, NT // 2 - 1) as j:
                for k in range(2):
                    sp.wait_ge(c_ready, 2 * j + k + 1)
                    sp.dma_start(rows_f[:, k, CTX, :], rows_d[:, bass.ds(2 * j + k + 2, 1), :].rearrange(
                        "p t n -> p (t n)")).then_inc(c_in[k], 16)
            for k in range(2):
                sp.wait_ge(c_in[k], 16 * NT // 2)

        @block.gpsimd
        def _(pool):
            nc.gpsimd.memset(minus_half[:], -0.5).then_inc(const_set, 1)
            pool.wait_ge(const_set, 1)
            pool.wait_ge(in_, 16 * LOADS)
            pool.wait_ge(env.staged.loaded["a3"], 16)
            for i in range(2):
                nc.gpsimd.tensor_copy(w[0][:, i, :], w_f[:, i, :]).then_inc(w_high, 1)
                pool.wait_ge(w_high, i + 1)
                nc.gpsimd.tensor_tensor(w[1][:, i, :], w_f[:, i, :], w[0][:, i, :], ALU.subtract).then_inc(w_ready, 1)

            def norm(t):
                pool.wait_ge(var_ready, t + 1)
                nc.gpsimd.tensor_tensor(rstd[:], var_eps[:], minus_half[:, 0:1], ALU.pow).then_inc(rstd_ready, 1)

            def split(t, k, which, ready, value, source_ready):
                pool.wait_ge(source_ready, value)
                if not (isinstance(t, int) and t < 2):
                    pool.wait_ge(proj_full, 16 * (t - 1))
                nc.gpsimd.tensor_tensor(rows[0][:, k, which, :], rows_f[:, k, which, :], ones_row(), ALU.mult)\
                    .then_inc(split_link, 1)
                pool.wait_ge(split_link, 2 * t + (1 if which == CTX else 2))
                nc.gpsimd.tensor_tensor(rows[1][:, k, which, :], rows_f[:, k, which, :], rows[0][:, k, which, :],
                                        ALU.subtract).then_inc(ready, 1)

            ones_row = lambda: env.ones[:, 0:1].broadcast_to([P, D])

            def split_tile(t, k, j):
                split(t, k, CTX, c_ready, 16 * (j + 1), c_in[k])
                split(t, k, XN, x_ready, t + 1, xn_ready)

            norm(0)
            split_tile(0, 0, 0)

            def steps(at, main, prev, ss, rep, ahead, read_ss, read_rep):
                b, c = at.b, at.c
                t = at.tile()
                if prev:
                    pool.wait_ge(qr_ready, b)
                    e = qe[:, (c - 1) % 2].rearrange("p n (h d) -> p (n h) d", h=H3)
                    nc.gpsimd.tensor_tensor(e, e, rqsum[:].unsqueeze(2).broadcast_to([P, NC * H3, HD3]), ALU.mult)\
                        .then_inc(qp_ready, 1)
                if read_ss:
                    t4 = at.tile(4)
                    pool.wait_ge(ss_read, t4 + 1)
                    nc.gpsimd.tensor_tensor(rn[:], ssm[:], minus_half[:], ALU.pow).then_inc(rn_link, 1)
                    pool.wait_ge(rn_link, t4 + 1)
                    wide = [P, 2 * NC, HD3]
                    nc.gpsimd.tensor_tensor(rn_rows[:], rn[:].unsqueeze(2).broadcast_to(wide),
                                            env.ones[:, 0:1].unsqueeze(2).broadcast_to(wide), ALU.mult)\
                        .then_inc(rn_ready, 1)
                if read_rep:
                    t5 = at.tile(5)
                    pool.wait_ge(rep_read, t5 + 1)
                    nc.gpsimd.tensor_tensor(env.x[:, t5, :], env.x[:, t5, :], vec[:], ALU.add).then_inc(x_done, 1)
                if ahead:
                    norm(t + 1)
                    split_tile(t + 1, (c // 2 + 1) % 2, at.j + c // 2)

            run(pool, steps)

        @block.tensor
        def _(pe):
            pe.wait_ge(in_, 16 * LOADS)
            for h in range(H3):
                r = slice((h % 2) * HD3, (h % 2 + 1) * HD3)
                last = nc.tensor.matmul(turn[h % 2][:, (h // 2) * HD3:(h // 2 + 1) * HD3], wv[r, h // 2, :],
                                        wo[r, h // 2, :], start=True, stop=True)
            last.then_inc(u_full, 1)
            pe.wait_ge(u_ready, 2)
            pe.wait_ge(w_ready, 2)

            def steps(at, main, prev, ss, rep, ahead, read_ss, read_rep):
                b, c = at.b, at.c
                k, r = c // 2, slice((c % 2) * S, (c % 2 + 1) * S)
                t = at.tile()
                first = at.first
                if main:
                    if c % 2 == 0:
                        pe.wait_ge(c_ready, t + 1)
                    for m in range(M3):
                        if not first:
                            pe.wait_ge(q_free, 4 * (b - 1) + m + 1)
                        for i, (a, bb) in enumerate(PASSES):
                            mm = nc.tensor.matmul(proj[m][:], w[a][r, 0, m * P:(m + 1) * P], rows[bb][r, k, CTX, :],
                                                  start=(i == 0), stop=(i == 2))
                        mm.then_inc(proj_full, 1)
                    if c % 2 == 0:
                        pe.wait_ge(x_ready, t + 1)
                    for n in range(NC):
                        pe.wait_ge(kexp_ready, 4 * b + n + 1)
                        for i, (a, bb) in enumerate(PASSES):
                            mm = nc.tensor.matmul(proj[n][:], rows[a][r, k, XN, n * P:(n + 1) * P], w[bb][r, 1, :],
                                                  start=(i == 0), stop=(i == 2))
                        mm.then_inc(proj_full, 1)
                if prev:
                    if at.old:
                        pe.wait_ge(rep_read if c % 2 else ss_read, at.tile(5 if c % 2 else 4) + 1)
                    elif not at.second:
                        pe.wait_ge(m_ready, 2 * (b - 1))
                    pe.wait_ge(kt_ready, 4 * b)
                    for n in range(NC):
                        for i, (a, bb) in enumerate(PASSES):
                            mm = nc.tensor.matmul(small[:], env.ct[a][:, n, bass.ds(at.tile(1) * P, P)],
                                                  kt[bb][:, n, :], start=(n == 0 and i == 0),
                                                  stop=(n == NC - 1 and i == 2))
                    mm.then_inc(g_full, 1)
                if prev:
                    pr = slice(((c - 1) % 2) * S, ((c - 1) % 2 + 1) * S)
                    pe.wait_ge(g_ready, b)
                    for m in range(M3):
                        mm = nc.tensor.matmul(small[:, m * P:(m + 1) * P], g[pr, m * P:(m + 1) * P],
                                              u_t[pr, 2 * m:2 * m + 2, :].rearrange("p h o -> p (h o)"),
                                              start=True, stop=True)
                    mm.then_inc(m_full, 1)
                    for m in range(M3):
                        if m == 0:
                            pe.wait_ge(qp_ready, b)
                        if m >= 2:
                            pe.wait_ge(qt_ready, 4 * (b - 1) + m - 1)
                        for n in range(NC):
                            mm = nc.tensor.transpose(turn[m % 2][:, n * P:(n + 1) * P],
                                                     qe[:, (c - 1) % 2, n, m * P:(m + 1) * P], env.ident[:])
                        mm.then_inc(qt_full, 1)
                def turn_keys(which):
                    for n in which:
                        if n >= 2:
                            pe.wait_ge(kt_ready, 4 * b + n - 1)
                        elif prev:
                            pe.wait_ge(qt_ready, 4 * (b - 1) + n + 3)
                        for m in range(M3):
                            last = nc.tensor.transpose(turn[n % 2][:, m * P:(m + 1) * P],
                                                       kexp[:, m, n * P:(n + 1) * P], env.ident[:])
                        last.then_inc(kt_full, 1)

                if main:
                    turn_keys(range(0, 2))
                if prev:
                    if (c - 1) % 2 == 0 and not at.second:
                        pe.wait_ge(out_ready, at.tile(1))
                    pe.wait_ge(qt_ready, 4 * (b - 1) + 4)
                    pe.wait_ge(m_ready, 2 * b)
                    for m in range(M3):
                        mm = nc.tensor.matmul(o_ps[pr, :], m_t[:, m, :], qt[:, m, :], start=(m == 0),
                                              stop=(m == M3 - 1))
                    mm.then_inc(o_full, 1)
                if main:
                    turn_keys(range(2, NC))
                if (ss or rep) and (main or prev):
                    pe.wait_ge(m_ready, 2 * b)
                if ss:
                    t3 = at.tile(3)
                    pe.wait_ge(out_ready, t3 + 1)
                    if not main:
                        pe.wait_ge(rep_read, t3)
                    for n in range(NC):
                        mm = nc.tensor.matmul(small[:, 2 * n:2 * n + 2], sq[:, ((c - 3) // 2) % 2, n * P:(n + 1) * P],
                                              half_ones[:], start=True, stop=True)
                    mm.then_inc(ss_full, 1)
                if rep:
                    t4 = at.tile(4)
                    pe.wait_ge(rn_ready, t4 + 1)
                    for n in range(NC):
                        mm = nc.tensor.matmul(small[:, n * P:(n + 1) * P],
                                              rn_rows[:, 2 * n:2 * n + 2, :].rearrange("p s o -> p (s o)"),
                                              env.ident[:], start=True, stop=True)
                    mm.then_inc(rep_full, 1)

            run(pe, steps)

        @block.scalar
        def _(act):
            act.wait_ge(in_, 16 * LOADS)

            def steps(at, main, prev, ss, rep, ahead, read_ss, read_rep):
                b, c = at.b, at.c
                if main:
                    for m in range(M3):
                        act.wait_ge(kmax_ready, 4 * b + m + 1)
                        nc.scalar.activation(kexp[:, m, :], proj[m][:], ACT.Exp, bias=nmax[:, c % 2, m:m + 1],
                                             accum_out=ksum[:, c % 2, m:m + 1]).then_inc(kexp_ready, 1)
                if prev:
                    act.wait_ge(g_full, b)
                    pr = slice(((c - 1) % 2) * S, ((c - 1) % 2 + 1) * S)
                    nc.scalar.activation(g[pr, :], small[pr, :], ACT.Copy).then_inc(g_ready, 1)
                    for m in range(M3):
                        act.wait_ge(qt_full, 4 * (b - 1) + m + 1)
                        nc.scalar.activation(qt[:, m, :], turn[m % 2][:], ACT.Copy).then_inc(qt_ready, 1)
                if main:
                    for n in range(NC):
                        act.wait_ge(kt_full, 4 * b + n + 1)
                        nc.scalar.activation(kt[0][:, n, :], turn[n % 2][:], ACT.Copy).then_inc(kt_high, 1)
                    for n in range(NC):
                        act.wait_ge(q_free, 4 * b + n + 1)
                        nc.scalar.activation(qe[:, c % 2, n, :], qe[:, c % 2, n, :], ACT.Exp).then_inc(qe_done, 1)
                if prev and (c - 1) % 2 == 1:
                    act.wait_ge(o_full, b)
                    k = ((c - 1) // 2) % 2
                    nc.scalar.activation(u[:, k, :], o_ps[:], ACT.Identity, bias=cols[:, 0:1])
                    nc.scalar.activation(sq[:, k, :], o_ps[:], ACT.Square, bias=cols[:, 0:1]).then_inc(out_ready, 1)

            run(act, steps)

        @block.vector
        def _(dve):
            dve.wait_ge(in_, 16 * LOADS)
            nc.vector.tensor_scalar(gain[:], cols[:, 1:2], env.tg[:, 3:4], float(np.sqrt(S)), ALU.mult, ALU.mult)\
                .then_inc(gain_ready, 1)

            def norm(t, k):
                nc.vector.bn_stats(stats[:], env.x[:, t, :]).then_inc(ln_link, 1)
                dve.wait_ge(ln_link, 2 * t + 1)
                nc.vector.memset(pace[:], 0.0)
                nc.vector.bn_aggr(mv[:], stats[:]).then_inc(ln_link, 1)
                dve.wait_ge(ln_link, 2 * t + 2)
                nc.vector.tensor_scalar(var_eps[:], mv[:, 1:2], EPS, None, ALU.add).then_inc(var_ready, 1)
                if not (isinstance(t, int) and t < 2):
                    dve.wait_ge(x_ready, t - 1)
                dve.wait_ge(rstd_ready, t + 1)
                nc.vector.tensor_scalar(rows_f[:, k, XN, :], env.x[:, t, :], mv[:, 0:1], rstd[:, 0:1],
                                        ALU.subtract, ALU.mult).then_inc(xn_ready, 1)

            norm(0, 0)
            dve.wait_ge(u_full, 1)
            for hh in range(2):
                nc.vector.tensor_copy(u_t[:].rearrange("p (m two) o -> p m two o", two=2)[:, :, hh, :],
                                      turn[hh][:, 0:M3 * HD3].rearrange("p (m o) -> p m o", m=M3)).then_inc(u_ready, 1)

            def steps(at, main, prev, ss, rep, ahead, read_ss, read_rep):
                b, c = at.b, at.c
                t = at.tile()
                if main:
                    for m in range(M3):
                        dve.wait_ge(proj_full, 8 * b + m + 1)
                        nc.vector.tensor_reduce(nmax[:, c % 2, m:m + 1], proj[m][:], AX.X, ALU.max, negate=True)\
                            .then_inc(kmax_ready, 1)
                if read_ss:
                    dve.wait_ge(ss_full, at.tile(4) + 1)
                    nc.vector.tensor_scalar(ssm[:], small[:, 0:2 * NC], 1e-24, None, ALU.max).then_inc(ss_read, 1)
                if read_rep:
                    dve.wait_ge(rep_full, at.tile(5) + 1)
                    nc.vector.scalar_tensor_tensor(vec[:], small[:], gain[:, 0:1], u[:, ((c - 5) // 2) % 2, :],
                                                   ALU.mult, ALU.mult).then_inc(rep_read, 1)
                if prev:
                    dve.wait_ge(qe_done, 4 * b)
                    nc.vector.tensor_reduce(qsum[:], qe[:, (c - 1) % 2].rearrange("p n (h d) -> p (n h) d", h=H3),
                                            AX.X, ALU.add).then_inc(sum_link, 1)
                    dve.wait_ge(sum_link, b)
                    if not at.second:
                        dve.wait_ge(qp_ready, b - 1)
                    nc.vector.reciprocal(rqsum[:], qsum[:]).then_inc(qr_ready, 1)
                if main:
                    for n in range(NC):
                        dve.wait_ge(proj_full, 8 * b + 4 + n + 1)
                        by_head = proj[n][:].rearrange("p (h d) -> p h d", h=H3)
                        nc.vector.tensor_reduce(qmax[:, n, :], by_head, AX.X, ALU.max).then_inc(q_link, 1)
                        dve.wait_ge(q_link, 4 * b + n + 1)
                        nc.vector.tensor_tensor(qe[:, c % 2, n, :].rearrange("p (h d) -> p h d", h=H3), by_head,
                                                qmax[:, n, :].unsqueeze(2).broadcast_to([P, H3, HD3]), ALU.subtract)\
                            .then_inc(q_free, 1)
                    if ahead:
                        norm(t + 1, (c // 2 + 1) % 2)
                if prev:
                    dve.wait_ge(kexp_ready, 4 * b)
                    nc.vector.reciprocal(rksum[:], ksum[:, (c - 1) % 2, :]).then_inc(rk_done, 1)
                    dve.wait_ge(rk_done, b)
                    dve.wait_ge(m_full, b)
                    for hh in range(2):
                        rr = slice(hh * HD3, (hh + 1) * HD3)
                        nc.vector.scalar_tensor_tensor(
                            m_t[rr], small[rr, :].rearrange("p (m two o) -> p m two o", m=M3, two=2)[:, :, hh, :],
                            float(HD3) ** -0.5, rksum[rr].unsqueeze(2).broadcast_to([HD3, M3, HD3]),
                            ALU.mult, ALU.mult).then_inc(m_ready, 1)
                if main:
                    for n in range(NC):
                        dve.wait_ge(kt_high, 4 * b + n + 1)
                        nc.vector.tensor_tensor(kt[1][:, n, :], turn[n % 2][:], kt[0][:, n, :], ALU.subtract)\
                            .then_inc(kt_ready, 1)
            run(dve, steps)



I3 = 1792
C3 = I3 // P
UNITS = 3 * C3
CH3 = 3 * D


def gated_phase(nc, env, d):
    with ExitStack() as ctx:
        sem = semaphores(nc, ctx, "f3_")
        sb = lambda n, shape, dt=F32: ctx.enter_context(nc.sbuf_tensor(f"f3_{n}", shape, dt))
        ps = lambda n, shape: ctx.enter_context(nc.psum_tensor(f"f3_{n}", shape, F32))
        norm = StepNorm(nc, env, ctx, "f3", "split")
        w = [sb(f"w{part}", [P, C3 * CH3], BF16) for part in range(2)]
        w_int = sb("w_int", [P, 2, 3, D], I32)
        zeros = sb("zeros", [P, D], I32)
        rows_f = sb("rows_f", [P, 2, D])
        rows = [sb(f"rows{i}", [P, 2, D], BF16) for i in range(3)]
        pick_f = sb("pick_f", [P, UNITS + 2])
        pick = sb("pick", [P, UNITS], BF16)
        centred = sb("centred", [P, D])
        w_f = sb("w_f", [P, 3, D])
        sg = sb("sg", [P, 2, W])
        hf = sb("hf", [P, 2, W])
        h = [sb(f"h{part}", [P, 2, W], BF16) for part in range(2)]
        gate_ps, up_ps = ps("gate", [P, W]), ps("up", [P, W])
        out_ps = [ps(f"out{t}", [P, D]) for t in range(ST)]
        zero_ps, scale_ps = (b[:].rearrange("p k c -> p (k c)") for b in norm.turned)
        w_in = [sem(f"w_in{k}") for k in range(2)]
        (rows_in, rows_ready, part_link, rep_full, sub_done, mul_done, w_high, w_ready) = map(sem, (
            "rows_in", "rows_ready", "part_link", "rep_full", "sub", "mul", "w_high", "w_ready"))
        (gate_full, up_full, sg_done, hf_done, h_high, h_ready, down_done, out_free) = map(sem, (
            "gate_full", "up_full", "sg", "hf", "h_high", "h_ready", "down_done", "out_free"))
        PARTS = 5
        block = ctx.enter_context(nc.Block())

        @block.sync
        def _(sp):
            sp.dma_start(zeros[:], d["f3_zeros"]).then_inc(rows_in, 16)
            sp.dma_start(rows_f[:, 1, :], d["f3_scales"]).then_inc(rows_in, 16)
            sp.dma_start(pick_f[:], d["f3_pick"]).then_inc(rows_in, 16)
            for k in range(2):
                sp.dma_start(w_int[:, k].rearrange("p u c -> p (u c)"), d["f3_w"][:, k, :]).then_inc(w_in[k], 16)
            with sp.Fori(1, C3 // 2) as i:
                for k in range(2):
                    sp.wait_ge(sub_done, 3 * (2 * i + k) - 3)
                    sp.dma_start(w_int[:, k].rearrange("p u c -> p (u c)"),
                                 d["f3_w"][:, bass.ds(2 * i + k, 1), :].rearrange("p c n -> p (c n)"))\
                        .then_inc(w_in[k], 16)
            for k in range(2):
                sp.wait_ge(w_in[k], 16 * C3 // 2)

        @block.gpsimd
        def _(pool):
            norm.pool_start(pool)
            norm.pool(pool, 0)
            norm.pool(pool, 1)

            def low(c, i):
                u = 3 * c + i
                pool.wait_ge(w_high, u + 1)
                cols = bass.ds(u * D, D)
                nc.gpsimd.tensor_tensor(w[1][:, cols], w_f[:, i, :], w[0][:, cols], ALU.subtract)\
                    .then_inc(w_ready, 1)

            with pool.Fori(0, C3) as c:
                for i in range(3):
                    low(c, i)
            for n in range(1, NS - 1):
                norm.pool(pool, n + 1)

        @block.tensor
        def _(pe):
            def repeat(c, i):
                u = 3 * c + i
                if not (isinstance(u, int) and u == 0):
                    pe.wait_ge(mul_done, u)
                for i_, bank in enumerate((zero_ps, scale_ps)):
                    mm = nc.tensor.matmul(bank, pick[:, bass.ds(u, 1)].broadcast_to([P, P]), rows[2][:, i_, :],
                                          start=True, stop=True)
                mm.then_inc(rep_full, 1)

            def product(bank, c, i, par, full):
                for k in range(KC):
                    for p, (a, b) in enumerate(PASSES):
                        mm = nc.tensor.matmul(bank[:], w[a][:, bass.ds(c * CH3 + i * D + k * P, P)],
                                              norm.xt[b][:, par, k, :], start=(k == 0 and p == 0),
                                              stop=(k == KC - 1 and p == 2))
                mm.then_inc(full, 1)

            def down(n, c, k, start, stop):
                if n == 0:
                    pe.wait_ge(w_ready, 3 * c + 3)
                pe.wait_ge(h_ready, C3 * n + c + 1)
                for t in range(ST):
                    for p, (a, b) in enumerate(PASSES):
                        mm = nc.tensor.matmul(out_ps[t][:], h[a][:, k, t * P:(t + 1) * P],
                                              w[b][:, bass.ds(c * CH3 + 2 * D, D)], start=(start and p == 0),
                                              stop=(stop and p == 2))
                mm.then_inc(down_done, 1)

            norm.pe(pe, 0)
            pe.wait_ge(part_link, PARTS)
            pe.wait_ge(norm.low_done, ST)
            for i in range(3):
                repeat(0, i)
            for n in range(NS):
                def chunk(c, k, last=False):
                    static = isinstance(c, int)
                    N = C3 * n + c
                    ahead = n == 0 and not last
                    if ahead:
                        repeat(c + 1, 0)
                    if n == 0:
                        pe.wait_ge(w_ready, 3 * c + 1)
                    if not (static and N == 0):
                        pe.wait_ge(sg_done, N)
                    product(gate_ps, c, 0, n % 2, gate_full)
                    if ahead:
                        repeat(c + 1, 1)
                    if n == 0:
                        pe.wait_ge(w_ready, 3 * c + 2)
                    if not (static and N == 0):
                        pe.wait_ge(hf_done, N)
                    product(up_ps, c, 1, n % 2, up_full)
                    if ahead:
                        repeat(c + 1, 2)
                    if static and c == 1 and n:
                        pe.wait_ge(out_free, ST * n)
                    if not (static and c == 0):
                        down(n, c - 1, 1 - k, static and c == 1, False)

                chunk(0, 0)
                chunk(1, 1)
                with pe.Fori(1, C3 // 2 - 1) as i:
                    for k in range(2):
                        chunk(2 * i + k, k)
                chunk(C3 - 2, 0)
                chunk(C3 - 1, 1, last=True)
                if n < NS - 1:
                    if n == 0:
                        pe.wait_ge(mul_done, UNITS)
                    norm.pe(pe, n + 1)
                down(n, C3 - 1, 1, False, True)
                if n < NS - 1:
                    pe.wait_ge(norm.low_done, ST * (n + 2))

        @block.scalar
        def _(act):
            def w_part(c, i):
                u = 3 * c + i
                act.wait_ge(mul_done, u + 1)
                nc.scalar.activation(w[0][:, bass.ds(u * D, D)], w_f[:, i, :], ACT.Copy).then_inc(w_high, 1)

            norm.act(act, 0, 0)
            for i in range(3):
                w_part(0, i)
            for n in range(NS):
                def chunk(c, k, last=False):
                    static = isinstance(c, int)
                    N = C3 * n + c
                    ahead = n == 0 and not last
                    if ahead:
                        w_part(c + 1, 0)
                    act.wait_ge(gate_full, N + 1)
                    if not (static and N < 2):
                        act.wait_ge(hf_done, N - 1)
                    nc.scalar.activation(sg[:, k, :], gate_ps[:], ACT.Silu).then_inc(sg_done, 1)
                    if ahead:
                        w_part(c + 1, 1)
                    act.wait_ge(hf_done, N + 1)
                    if not (static and N < 2):
                        act.wait_ge(down_done, N - 1)
                    nc.scalar.activation(h[0][:, k, :], hf[:, k, :], ACT.Copy).then_inc(h_high, 1)
                    if ahead:
                        w_part(c + 1, 2)

                chunk(0, 0)
                chunk(1, 1)
                with act.Fori(1, C3 // 2 - 1) as i:
                    for k in range(2):
                        chunk(2 * i + k, k)
                chunk(C3 - 2, 0)
                chunk(C3 - 1, 1, last=True)
                if n < NS - 1:
                    norm.act(act, n + 1, (n + 1) % 2)

        @block.vector
        def _(dve):
            def weights(c, i, k):
                u = 3 * c + i
                if i == 0:
                    dve.wait_ge(w_in[k], 16 if isinstance(c, int) and c < 2 else (c - k) * 8 + 16)
                dve.wait_ge(rep_full, u + 1)
                nc.vector.tensor_tensor(centred[:], w_int[:, k, i, :], zero_ps, ALU.subtract).then_inc(sub_done, 1)
                if not (isinstance(u, int) and u < 3):
                    dve.wait_ge(w_ready, u - 2)
                dve.wait_ge(sub_done, u + 1)
                nc.vector.tensor_tensor(w_f[:, i, :], centred[:], scale_ps, ALU.mult).then_inc(mul_done, 1)

            norm.dve(dve, 0, 0, 0)
            dve.wait_ge(rows_in, 48)
            nc.vector.tensor_copy(rows_f[:, 0, :], zeros[:]).then_inc(rows_ready, 1)
            nc.vector.tensor_copy(pick[:], pick_f[:, 0:UNITS]).then_inc(part_link, 1)
            dve.wait_ge(rows_ready, 1)
            for p in range(2):
                nc.vector.tensor_copy(rows[p][:], rows_f[:]).then_inc(part_link, 1)
                dve.wait_ge(part_link, 2 * p + 2)
                out = rows_f if p == 0 else rows[2]
                nc.vector.scalar_tensor_tensor(out[:], rows[p][:], pick_f[:, UNITS + p:UNITS + p + 1], rows_f[:],
                                               ALU.mult, ALU.add).then_inc(part_link, 1)
                dve.wait_ge(part_link, 2 * p + 3)
            norm.dve_low(dve, 0, 0)
            for i in range(3):
                weights(0, i, 0)
            for n in range(NS):
                def chunk(c, k, last=False):
                    static = isinstance(c, int)
                    N = C3 * n + c
                    ahead = n == 0 and not last
                    if ahead:
                        weights(c + 1, 0, 1 - k)
                        weights(c + 1, 1, 1 - k)
                    dve.wait_ge(up_full, N + 1)
                    dve.wait_ge(sg_done, N + 1)
                    if not (static and N < 2):
                        dve.wait_ge(h_ready, N - 1)
                    nc.vector.tensor_tensor(hf[:, k, :], sg[:, k, :], up_ps[:], ALU.mult).then_inc(hf_done, 1)
                    if ahead:
                        weights(c + 1, 2, 1 - k)
                    dve.wait_ge(h_high, N + 1)
                    nc.vector.tensor_tensor(h[1][:, k, :], hf[:, k, :], h[0][:, k, :], ALU.subtract)\
                        .then_inc(h_ready, 1)

                if n < NS - 1:
                    norm.dve(dve, n + 1, (n + 1) % 2, (n + 1) * ST)
                chunk(0, 0)
                chunk(1, 1)
                with dve.Fori(1, C3 // 2 - 1) as i:
                    for k in range(2):
                        chunk(2 * i + k, k)
                chunk(C3 - 2, 0)
                chunk(C3 - 1, 1, last=True)
                if n < NS - 1:
                    norm.dve_low(dve, n + 1, (n + 1) % 2)
                dve.wait_ge(down_done, C3 * (n + 1))
                for t in range(ST):
                    tile = env.x[:, n * ST + t, :]
                    nc.vector.scalar_tensor_tensor(tile, out_ps[t][:], env.tg[:, 7:8], tile,
                                                   ALU.mult, ALU.add).then_inc(out_free, 1)



PHASES = ("a0", "f0", "a1", "f1", "a2", "f2", "a3", "f3")


def build(nc, d, out, phases=PHASES):
    with ExitStack() as ctx:
        sb = lambda n, shape, dt: ctx.enter_context(nc.sbuf_tensor(n, shape, dt))
        env = Env()
        env.x = sb("x_res", [P, NT, D], F32)
        env.ident = sb("ident", [P, P], F32)
        env.ones = sb("ones", [P, P], F32)
        env.tg = sb("tanh_gates", [P, 8], F32)
        with ExitStack() as inner:
            high, low = (inner.enter_context(nc.sbuf_tensor(f"ctx_{n}", [P, KC, T], BF16)) for n in ("high", "low"))
            env.ct = env.cth, env.ctl = high, low
            env.staged = Staged(nc, inner, d, [p for p in ("a0", "a1", "a2", "f2", "a3") if p in phases])
            if "a0" in phases:
                with nc.sbuf_tensor("x_high", [P, KC, T], BF16) as high, \
                        nc.sbuf_tensor("x_low", [P, KC, T], BF16) as low:
                    env.xt = high, low
                    load_phase(nc, env, d, True)
                    attention0_phase(nc, env, d)
            else:
                load_phase(nc, env, d, False)
            if "f0" in phases:
                experts_phase(nc, env, d, "f0", 16, True, 4.0, 4)
            if "a1" in phases:
                attention1_phase(nc, env, d)
            if "f1" in phases:
                experts_phase(nc, env, d, "f1", 8, False, 2.0, 5)
            if "a2" in phases:
                attention2_phase(nc, env, d)
            if "f2" in phases:
                quantized_phase(nc, env, d)
            if "a3" in phases:
                attention3_phase(nc, env, d)
        if "f3" in phases:
            gated_phase(nc, env, d)
        store_phase(nc, env, out)


def store_phase(nc, env, out):
    with ExitStack() as ctx:
        stored = ctx.enter_context(nc.semaphore("stored"))
        block = ctx.enter_context(nc.Block())

        @block.sync
        def _(sp):
            sp.dma_start(out.rearrange("(t p) d -> p t d", p=P), env.x[:]).then_inc(stored, 16)
            sp.wait_ge(stored, 16)


def layouts(inputs, np):
    i = {k: np.asarray(v) for k, v in inputs.items()}
    out = {}
    out["x"] = i["x"].reshape(T, D)
    out["ctxT"] = i["ctx_4096"].reshape(T, D).T
    gates = np.concatenate([i["g_xattn"], i["g_ffn"]])
    out["gates"] = np.broadcast_to(gates, (P, 8))
    out["mask"] = i["mask_1x1xSxS2_ff0"].reshape(S, S)
    out["qk_norm_w"] = np.stack([i["L0_xattn_q_norm_w"], i["L0_xattn_k_norm_w"]], 1)
    wq = i["L0_xattn_Wq"].reshape(G0, QCOLS, KC, P).transpose(0, 3, 2, 1)
    wk = i["L0_xattn_Wk"].reshape(G0, HD0, KC, P).transpose(0, 3, 2, 1)
    wv = i["L0_xattn_Wv"].reshape(G0, HD0, KC, P).transpose(0, 3, 2, 1)
    wo = i["L0_xattn_Wo"].reshape(D, G0, H0, P).transpose(1, 3, 2, 0)
    w0 = np.concatenate([wq.reshape(G0, P, -1), np.concatenate([wk, wv], 3).reshape(G0, P, -1),
                         wo.reshape(G0, P, -1)], 2)
    out["w0"] = w0
    out["ctx"] = i["ctx_4096"].reshape(T, D)
    chunks = lambda w: w.reshape(KC, P, -1).transpose(1, 0, 2)
    out["f0_down"] = chunks(np.concatenate([i["L0_ffn_A"].reshape(-1, D), i["L0_ffn_router_w"]]).T)
    out["f0_up"] = i["L0_ffn_B"].transpose(0, 2, 1).reshape(-1, D)
    out["a1_w"] = np.concatenate([chunks(i[f"L1_xattn_{n}"].T).reshape(P, -1) for n in ("Wq", "Wk")], 1)
    out["a1_bias"] = np.stack([i["L1_xattn_bq"].reshape(KC, P).T, i["L1_xattn_bk"].reshape(KC, P).T], 1)
    out["f1_down"] = chunks(np.concatenate([i["L1_ffn_A"].reshape(-1, D), i["L1_ffn_Wr"]]).T)
    out["f1_up"] = np.concatenate([i["L1_ffn_Bm"].transpose(0, 2, 1).reshape(-1, D), i["L1_ffn_b"][None]])
    out["f1_dense"] = chunks(i["L1_ffn_W"].T)
    by_j = lambda w: w.reshape(-1, G2, J2, HD2).transpose(0, 2, 1, 3).reshape(-1, D)
    out["a2_w"] = chunks(np.concatenate([by_j(i["L2_xattn_Wq"]), i["L2_xattn_Wk"], i["L2_xattn_Wv"]], 1)).reshape(P, -1)
    out["a2_wo"] = i["L2_xattn_Wo"].reshape(G2, J2, HD2, D).transpose(0, 2, 1, 3).reshape(KV2, J2, D)
    out["a2_bo"] = i["L2_xattn_bo"][None]
    out["a2_qk_bias"] = np.concatenate([by_j(i["L2_xattn_bq"]).reshape(J2, KV2).T, i["L2_xattn_bk"][:, None]], 1)
    out["a2_v_bias"] = np.broadcast_to(i["L2_xattn_bv"], (P, KV2))
    row = np.arange(P)
    out["g_mask"] = (row[:, None] // HD2 == np.arange(G2)).astype(np.float32)
    out["v_mask"] = (row[:, None] // S == (row // HD2) % 2).astype(np.float32)
    out["f2_w"] = np.concatenate([i[f"L2_ffn_{n}"].reshape(KC, P, D).transpose(1, 0, 2).reshape(P, -1)
                                  for n in ("w1", "w3")], 1)
    out["f2_reps"] = np.stack([np.broadcast_to(i[f"L2_ffn_{n}"], (P, D)) for n in ("gamma", "beta", "b1", "b3")], 1)
    twice = lambda w: np.concatenate([w, w])
    out["a3_w"] = np.concatenate([twice(i["L3_xattn_Wk"].T), twice(i["L3_xattn_Wq"].T)], 1)
    wv3 = i["L3_xattn_Wv"].reshape(M3, P, S).transpose(1, 0, 2)
    out["a3_wv"] = np.concatenate([wv3, wv3], 2)
    out["a3_wo"] = i["L3_xattn_Wo"].reshape(S, M3, P).transpose(2, 1, 0)
    out["a3_cols"] = np.stack([twice(i["L3_xattn_bo"]), twice(i["L3_xattn_g"].reshape(S))], 1)
    out["half_ones"] = (row[:, None] // S == np.arange(2)).astype(np.float32)
    by_column = lambda w: w.reshape(KC, -1, C3, P).transpose(1, 2, 0, 3).reshape(-1, C3, D)
    units = lambda gate, up, down: np.stack([by_column(i[f"L3_ffn_{gate}"]), by_column(i[f"L3_ffn_{up}"]),
                                             i[f"L3_ffn_{down}"].reshape(C3, -1, D).transpose(1, 0, 2)], 2)
    out["f3_w"] = units("gate_w", "up_w", "down_w").reshape(P, C3, CH3)
    thrice = lambda rows: np.concatenate([rows, rows, rows, rows[:P - 3 * UNITS]])
    out["f3_zeros"] = thrice(units("gate_z", "up_z", "down_z").reshape(UNITS, D))
    out["f3_scales"] = thrice(units("gate_s", "up_s", "down_s").reshape(UNITS, D))
    col = lambda cond: np.where(cond, 1.0, 0.0).astype(np.float32)
    out["f3_pick"] = np.concatenate([col((row[:, None] % UNITS == np.arange(UNITS)) & (row[:, None] < 3 * UNITS)),
                                     -col(row[:, None] >= UNITS), -col(row[:, None] >= 2 * UNITS)], 1)
    return {k: np.ascontiguousarray(v) for k, v in out.items()}


def kernel(**inputs):
    import numpy as _np
    import concourse.bacc as _bacc
    from concourse import mybir as _mybir
    from concourse.bass_utils import run_bass_kernel_spmd as _run

    nc = _bacc.Bacc("TRN2", target_bir_lowering=False, num_devices=1)
    arrays = layouts(inputs, _np)
    d = {k: nc.dram_tensor(f"in_{k}", a.shape, _mybir.dt.from_np(a.dtype), kind="ExternalInput").ap()
         for k, a in arrays.items()}
    out = nc.dram_tensor("out_x", (T, D), _mybir.dt.float32, kind="ExternalOutput").ap()
    build(nc, d, out)
    r = _run(nc, [{f"in_{k}": a for k, a in arrays.items()}], core_ids=[0])
    return r.results[0]["out_x"].reshape(B, S, D)
```
